# Optimizing a Trainium2 kernel written in Bass

```python
import numpy as np
import jax
import jax.numpy as jnp

def _softmax(x, axis=-1):
    return jax.nn.softmax(x, axis=axis)

def _gelu(x):
    return jax.nn.gelu(x, approximate=True)

def _silu(x):
    return jax.nn.silu(x)

def _sigmoid(x):
    return jax.nn.sigmoid(x)

def _layernorm(x, axis=-1, eps=1e-05):
    m = jnp.mean(x, axis=axis, keepdims=True)
    v = jnp.var(x, axis=axis, keepdims=True)
    return (x - m) / jnp.sqrt(v + eps)

def _scatter_add(tgt, idx, src, axis=0):
    return tgt.at[idx].add(src)

def _segment_sum(src, seg, n):
    return jax.ops.segment_sum(src, seg, n)
kernel_name = 'mk_seq_postln_d2_jaxref_r8_999a2c'

def setup_inputs(seed: int=0):
    np.random.seed(seed)
    _w = jnp.asarray

    def _L0_attn_setup():
        import jax, jax.numpy as jnp
        import numpy as np
        from jax import lax
        CHUNK = 32
        NUM_HEADS = 4
        HEAD_V = 32
        GATE_EPS = 0.02
        RMS_EPS = 1e-05

        def _l2norm(x):
            return x / jnp.sqrt(jnp.sum(x * x, axis=-1, keepdims=True) + 1e-06)

        def _causal_dwconv(x, w):
            k = w.shape[-1]
            lhs = jnp.transpose(x, (0, 2, 1))
            rhs = w[:, None, :]
            y = lax.conv_general_dilated(lhs, rhs, (1,), [(k - 1, 0)], feature_group_count=w.shape[0], dimension_numbers=('NCH', 'OIH', 'NCH'))
            return jnp.transpose(y, (0, 2, 1))

        def _delta_rule_chunkwise(q, k, v, beta):
            b, h, L, dk = q.shape
            dv = v.shape[-1]
            n = L // CHUNK
            q = _l2norm(q)
            k = _l2norm(k)
            v = v * beta[..., None]
            kb = k * beta[..., None]
            ch = lambda t: t.reshape(b, h, n, CHUNK, -1)
            qc, kc, vc, kbc = map(ch, (q, k, v, kb))
            A = jnp.einsum('bhnid,bhnjd->bhnij', kbc, kc)
            eye = jnp.eye(CHUNK, dtype=q.dtype)
            M = eye + jnp.tril(A, -1)
            rhs = jnp.concatenate([vc, kbc], axis=-1)
            sol = lax.linalg.triangular_solve(M, rhs, left_side=True, lower=True, unit_diagonal=True)
            u, w = (sol[..., :dv], sol[..., dv:])

            def step(S, inp):
                q_i, k_i, u_i, w_i = inp
                attn = jnp.tril(jnp.einsum('bhid,bhjd->bhij', q_i, k_i))
                u_adj = u_i - jnp.einsum('bhid,bhde->bhie', w_i, S)
                out_i = jnp.einsum('bhid,bhde->bhie', q_i, S) + attn @ u_adj
                S = S + jnp.einsum('bhid,bhie->bhde', k_i, u_adj)
                return (S, out_i)
            mv = lambda t: jnp.moveaxis(t, 2, 0)
            S0 = jnp.zeros((b, h, dk, dv), q.dtype)
            S, outs = lax.scan(step, S0, (mv(qc), mv(kc), mv(u), mv(w)))
            out = jnp.moveaxis(outs, 0, 2).reshape(b, h, L, dv)
            return (out, S)

        def _forward(hidden_states, w_q, w_k, w_v, w_b, conv_q_w, conv_k_w, conv_v_w, fir1, fir3, fir7, fir15, fir31, gate_w1, gate_b1, gate_w2, gate_b2, norm_w, w_o):
            b, l, _ = hidden_states.shape
            H, Dv = (NUM_HEADS, HEAD_V)
            silu = jax.nn.silu
            q = silu(_causal_dwconv(hidden_states @ w_q, conv_q_w))
            k = silu(_causal_dwconv(hidden_states @ w_k, conv_k_w))
            v = silu(_causal_dwconv(hidden_states @ w_v, conv_v_w))
            beta = jax.nn.sigmoid(hidden_states @ w_b)
            to_bhl = lambda t: jnp.transpose(t.reshape(b, l, H, -1), (0, 2, 1, 3))
            delta_out, _S = _delta_rule_chunkwise(to_bhl(q), to_bhl(k), to_bhl(v), jnp.transpose(beta, (0, 2, 1)))
            delta_out = jnp.transpose(delta_out, (0, 2, 1, 3))
            v4 = v.reshape(b, l, H, Dv)
            firs = [_causal_dwconv(v, f).reshape(b, l, H, Dv) for f in (fir1, fir3, fir7, fir15, fir31)]
            streams = firs + [delta_out, v4]
            stats = jnp.concatenate([jnp.mean(jnp.abs(s), axis=-1) for s in streams], axis=-1)
            gate_inp = jnp.concatenate([hidden_states, stats], axis=-1)
            hmid = jax.nn.gelu(gate_inp @ gate_w1 + gate_b1, approximate=False)
            logits = (hmid @ gate_w2 + gate_b2).reshape(b, l, H, len(streams))
            wts = jax.nn.softplus(logits) + GATE_EPS
            wts = wts / jnp.sum(wts, axis=-1, keepdims=True)
            stacked = jnp.stack(streams, axis=-2)
            o = jnp.einsum('blhsd,blhs->blhd', stacked, wts)
            o = o * lax.rsqrt(jnp.mean(o * o, axis=-1, keepdims=True) + RMS_EPS) * norm_w
            return o.reshape(b, l, H * Dv) @ w_o
        key = jax.random.key(seed)
        ks = jax.random.split(key, 20)
        D = 128
        n = lambda i, shape, s=0.02: jax.random.normal(ks[i], shape, jnp.float32) * s
        return {'hidden_states': jax.random.normal(ks[0], (4, 512, D), jnp.float32), 'w_q': n(1, (D, D)), 'w_k': n(2, (D, D)), 'w_v': n(3, (D, D)), 'w_b': n(4, (D, NUM_HEADS)), 'conv_q_w': n(5, (D, 4), 0.2), 'conv_k_w': n(6, (D, 4), 0.2), 'conv_v_w': n(7, (D, 4), 0.2), 'fir1': n(8, (D, 1), 0.2), 'fir3': n(9, (D, 3), 0.2), 'fir7': n(10, (D, 7), 0.2), 'fir15': n(11, (D, 15), 0.2), 'fir31': n(12, (D, 31), 0.2), 'gate_w1': n(13, (D + NUM_HEADS * 7, 2 * D)), 'gate_b1': n(14, (2 * D,)), 'gate_w2': n(15, (2 * D, NUM_HEADS * 7)), 'gate_b2': n(16, (NUM_HEADS * 7,)) + 0.5, 'norm_w': 1.0 + n(17, (HEAD_V,)), 'w_o': n(18, (D, D))}
    _L0_attn_in = _L0_attn_setup()

    def _L0_ffn_setup():
        import jax, jax.numpy as jnp
        import numpy as np
        TOP_K = 2
        key = jax.random.key(seed)
        ks = jax.random.split(key, 6)
        B, S, D, BN, E = (32, 256, 128, 64, 8)
        return {'x': jax.random.normal(ks[0], (B, S, D), dtype=jnp.float32), 'gate_w': jax.random.normal(ks[1], (E, D), dtype=jnp.float32) * 0.02, 'down_w': jax.random.normal(ks[2], (E, BN, D), dtype=jnp.float32) * 0.02, 'down_b': jax.random.normal(ks[3], (E, BN), dtype=jnp.float32) * 0.02, 'up_w': jax.random.normal(ks[4], (E, D, BN), dtype=jnp.float32) * 0.02, 'up_b': jax.random.normal(ks[5], (E, D), dtype=jnp.float32) * 0.02}
    _L0_ffn_in = _L0_ffn_setup()

    def _L1_attn_setup():
        import jax, jax.numpy as jnp
        import numpy as np
        DIM = 128
        HID = 512
        NUM_HEADS = 4
        WINDOW = 64
        NUM_PM = 64
        NEG = -1e+30

        def _swa(x_in, wq, wk, wv, wo):
            B, S, D = x_in.shape
            h, dh = (NUM_HEADS, D // NUM_HEADS)
            q = (x_in @ wq.T).reshape(B, S, h, dh).transpose(0, 2, 1, 3)
            k = (x_in @ wk.T).reshape(B, S, h, dh).transpose(0, 2, 1, 3)
            v = (x_in @ wv.T).reshape(B, S, h, dh).transpose(0, 2, 1, 3)
            i = jnp.arange(S)[:, None]
            j = jnp.arange(S)[None, :]
            mask = (j <= i) & (j > i - WINDOW)
            logits = jnp.einsum('bhqd,bhkd->bhqk', q, k) / np.sqrt(dh).astype(np.float32)
            logits = jnp.where(mask, logits, NEG)
            attn = jax.nn.softmax(logits, axis=-1)
            out = jnp.einsum('bhqk,bhkd->bhqd', attn, v)
            out = out.transpose(0, 2, 1, 3).reshape(B, S, D)
            return out @ wo.T

        def _mlp(w1, b1, w2, b2, x):
            return jax.nn.silu(x @ w1.T + b1) @ w2.T + b2
        key = jax.random.key(seed)
        ks = jax.random.split(key, 12)
        B, S = (2, 256)
        sc = 0.02
        n = lambda k, shape, s=sc: jax.random.normal(k, shape, jnp.float32) * s
        return {'x': n(ks[0], (B, S, DIM), 1.0), 'mem': n(ks[1], (NUM_PM, DIM), 1.0), 'wq': n(ks[2], (DIM, DIM)), 'wk': n(ks[3], (DIM, DIM)), 'wv': n(ks[4], (DIM, DIM)), 'wo': n(ks[5], (DIM, DIM)), 'w1': n(ks[6], (HID, DIM)), 'b1': jnp.zeros((HID,), jnp.float32), 'w2': n(ks[7], (DIM, HID)), 'b2': jnp.zeros((DIM,), jnp.float32), 'lin1': n(ks[8], (DIM, DIM)), 'lin2': n(ks[9], (DIM, DIM)), 'alpha': jnp.float32(0.0001), 'theta': jnp.float32(0.0001)}
    _L1_attn_in = _L1_attn_setup()

    def _L1_ffn_setup():
        import jax, jax.numpy as jnp
        import numpy as np
        B, S, D, F, E = (2, 256, 128, 512, 8)
        LN_EPS = 1e-05

        def _layer_norm(x, gamma, beta):
            mu = jnp.mean(x, axis=-1, keepdims=True)
            var = jnp.mean(jnp.square(x - mu), axis=-1, keepdims=True)
            return (x - mu) * jax.lax.rsqrt(var + LN_EPS) * gamma + beta
        key = jax.random.key(seed)
        ks = jax.random.split(key, 8)

        def xavier(k, shape):
            fan_in, fan_out = (shape[-1], shape[-2])
            a = jnp.sqrt(6.0 / (fan_in + fan_out))
            return jax.random.uniform(k, shape, jnp.float32, -a, a)
        return {'tgt': jax.random.normal(ks[0], (B, S, D), jnp.float32), 'Wr': xavier(ks[1], (E, D)), 'br': jnp.zeros((E,), jnp.float32), 'W1': xavier(ks[2], (E, F, D)), 'b1': jnp.zeros((E, F), jnp.float32), 'W2': xavier(ks[3], (E, D, F)), 'b2': jnp.zeros((E, D), jnp.float32), 'gamma': jnp.ones((D,), jnp.float32), 'beta': jnp.zeros((D,), jnp.float32)}
    _L1_ffn_in = _L1_ffn_setup()
    _d = {'L0_attn_hidden_states': _L0_attn_in['hidden_states'], 'L0_attn_w_q': _L0_attn_in['w_q'], 'L0_attn_w_k': _L0_attn_in['w_k'], 'L0_attn_w_v': _L0_attn_in['w_v'], 'L0_attn_w_b': _L0_attn_in['w_b'], 'L0_attn_conv_q_w': _L0_attn_in['conv_q_w'], 'L0_attn_conv_k_w': _L0_attn_in['conv_k_w'], 'L0_attn_conv_v_w': _L0_attn_in['conv_v_w'], 'L0_attn_fir1': _L0_attn_in['fir1'], 'L0_attn_fir3': _L0_attn_in['fir3'], 'L0_attn_fir7': _L0_attn_in['fir7'], 'L0_attn_fir15': _L0_attn_in['fir15'], 'L0_attn_fir31': _L0_attn_in['fir31'], 'L0_attn_gate_w1': _L0_attn_in['gate_w1'], 'L0_attn_gate_b1': _L0_attn_in['gate_b1'], 'L0_attn_gate_w2': _L0_attn_in['gate_w2'], 'L0_attn_gate_b2': _L0_attn_in['gate_b2'], 'L0_attn_norm_w': _L0_attn_in['norm_w'], 'L0_attn_w_o': _L0_attn_in['w_o'], 'L0_ffn_gate_w': _L0_ffn_in['gate_w'], 'L0_ffn_down_w': _L0_ffn_in['down_w'], 'L0_ffn_down_b': _L0_ffn_in['down_b'], 'L0_ffn_up_w': _L0_ffn_in['up_w'], 'L0_ffn_up_b': _L0_ffn_in['up_b'], 'L1_attn_mem': _L1_attn_in['mem'], 'L1_attn_wq': _L1_attn_in['wq'], 'L1_attn_wk': _L1_attn_in['wk'], 'L1_attn_wv': _L1_attn_in['wv'], 'L1_attn_wo': _L1_attn_in['wo'], 'L1_attn_w1': _L1_attn_in['w1'], 'L1_attn_b1': _L1_attn_in['b1'], 'L1_attn_w2': _L1_attn_in['w2'], 'L1_attn_b2': _L1_attn_in['b2'], 'L1_attn_lin1': _L1_attn_in['lin1'], 'L1_attn_lin2': _L1_attn_in['lin2'], 'L1_attn_alpha': _L1_attn_in['alpha'], 'L1_attn_theta': _L1_attn_in['theta'], 'L1_ffn_Wr': _L1_ffn_in['Wr'], 'L1_ffn_br': _L1_ffn_in['br'], 'L1_ffn_W1': _L1_ffn_in['W1'], 'L1_ffn_b1': _L1_ffn_in['b1'], 'L1_ffn_W2': _L1_ffn_in['W2'], 'L1_ffn_b2': _L1_ffn_in['b2'], 'L1_ffn_gamma': _L1_ffn_in['gamma'], 'L1_ffn_beta': _L1_ffn_in['beta']}
    _x0 = _d['L0_attn_hidden_states']
    _d['L0_attn_hidden_states'] = jax.random.normal(jax.random.fold_in(jax.random.key(seed), 1), (8, 512, 128), dtype=_x0.dtype)
    del _x0
    return _d

def reference(L0_attn_hidden_states, L0_attn_w_q, L0_attn_w_k, L0_attn_w_v, L0_attn_w_b, L0_attn_conv_q_w, L0_attn_conv_k_w, L0_attn_conv_v_w, L0_attn_fir1, L0_attn_fir3, L0_attn_fir7, L0_attn_fir15, L0_attn_fir31, L0_attn_gate_w1, L0_attn_gate_b1, L0_attn_gate_w2, L0_attn_gate_b2, L0_attn_norm_w, L0_attn_w_o, L0_ffn_gate_w, L0_ffn_down_w, L0_ffn_down_b, L0_ffn_up_w, L0_ffn_up_b, L1_attn_mem, L1_attn_wq, L1_attn_wk, L1_attn_wv, L1_attn_wo, L1_attn_w1, L1_attn_b1, L1_attn_w2, L1_attn_b2, L1_attn_lin1, L1_attn_lin2, L1_attn_alpha, L1_attn_theta, L1_ffn_Wr, L1_ffn_br, L1_ffn_W1, L1_ffn_b1, L1_ffn_W2, L1_ffn_b2, L1_ffn_gamma, L1_ffn_beta):

    def _L0_attn_ref(hidden_states, w_q, w_k, w_v, w_b, conv_q_w, conv_k_w, conv_v_w, fir1, fir3, fir7, fir15, fir31, gate_w1, gate_b1, gate_w2, gate_b2, norm_w, w_o):
        import jax, jax.numpy as jnp
        import numpy as np
        from jax import lax
        CHUNK = 32
        NUM_HEADS = 4
        HEAD_V = 32
        GATE_EPS = 0.02
        RMS_EPS = 1e-05

        def _l2norm(x):
            return x / jnp.sqrt(jnp.sum(x * x, axis=-1, keepdims=True) + 1e-06)

        def _causal_dwconv(x, w):
            k = w.shape[-1]
            lhs = jnp.transpose(x, (0, 2, 1))
            rhs = w[:, None, :]
            y = lax.conv_general_dilated(lhs, rhs, (1,), [(k - 1, 0)], feature_group_count=w.shape[0], dimension_numbers=('NCH', 'OIH', 'NCH'))
            return jnp.transpose(y, (0, 2, 1))

        def _delta_rule_chunkwise(q, k, v, beta):
            b, h, L, dk = q.shape
            dv = v.shape[-1]
            n = L // CHUNK
            q = _l2norm(q)
            k = _l2norm(k)
            v = v * beta[..., None]
            kb = k * beta[..., None]
            ch = lambda t: t.reshape(b, h, n, CHUNK, -1)
            qc, kc, vc, kbc = map(ch, (q, k, v, kb))
            A = jnp.einsum('bhnid,bhnjd->bhnij', kbc, kc)
            eye = jnp.eye(CHUNK, dtype=q.dtype)
            M = eye + jnp.tril(A, -1)
            rhs = jnp.concatenate([vc, kbc], axis=-1)
            sol = lax.linalg.triangular_solve(M, rhs, left_side=True, lower=True, unit_diagonal=True)
            u, w = (sol[..., :dv], sol[..., dv:])

            def step(S, inp):
                q_i, k_i, u_i, w_i = inp
                attn = jnp.tril(jnp.einsum('bhid,bhjd->bhij', q_i, k_i))
                u_adj = u_i - jnp.einsum('bhid,bhde->bhie', w_i, S)
                out_i = jnp.einsum('bhid,bhde->bhie', q_i, S) + attn @ u_adj
                S = S + jnp.einsum('bhid,bhie->bhde', k_i, u_adj)
                return (S, out_i)
            mv = lambda t: jnp.moveaxis(t, 2, 0)
            S0 = jnp.zeros((b, h, dk, dv), q.dtype)
            S, outs = lax.scan(step, S0, (mv(qc), mv(kc), mv(u), mv(w)))
            out = jnp.moveaxis(outs, 0, 2).reshape(b, h, L, dv)
            return (out, S)

        def _forward(hidden_states, w_q, w_k, w_v, w_b, conv_q_w, conv_k_w, conv_v_w, fir1, fir3, fir7, fir15, fir31, gate_w1, gate_b1, gate_w2, gate_b2, norm_w, w_o):
            b, l, _ = hidden_states.shape
            H, Dv = (NUM_HEADS, HEAD_V)
            silu = jax.nn.silu
            q = silu(_causal_dwconv(hidden_states @ w_q, conv_q_w))
            k = silu(_causal_dwconv(hidden_states @ w_k, conv_k_w))
            v = silu(_causal_dwconv(hidden_states @ w_v, conv_v_w))
            beta = jax.nn.sigmoid(hidden_states @ w_b)
            to_bhl = lambda t: jnp.transpose(t.reshape(b, l, H, -1), (0, 2, 1, 3))
            delta_out, _S = _delta_rule_chunkwise(to_bhl(q), to_bhl(k), to_bhl(v), jnp.transpose(beta, (0, 2, 1)))
            delta_out = jnp.transpose(delta_out, (0, 2, 1, 3))
            v4 = v.reshape(b, l, H, Dv)
            firs = [_causal_dwconv(v, f).reshape(b, l, H, Dv) for f in (fir1, fir3, fir7, fir15, fir31)]
            streams = firs + [delta_out, v4]
            stats = jnp.concatenate([jnp.mean(jnp.abs(s), axis=-1) for s in streams], axis=-1)
            gate_inp = jnp.concatenate([hidden_states, stats], axis=-1)
            hmid = jax.nn.gelu(gate_inp @ gate_w1 + gate_b1, approximate=False)
            logits = (hmid @ gate_w2 + gate_b2).reshape(b, l, H, len(streams))
            wts = jax.nn.softplus(logits) + GATE_EPS
            wts = wts / jnp.sum(wts, axis=-1, keepdims=True)
            stacked = jnp.stack(streams, axis=-2)
            o = jnp.einsum('blhsd,blhs->blhd', stacked, wts)
            o = o * lax.rsqrt(jnp.mean(o * o, axis=-1, keepdims=True) + RMS_EPS) * norm_w
            return o.reshape(b, l, H * Dv) @ w_o
        return _forward(hidden_states, w_q, w_k, w_v, w_b, conv_q_w, conv_k_w, conv_v_w, fir1, fir3, fir7, fir15, fir31, gate_w1, gate_b1, gate_w2, gate_b2, norm_w, w_o)

    def _L0_ffn_ref(x, gate_w, down_w, down_b, up_w, up_b):
        import jax, jax.numpy as jnp
        import numpy as np
        TOP_K = 2
        pooled = x.mean(axis=1)
        gate = jax.nn.softmax(pooled @ gate_w.T, axis=-1)
        top_w, top_i = jax.lax.top_k(gate, TOP_K)
        top_w = top_w / (top_w.sum(axis=-1, keepdims=True) + 1e-08)
        Wd = down_w[top_i]
        bd = down_b[top_i]
        Wu = up_w[top_i]
        bu = up_b[top_i]
        h = jax.nn.gelu(jnp.einsum('bsd,bkcd->bksc', x, Wd) + bd[:, :, None, :], approximate=False)
        h = h * top_w[:, :, None, None]
        out = jnp.einsum('bksc,bkdc->bsd', h, Wu)
        out = out + (top_w[:, :, None] * bu).sum(axis=1)[:, None, :]
        return out

    def _L1_attn_ref(x, mem, wq, wk, wv, wo, w1, b1, w2, b2, lin1, lin2, alpha, theta):
        import jax, jax.numpy as jnp
        import numpy as np
        DIM = 128
        HID = 512
        NUM_HEADS = 4
        WINDOW = 64
        NUM_PM = 64
        NEG = -1e+30

        def _swa(x_in, wq, wk, wv, wo):
            B, S, D = x_in.shape
            h, dh = (NUM_HEADS, D // NUM_HEADS)
            q = (x_in @ wq.T).reshape(B, S, h, dh).transpose(0, 2, 1, 3)
            k = (x_in @ wk.T).reshape(B, S, h, dh).transpose(0, 2, 1, 3)
            v = (x_in @ wv.T).reshape(B, S, h, dh).transpose(0, 2, 1, 3)
            i = jnp.arange(S)[:, None]
            j = jnp.arange(S)[None, :]
            mask = (j <= i) & (j > i - WINDOW)
            logits = jnp.einsum('bhqd,bhkd->bhqk', q, k) / np.sqrt(dh).astype(np.float32)
            logits = jnp.where(mask, logits, NEG)
            attn = jax.nn.softmax(logits, axis=-1)
            out = jnp.einsum('bhqk,bhkd->bhqd', attn, v)
            out = out.transpose(0, 2, 1, 3).reshape(B, S, D)
            return out @ wo.T

        def _mlp(w1, b1, w2, b2, x):
            return jax.nn.silu(x @ w1.T + b1) @ w2.T + b2
        B, S, D = x.shape
        pm = jnp.broadcast_to(mem[None], (B, NUM_PM, D))
        x_in = jnp.concatenate([pm, x], axis=1)
        out_swa = _swa(x_in, wq, wk, wv, wo)
        k_flat = x_in.reshape(-1, D)
        v_flat = out_swa.reshape(-1, D)

        def loss_fn(params):
            pred = _mlp(*params, k_flat)
            return 0.5 * jnp.sum((pred - v_flat) ** 2)
        grads = jax.grad(loss_fn)((w1, b1, w2, b2))
        upd = jax.tree_util.tree_map(lambda p, g: (1.0 - alpha) * p - theta * g, (w1, b1, w2, b2), grads)
        out_mem = _mlp(*upd, k_flat).reshape(x_in.shape)
        g1 = jax.nn.sigmoid(out_swa @ lin1.T)
        g2 = jax.nn.sigmoid(out_mem @ lin2.T)
        out_merged = g1 * out_swa + g2 * out_mem
        return out_merged[:, NUM_PM:, :]

    def _L1_ffn_ref(tgt, Wr, br, W1, b1, W2, b2, gamma, beta):
        import jax, jax.numpy as jnp
        import numpy as np
        B, S, D, F, E = (2, 256, 128, 512, 8)
        LN_EPS = 1e-05

        def _layer_norm(x, gamma, beta):
            mu = jnp.mean(x, axis=-1, keepdims=True)
            var = jnp.mean(jnp.square(x - mu), axis=-1, keepdims=True)
            return (x - mu) * jax.lax.rsqrt(var + LN_EPS) * gamma + beta
        logits = jnp.einsum('bsd,ed->bse', tgt, Wr) + br
        top_v, top_i = jax.lax.top_k(logits, 2)
        top_w = jax.nn.softmax(top_v, axis=-1)
        n_exp = logits.shape[-1]
        router_w = jnp.sum(jax.nn.one_hot(top_i, n_exp, dtype=top_w.dtype) * top_w[..., None], axis=-2)
        h = jnp.einsum('bsd,efd->bsef', tgt, W1) + b1
        h = jax.nn.relu(h)
        o = jnp.einsum('bsef,edf->bsed', h, W2) + b2
        tgt2 = jnp.einsum('bsed,bse->bsd', o, router_w)
        return _layer_norm(tgt + tgt2, gamma, beta)
    x = L0_attn_hidden_states
    x = _layernorm(x + _L0_attn_ref(x, L0_attn_w_q, L0_attn_w_k, L0_attn_w_v, L0_attn_w_b, L0_attn_conv_q_w, L0_attn_conv_k_w, L0_attn_conv_v_w, L0_attn_fir1, L0_attn_fir3, L0_attn_fir7, L0_attn_fir15, L0_attn_fir31, L0_attn_gate_w1, L0_attn_gate_b1, L0_attn_gate_w2, L0_attn_gate_b2, L0_attn_norm_w, L0_attn_w_o), axis=-1)
    x = _layernorm(x + _L0_ffn_ref(x, L0_ffn_gate_w, L0_ffn_down_w, L0_ffn_down_b, L0_ffn_up_w, L0_ffn_up_b), axis=-1)
    x = _layernorm(x + _L1_attn_ref(x, L1_attn_mem, L1_attn_wq, L1_attn_wk, L1_attn_wv, L1_attn_wo, L1_attn_w1, L1_attn_b1, L1_attn_w2, L1_attn_b2, L1_attn_lin1, L1_attn_lin2, L1_attn_alpha, L1_attn_theta), axis=-1)
    x = _layernorm(x + _L1_ffn_ref(x, L1_ffn_Wr, L1_ffn_br, L1_ffn_W1, L1_ffn_b1, L1_ffn_W2, L1_ffn_b2, L1_ffn_gamma, L1_ffn_beta), axis=-1)
    return x

_drawn_inputs = setup_inputs


def setup_inputs(seed=0):
    import zlib

    import numpy as np

    out = dict(_drawn_inputs(seed))
    spreads = {'L1_attn_b1': (0.0, 0.1),
     'L1_attn_b2': (0.0, 0.432),
     'L1_ffn_br': (0.0, 0.504),
     'L1_ffn_b1': (0.0, 0.1),
     'L1_ffn_b2': (0.0, 0.1),
     'L1_ffn_gamma': (1.0, 0.2),
     'L1_ffn_beta': (0.0, 0.1)}
    factors = {'L0_attn_w_b': 4.087,
     'L0_attn_gate_w1': 6.635,
     'L0_attn_gate_b1': 8.0,
     'L0_attn_gate_w2': 6.884,
     'L0_attn_gate_b2': 8.0,
     'L0_attn_norm_w': 28.52,
     'L0_ffn_down_w': 2.835,
     'L0_ffn_down_b': 8.0,
     'L0_ffn_up_w': 2.753,
     'L0_ffn_up_b': 2.833,
     'L1_attn_mem': 8.0,
     'L1_attn_wq': 8.0,
     'L1_attn_wk': 8.0,
     'L1_attn_wv': 8.0,
     'L1_attn_wo': 6.655,
     'L1_attn_lin1': 8.0,
     'L1_attn_lin2': 8.0}
    for name, (base, spread) in spreads.items():
        noise = np.random.default_rng([zlib.crc32(name.encode()), seed]).standard_normal(out[name].shape)
        drawn = base * np.exp(spread * noise) if base else spread * noise
        out[name] = jnp.asarray(drawn.astype(out[name].dtype))
    for name, factor in factors.items():
        out[name] = (out[name] * factor).astype(out[name].dtype)
    return out
```

```python
from contextlib import ExitStack

import numpy as np
import concourse.bass as bass
import concourse.mybir as mybir

F32 = mybir.dt.float32
ACT = mybir.ActivationFunctionType
ALU = mybir.AluOpType
AX = mybir.AxisListType

P = 128
D = 128
B, L = 8, 512
H, DH = 4, 32
CH = 32
NB = 2
PAIRS = B // NB
T = NB * L
NT = T // P
NC = L // CH
G = NB * NC
S7 = 7
FIRS = (1, 3, 7, 15, 31)
FOFF = (0, 1, 4, 11, 26)
PADC, PADF = 3, 30
BANK = 512
E = 8
NM = 64
FH = 512
NEG = -1e30


def program(nc, A, out):
    ctx = ExitStack()
    with ctx:
        def sb(name, shape, dt=F32):
            return ctx.enter_context(nc.sbuf_tensor(name, shape, dt))

        PS = ctx.enter_context(nc.psum_tensor("PS", [P, 8 * BANK], F32))

        def banks(first, n=1):
            return PS[:, first * BANK:(first + n) * BANK]

        arena = {"front": sb("front", [P, 9 * T]), "middle": sb("middle", [P, 23 * T + 256])}
        used = {"front": 0, "middle": 0}

        def part(where, name, *shape):
            size = int(np.prod(shape))
            at = used[where]
            used[where] = at + size
            assert at + size <= arena[where].shape[1], (name, at + size)
            v = arena[where][:, at:at + size]
            if len(shape) == 2:
                v = v.rearrange("p (a b) -> p a b", a=shape[0])
            if len(shape) == 3:
                v = v.rearrange("p (a b c) -> p a b c", a=shape[0], b=shape[1])
            return v

        def part_in(name, *shape):
            return part("middle", name, *shape)

        ident = sb("ident", [P, P])
        ones = sb("ones", [P, P])
        headones = sb("headones", [P, P])
        statsel = sb("statsel", [P, S7, 28])
        den_sel = sb("den_sel", [28, 28])
        expand = sb("expand", [28, S7, P])
        keep_j_le_i = sb("keep_j_le_i", [P, CH])
        low_free = sb("low_free", [P, CH, CH])
        eye_quad = sb("eye_quad", [P, DH])
        eps6 = sb("eps6", [P, 1])
        eps5 = sb("eps5", [P, 1])
        one1 = sb("one1", [P, 1])
        w_q, w_k, w_v = sb("w_q", [D, D]), sb("w_k", [D, D]), sb("w_v", [D, D])
        w_b = sb("w_b", [D, H])
        w_bx = sb("w_bx", [D, D])
        conv_w = sb("conv_w", [P, 3, 4])
        fir_w = sb("fir_w", [P, 57])
        fir_diag = sb("fir_diag", [P, 31, P])
        gw1a = sb("gw1a", [D, 256])
        gw1b = sb("gw1b", [28, 256])
        gb1 = sb("gb1", [P, 2])
        gw2 = sb("gw2", [P, 2, 28])
        gb2 = sb("gb2", [28, 1])
        norm_col = sb("norm_col", [P, 1])
        w_o = sb("w_o", [P, D])
        w_on = sb("w_on", [P, D])

        gwT = sb("gwT", [D, E])
        dn_in = part_in("dn_in", 4, P)
        up_in = part_in("up_in", E, 64)
        w1_in = part_in("w1_in", 4, D)
        sq_in = part_in("sq_in", 4, D)
        mem_in = sb("mem_in", [NM, D])
        m_q = part("middle", "m_q", NM)
        m_v = part("middle", "m_v", H, DH + 1)
        m_sc = part("middle", "m_sc", H, NM)
        m_st = part("middle", "m_st", 2, H)
        m_prT = part("middle", "m_prT", H, NM)
        m_ao = part("middle", "m_ao", D)
        m_aoT = part("middle", "m_aoT", NM)
        m_swaT = part("middle", "m_swaT", NM)
        m_aT = part("middle", "m_aT", 4, NM)
        m_eT = part("middle", "m_eT", NM)
        m_e = part("middle", "m_e", D)
        m_zb, m_a, m_th, m_t1 = (part("middle", n, FH) for n in ("m_zb", "m_a", "m_th", "m_t1"))
        dnT = sb("dnT", [P, 4, P])
        upT = sb("upT", [P, 4, D])
        dnb = sb("dnb", [P, 4])
        upb = sb("upb", [E, D])
        w1T = sb("w1T", [P, 4, P])
        w2 = sb("w2", [P, FH])
        w2T = sb("w2T", [P, 4, D])
        aw = sb("aw", [P, 4, D])
        memT = sb("memT", [P, NM])
        b1c = sb("b1c", [P, 4])
        b1r = sb("b1r", [P, FH])
        b2c = sb("b2c", [P, 1])
        eight_low = sb("eight_low", [P, E, E])
        pick = sb("pick", [P, 4, E])
        wmask = sb("wmask", [P, P])
        gW1, gW2, dzsum = sb("gW1", [P, FH]), sb("gW2", [P, FH]), sb("dzsum", [P, FH])
        gb2s = sb("gb2s", [P, 1])
        esum = sb("esum", [P, 1])

        arena["late"] = fir_diag[:, :, :].rearrange("p k c -> p (k c)")
        used["late"] = 0
        lin_in = part("late", "lin_in", 2, D)
        lT = part("late", "lT", 2, D)
        keep_lr = sb("keep_lr", [P, 2])
        wrT = part("late", "wrT", E)
        brr = part("late", "brr", E)
        b1e = part("late", "b1e", E, 4)
        b2e = part("late", "b2e", D)[0:E]
        gamma_r, beta_r = part("late", "gamma_r", D), part("late", "beta_r", D)

        used["middle"] = 0
        x_tc = sb("x_tc", [P, NT, D])
        xe = sb("xe", [P, NB, NM + L])
        xT = xe[:, :, NM:]
        v_pad = sb("v_pad", [P, NB, PADF + L])
        conv = part("front", "conv", 3, NB, L)
        sq = part("front", "sq", 2, T)
        nrm = sq
        beta = part("front", "beta", T)
        ab = part("front", "ab", 2, T)
        acc = part("front", "acc", T)
        used["front"] = 0
        hmid = part("front", "hmid", 2, T)
        sp = part("front", "sp", 3, T)[0:28]
        stats = part("front", "stats", T)[0:28]

        kbq = part("middle", "kbq", 2, T)
        k_n = part("middle", "k_n", T)
        vb = part("middle", "vb", T)
        Dm = part("middle", "Dm", CH, CH)
        Dt = part("middle", "Dt", G, CH)
        tmp = part("middle", "tmp", 256)
        ka = part("middle", "ka", G, 64)
        kv = part("middle", "kv", G, 64)
        before = used["middle"]
        q_raw, k_raw, v_raw = (part("middle", n, NB, PADC + L) for n in ("q_raw", "k_raw", "v_raw"))
        used["middle"] = before
        wu = part("middle", "wu", G, 64)
        pt = part("middle", "pt", G, DH)
        gk = part("middle", "gk", NB, NC, DH)
        qwT = part("middle", "qwT", T)
        fir = part("middle", "fir", 5, T)
        delta = part("middle", "delta", T)
        state = part("middle", "state", NB, NC, DH)
        used["middle"] = 0
        x1T = part("middle", "x1T", NB, L)
        hf = part("middle", "hf", 4, T)
        ups = part("middle", "ups", NB, 4, D)
        x1 = part("middle", "x1", NT, D)
        x2 = part("middle", "x2", NT, D)
        qs = part("middle", "qs", T)
        ve = part("middle", "ve", 2 * NT, H, DH + 1)
        sc = [part("middle", f"sc{b}", H * 4, P) for b in range(NB)]
        prT = [part("middle", f"prT{b}", H * 4, P) for b in range(NB)]
        ao = part("middle", "ao", NT, D)
        aoT = part("middle", "aoT", T)
        swaT = part("middle", "swaT", T)
        used["middle"], used["front"] = 0, 0
        eT = part("middle", "eT", NB, L)
        e_tc = part("middle", "e_tc", NT, D)
        aT = part("front", "aT", 4, T)
        zb, a_tc, th, t1, dz = (part("front", n, 2, FH) for n in ("zb", "a_tc", "th", "t1", "dz"))
        ke = sb("ke", [P, NB, NM + L])
        bn6 = sb("bn6", [P, NT, 6])
        bn2 = sb("bn2", [P, NT, 2])
        rstd = sb("rstd", [P, NT])
        used["middle"], used["front"] = 0, 0
        w1eT = part("middle", "w1eT", E, 4, P)
        w2eT = part("middle", "w2eT", E, 4, D)
        before = used["middle"]
        hT = [part("middle", f"hT{o}", 4, T) for o in range(2)]
        used["middle"] = before
        w1n = part("middle", "w1n", E, 4, D)
        w2n = part("middle", "w2n", E, FH)
        bx2T, bswaT, bx2, omT, mT, x3, x3T = (part("middle", n, T) for n in ("bx2T", "bswaT", "bx2", "omT", "mT", "x3", "x3T"))
        baT = part("front", "baT", 4, T)
        tg = part("front", "tg", 2, T)
        y = part("front", "y", T)
        used["front"] -= T
        tok_pair = part("front", "tok_pair", NT * E, E)
        used["front"] += T
        rwT = part("front", "rwT", T)[0:E]
        rw = part("late", "rw", 5, NT, E)
        pooled = sb("pooled", [P, NB])
        pooled_b = sb("pooled_b", [P, NB, P])
        rt = sb("rt", [P, 8, 2 * E])
        pair8 = sb("pair8", [P, NB, E, E])
        eq8 = sb("eq8", [P, NB, E, E])
        cvec = sb("cvec", [P, NB, 4])
        cdiag = sb("cdiag", [E, NB, E])
        cd = sb("cd", [E, NB])
        c_rows = sb("c_rows", [E, NB, P])
        mx = sb("mx", [P, NB, H * 4])
        ri = sb("ri", [P, NT, H])

        sems = {}

        def s(name):
            if name not in sems:
                sems[name] = ctx.enter_context(nc.semaphore(name))
            return sems[name]

        second = {}

        def s2(name):
            if name not in second:
                second[name] = list(sems.values())[len(second)]
            return second[name]

        single = {}

        def once(name):
            if name not in single:
                single[name] = ctx.enter_context(nc.semaphore(name))
            return single[name]

        loaded, masks, prepared, step_go = (
            once(n) for n in ("loaded", "masks", "prepared", "step_go"))
        for n in ("turned", "turned_sb", "m_pe", "m_dve", "m_act", "m_done", "step2_done", "step2_go"):
            once(n)
        loads = [
            (w_q[:, :], A["L0_attn_w_q"]), (w_k[:, :], A["L0_attn_w_k"]), (w_v[:, :], A["L0_attn_w_v"]),
            (w_b[:, :], A["L0_attn_w_b"]), (conv_w[:, 0, :], A["L0_attn_conv_q_w"]),
            (conv_w[:, 1, :], A["L0_attn_conv_k_w"]), (conv_w[:, 2, :], A["L0_attn_conv_v_w"]),
            (gw1a[:, :], A["L0_attn_gate_w1"][0:D, :]), (gw1b[:, :], A["L0_attn_gate_w1"][D:D + 28, :]),
            (gb1[:, :], A["L0_attn_gate_b1"].rearrange("(m p) -> p m", p=P)),
            (gw2[:, :, :], A["L0_attn_gate_w2"].rearrange("(m p) c -> p m c", p=P)),
            (gb2[:, :], A["L0_attn_gate_b2"].rearrange("(p a) -> p a", a=1)),
            (w_o[:, :], A["L0_attn_w_o"]),
        ]
        loads += [(fir_w[:, FOFF[n]:FOFF[n] + k], A[f"L0_attn_fir{k}"]) for n, k in enumerate(FIRS)]
        loads += [(norm_col[DH * h:DH * h + DH, :], A["L0_attn_norm_w"].rearrange("(p a) -> p a", a=1)) for h in range(H)]
        loads += [
            (gwT[:, :], A["L0_ffn_gate_w"].rearrange("e d -> d e")),
            (dn_in, A["L0_ffn_down_w"].rearrange("e c d -> (e c) d").rearrange("(m p) d -> p m d", p=P)),
            (up_in, A["L0_ffn_up_w"].rearrange("e d c -> d e c")),
            (dnb[:, :], A["L0_ffn_down_b"].rearrange("(m a) c -> (a c) m", a=2)),
            (upb[:, :], A["L0_ffn_up_b"]),
            (w1_in, A["L1_attn_w1"].rearrange("(m p) d -> p m d", p=P)),
            (w2[:, :], A["L1_attn_w2"]),
            (mem_in[:, :], A["L1_attn_mem"]),
            (b1c[:, :], A["L1_attn_b1"].rearrange("(m p) -> p m", p=P)),
            (b2c[:, :], A["L1_attn_b2"].rearrange("(p a) -> p a", a=1)),
            (b1r[:, :], A["L1_attn_b1"].partition_broadcast(P)),
        ]
        late_loads = [
            (lin_in[:, 0, :], A["L1_attn_lin1"]), (lin_in[:, 1, :], A["L1_attn_lin2"]),
            (wrT, A["L1_ffn_Wr"].rearrange("e d -> d e")),
            (brr, A["L1_ffn_br"].partition_broadcast(P)),
            (b1e, A["L1_ffn_b1"].rearrange("e (m p) -> p e m", p=P)),
            (b2e, A["L1_ffn_b2"]),
            (gamma_r, A["L1_ffn_gamma"].partition_broadcast(P)),
            (beta_r, A["L1_ffn_beta"].partition_broadcast(P)),
            (w1n, A["L1_ffn_W1"].rearrange("e (m p) d -> p e m d", p=P)),
            (w2n, A["L1_ffn_W2"].rearrange("e d f -> d e f")),
        ]
        loads += [
            (keep_lr[:, 0:1], A["L1_attn_alpha"].partition_broadcast(P)),
            (keep_lr[:, 1:2], A["L1_attn_theta"].partition_broadcast(P)),
        ]
        loads += [(sq_in[:, n, :], A[f"L1_attn_w{c}"]) for n, c in enumerate("qkvo")]
        x2T_d = nc.dram_tensor("x2T_d", [PAIRS, P, T], F32).ap()
        swaT_d = nc.dram_tensor("swaT_d", [PAIRS, P, T], F32).ap()
        x2_d = nc.dram_tensor("x2_d", [PAIRS, P, T], F32).ap()
        block = ctx.enter_context(nc.Block())

        @block.gpsimd
        def _(pool):
            n = 0

            def fill(t, v):
                nonlocal n
                if n:
                    pool.wait_ge(masks, n)
                pool.memset(t, v).then_inc(masks, 1)
                n += 1

            def keep(t, op, pattern, base, mult, value):
                nonlocal n
                pool.wait_ge(masks, n)
                pool.affine_select(out=t, in_=t, compare_op=op, fill=value, base=base, pattern=pattern,
                                   channel_multiplier=mult).then_inc(masks, 1)
                n += 1

            fill(ident[:, :], 0.0)
            keep(ident[:, :], ALU.not_equal, [[-1, P]], 0, 1, 1.0)
            fill(ones[:, :], 1.0)
            for t, v in ((headones, 1.0),):
                fill(t[:, :], v)
                keep(t[:, :].rearrange("p (h d) -> p h d", h=H), ALU.is_ge, [[-DH, H], [0, DH]], 0, 1, 0.0)
                keep(t[:, :].rearrange("p (h d) -> p h d", h=H), ALU.is_ge, [[DH, H], [0, DH]], DH - 1, -1, 0.0)
            fill(statsel[:, :, :], 0.0)
            for k in range(S7):
                pool.wait_ge(masks, n)
                for h in range(H):
                    fill(statsel[DH * h:DH * h + DH, k, 4 * k + h:4 * k + h + 1], 1 / DH)
            fill(den_sel[:, :], 1.0)
            keep(den_sel[:, :].rearrange("p (h k) -> p h k", h=H), ALU.is_ge, [[-S7, H], [0, S7]], 0, 1, 0.0)
            keep(den_sel[:, :].rearrange("p (h k) -> p h k", h=H), ALU.is_ge, [[S7, H], [0, S7]], S7 - 1, -1, 0.0)
            fill(expand[:, :, :], 0.0)
            keep(expand[:, :, :].rearrange("p k (h d) -> p k h d", h=H), ALU.not_equal,
                 [[-1, S7], [-S7, H], [0, DH]], 0, 1, 1.0)
            for h in range(H):
                fill(keep_j_le_i[DH * h:DH * h + DH, :], 1.0)
                keep(keep_j_le_i[DH * h:DH * h + DH, :], ALU.is_ge, [[1, CH]], 0, -1, 0.0)
                fill(eye_quad[DH * h:DH * h + DH, :], 0.0)
                keep(eye_quad[DH * h:DH * h + DH, :], ALU.not_equal, [[-1, CH]], 0, 1, 1.0)
            fill(low_free[:, :, :], -1.0)
            keep(low_free[:, :, :], ALU.is_gt, [[1, CH], [-1, CH]], 0, 0, 0.0)
            fill(eps6[:, :], 1e-6)
            fill(eps5[:, :], 1e-5)
            fill(one1[:, :], 1.0)
            fill(eight_low[:, :, :], 1.0)
            keep(eight_low[:, :, :], ALU.is_gt, [[1, E], [-1, E]], 0, 0, 0.0)
            for half in range(2):
                v = pick[64 * half:64 * half + 64, :, :]
                fill(v, 0.0)
                keep(v, ALU.not_equal, [[-2, 4], [1, E]], -half, 0, 1.0)
                v = wmask[64 * half:64 * half + 64, :]
                fill(v, 0.0)
                keep(v, ALU.is_gt, [[1, P]], 0, -1, NEG)
                keep(v, ALU.is_ge, [[-1, P]], NM, 1, NEG)
            fill(v_pad[:, :, 0:PADF], 0.0)
            pool.wait_ge(masks, n)
            pool.wait_ge(loaded, 16 * len(loads))
            for j in range(31):
                pool.tensor_scalar(fir_diag[:, j, :], ident[:, :], fir_w[:, FOFF[4] + j:FOFF[4] + j + 1], None,
                                   ALU.mult).then_inc(masks, 1)
                n += 1
            pool.wait_ge(masks, n)
            pool.sem_inc(prepared, 1)
            pool.wait_ge(once("m_done"), 1)
            with pool.Fori(0, PAIRS) as i:
                for t in (q_raw, k_raw, v_raw):
                    pool.memset(t[:, :, 0:PADC], 0.0).then_inc(s("pads"), 1)
                pool.wait_ge(s("x1"), NT)
                pool.memset(ve[:, :, :, DH:DH + 1], 1.0).then_inc(s("ones_column"), 1)
                for t in range(NT):
                    pool.wait_ge(s("dz"), t + 1)
                    if t:
                        pool.wait_ge(s("dzsum"), t)
                    pool.tensor_tensor(dzsum[:, :], dzsum[:, :], dz[:, t % 2, :], ALU.add).then_inc(s("dzsum"), 1)
                pool.wait_ge(s("dzsum"), NT)
                pool.sem_inc(s("step_done"), 1)
                pool.wait_ge(step_go, i + 1)

        @block.vector
        def _(dve):
            dve.wait_ge(loaded, 16 * len(loads))
            dve.tensor_copy(w_bx[:, :].rearrange("p (h d) -> p h d", h=H),
                            w_b[:, :].unsqueeze(2).broadcast_to([P, H, DH])).then_inc(prepared, 1)
            dve.tensor_scalar(w_on[:, :], w_o[:, :], norm_col[:, 0:1], None, ALU.mult).then_inc(prepared, 1)
            dve.wait_ge(prepared, 3)
            for n, dst in enumerate((dnT, upT, w1T, w2T, aw)):
                dve.wait_ge(once("turned"), n + 1)
                dve.tensor_copy(dst[:, :, :], banks(n).rearrange("p (m c) -> p m c", c=P)).then_inc(once("turned_sb"), 1)
            dve.wait_ge(once("turned"), 6)
            dve.tensor_copy(memT[:, :], banks(5)[:, 0:NM]).then_inc(once("turned_sb"), 1)
            dve.tensor_copy(xe[:, :, 0:NM], banks(5)[:, 0:NM].unsqueeze(1).broadcast_to([P, NB, NM]))
            dve.memset(dzsum[NM:P, :], 0.0)
            dve.wait_ge(once("m_pe"), 1)
            dve.tensor_copy(m_q, banks(0)[:, 0:NM]).then_inc(once("m_dve"), 1)
            dve.tensor_copy(ke[:, :, 0:NM], banks(0)[:, NM:2 * NM].unsqueeze(1).broadcast_to([P, NB, NM])).then_inc(once("m_dve"), 1)
            dve.memset(m_v[0:NM, :, DH:DH + 1], 1.0)
            dve.tensor_copy(m_v[0:NM, :, 0:DH], banks(0)[0:NM, P:P + D].rearrange("p (h d) -> p h d", h=H)).then_inc(once("m_dve"), 1)
            dve.wait_ge(once("m_pe"), 2)
            dve.tensor_tensor(m_sc[0:NM, :, :], banks(2, 4)[0:NM].rearrange("p (h k) -> p h k", h=H)[:, :, 0:NM],
                              wmask[0:NM, NM:].unsqueeze(1).broadcast_to([NM, H, NM]), ALU.add).then_inc(once("m_dve"), 1)
            dve.wait_ge(once("m_dve"), 4)
            dve.tensor_reduce(m_st[0:NM, 0, :], m_sc[0:NM, :, :], AX.X, ALU.max).then_inc(once("m_dve"), 1)
            dve.wait_ge(once("m_dve"), 5)
            dve.tensor_tensor(m_sc[0:NM, :, :], m_sc[0:NM, :, :], m_st[0:NM, 0, :].unsqueeze(2).broadcast_to([NM, H, NM]),
                              ALU.subtract).then_inc(once("m_dve"), 1)
            dve.wait_ge(once("m_pe"), 3)
            dve.tensor_copy(m_prT[0:NM, :, :], banks(6)[0:NM, 0:H * NM].rearrange("p (h q) -> p h q", h=H)).then_inc(once("m_dve"), 1)
            dve.wait_ge(once("m_pe"), 4)
            pv = banks(7)[0:NM, 0:H * 33].rearrange("p (h e) -> p h e", h=H)
            dve.reciprocal(m_st[0:NM, 1, :].unsqueeze(2), pv[:, :, DH:DH + 1]).then_inc(once("m_dve"), 1)
            dve.wait_ge(once("m_dve"), 8)
            dve.tensor_tensor(m_ao[0:NM, :].rearrange("p (h e) -> p h e", h=H), pv[:, :, 0:DH],
                              m_st[0:NM, 1, :].unsqueeze(2).broadcast_to([NM, H, DH]), ALU.mult).then_inc(once("m_dve"), 1)
            dve.wait_ge(once("m_pe"), 5)
            dve.tensor_copy(m_aoT, banks(0)[:, 0:NM]).then_inc(once("m_dve"), 1)
            dve.wait_ge(once("m_pe"), 6)
            dve.tensor_copy(m_swaT, banks(1)[:, 0:NM]).then_inc(once("m_dve"), 1)
            dve.wait_ge(once("m_pe"), 8)
            dve.tensor_tensor(m_zb[0:NM, :], banks(5)[0:NM], b1r[0:NM, :], ALU.add).then_inc(once("m_dve"), 1)
            dve.wait_ge(once("m_pe"), 9)
            dve.wait_ge(once("m_dve"), 11)
            dve.scalar_tensor_tensor(out=m_eT, in0=banks(3)[:, 0:NM], scalar=b2c[:, 0:1], in1=m_swaT, op0=ALU.add,
                                     op1=ALU.subtract).then_inc(once("m_dve"), 1)
            dve.wait_ge(once("m_dve"), 13)
            dve.tensor_scalar(m_eT, m_eT, float(B), None, ALU.mult).then_inc(once("m_dve"), 1)
            dve.wait_ge(once("m_dve"), 14)
            dve.tensor_reduce(gb2s[:, :], m_eT, AX.X, ALU.add)
            dve.wait_ge(once("m_pe"), 10)
            dve.tensor_copy(m_e[0:NM, :], banks(4)[0:NM, 0:P]).then_inc(once("m_dve"), 1)
            dve.wait_ge(once("m_act"), 7)
            dve.scalar_tensor_tensor(out=m_t1[0:NM, :], in0=m_zb[0:NM, :], scalar=1.0, in1=m_a[0:NM, :], op0=ALU.add,
                                     op1=ALU.subtract).then_inc(once("m_dve"), 1)
            dve.wait_ge(once("m_dve"), 16)
            dve.scalar_tensor_tensor(out=m_t1[0:NM, :], in0=m_th[0:NM, :], scalar=1.0, in1=m_t1[0:NM, :], op0=ALU.add,
                                     op1=ALU.mult).then_inc(once("m_dve"), 1)
            dve.wait_ge(once("m_dve"), 17)
            dve.wait_ge(once("m_pe"), 11)
            dve.scalar_tensor_tensor(out=m_t1[0:NM, :], in0=m_t1[0:NM, :], scalar=0.5, in1=banks(6)[0:NM], op0=ALU.mult,
                                     op1=ALU.mult).then_inc(once("m_dve"), 1)
            dve.wait_ge(once("m_dve"), 18)
            dve.tensor_copy(dzsum[0:NM, :], m_t1[0:NM, :])
            dve.wait_ge(once("m_pe"), 12)
            dve.tensor_copy(gW2[:, :], banks(7))
            dve.tensor_copy(gW1[:, :], banks(0)).then_inc(once("m_done"), 1)
            dve.wait_ge(once("m_done"), 1)
            with dve.Fori(0, PAIRS) as i:
                def convolve(name, src, dst):
                    dve.wait_ge(s(name + "_raw"), 2)
                    c = {"q": 0, "k": 1, "v": 2}[name]
                    for j in range(4):
                        sh, w = src[:, :, j:j + L], conv_w[:, c, j:j + 1]
                        if j == 0:
                            ins = dve.tensor_scalar(dst, sh, w, None, ALU.mult)
                        else:
                            dve.wait_ge(s(name + "_conv"), j)
                            ins = dve.scalar_tensor_tensor(out=dst, in0=sh, scalar=w, in1=dst, op0=ALU.mult, op1=ALU.add)
                        ins.then_inc(s(name + "_conv"), 1)

                def fir_tap(n, j):
                    k = FIRS[n]
                    dst = fir[:, n, :].rearrange("p (b t) -> p b t", b=NB)
                    sh = v_pad[:, :, PADF - k + 1 + j:PADF - k + 1 + j + L]
                    w = fir_w[:, FOFF[n] + j:FOFF[n] + j + 1]
                    if j == 0:
                        dve.wait_ge(s("v_act"), 1)
                        ins = dve.tensor_scalar(dst, sh, w, None, ALU.mult)
                    else:
                        dve.wait_ge(s(f"fir{k}"), j)
                        ins = dve.scalar_tensor_tensor(out=dst, in0=sh, scalar=w, in1=dst, op0=ALU.mult, op1=ALU.add)
                    ins.then_inc(s(f"fir{k}"), 1)

                dve.wait_ge(s("pads"), 3)
                convolve("k", k_raw, conv[:, 1])
                convolve("q", q_raw, conv[:, 0])
                convolve("v", v_raw, conv[:, 2])
                dve.wait_ge(s("k_norm"), 1)
                dve.reciprocal(nrm[:, 1, :], nrm[:, 1, :]).then_inc(s("k_rnorm"), 1)
                dve.wait_ge(s("q_norm"), 1)
                dve.reciprocal(nrm[:, 0, :], nrm[:, 0, :]).then_inc(s("q_rnorm"), 1)
                dve.wait_ge(s("beta_tanh"), 1)
                dve.tensor_scalar(beta[:, :], beta[:, :], 0.5, 0.5, ALU.mult, ALU.add).then_inc(s("beta"), 1)
                dve.wait_ge(s("k_rnorm"), 1)
                dve.tensor_tensor(k_n[:, :], k_n[:, :], nrm[:, 1, :], ALU.mult).then_inc(s("k_n"), 1)
                dve.wait_ge(s("q_rnorm"), 1)
                dve.tensor_tensor(kbq[:, 1, :], kbq[:, 1, :], nrm[:, 0, :], ALU.mult).then_inc(s("kbq"), 1)
                dve.wait_ge(s("k_n"), 1)
                dve.wait_ge(s("beta"), 1)
                dve.tensor_tensor(kbq[:, 0, :], k_n[:, :], beta[:, :], ALU.mult).then_inc(s("kbq"), 1)
                dve.wait_ge(s("v_act"), 1)
                dve.tensor_tensor(vb[:, :].rearrange("p (b t) -> p b t", b=NB), v_pad[:, :, PADF:],
                                  beta[:, :].rearrange("p (b t) -> p b t", b=NB), ALU.mult).then_inc(s("vb"), 1)
                dve.transpose(ka[:, :, 0:32], k_n[:, :].rearrange("p (g i) -> p g i", g=G)).then_inc(s("ka"), 1)
                dve.wait_ge(s("kbq"), 2)
                dve.transpose(kv[:, :, 0:32], kbq[:, 0, :].rearrange("p (g i) -> p g i", g=G)).then_inc(s("kv"), 1)
                dve.wait_ge(s("vb"), 1)
                dve.transpose(kv[:, :, 32:64], vb[:, :].rearrange("p (g i) -> p g i", g=G)).then_inc(s("kv"), 1)
                for j in range(3):
                    fir_tap(1, j)
                dve.wait_ge(s("r1"), 4)
                for half in range(2):
                    src = banks(6 if half == 0 else 0, 2).rearrange("p (g c) -> p g c", c=64)
                    dve.tensor_tensor(ka[:, 16 * half:16 * half + 16, 32:64], src[:, :, 32:64],
                                      keep_j_le_i[:, :].unsqueeze(1).broadcast_to([P, 16, CH]),
                                      ALU.mult).then_inc(s("ka"), 1)
                    dve.tensor_copy(wu[:, 16 * half:16 * half + 16, 0:32], src[:, :, 0:32]).then_inc(s("a_copy"), 1)
                dve.wait_ge(s("a_copy"), 2)
                dve.transpose(Dm[:, :, :], wu[:, :, 0:32].rearrange("p g i -> p i g")).then_inc(s("inv"), 1)
                dve.wait_ge(s("inv"), 1)
                dve.tensor_tensor(Dm[:, :, :], Dm[:, :, :], low_free[:, :, :], ALU.mult).then_inc(s("inv"), 1)
                for j in range(1, CH - 1):
                    r = CH - 1 - j
                    dve.wait_ge(s("inv"), 2 * j)
                    t2 = tmp[:, 0:r * j].rearrange("p (r c) -> p r c", c=j)
                    dve.tensor_tensor(t2, Dm[:, j + 1:, j:j + 1].broadcast_to([P, r, j]),
                                      Dm[:, j:j + 1, 0:j].broadcast_to([P, r, j]), ALU.mult).then_inc(s("inv"), 1)
                    dve.wait_ge(s("inv"), 1 + 2 * j)
                    dve.tensor_tensor(Dm[:, j + 1:, 0:j], Dm[:, j + 1:, 0:j], t2, ALU.add).then_inc(s("inv"), 1)
                dve.wait_ge(s("inv"), 2 + 2 * 30)
                dve.transpose(Dt[:, :, :].rearrange("p g i -> p i g"), Dm[:, :, :]).then_inc(s("inv"), 1)
                dve.wait_ge(s("inv"), 3 + 2 * 30)
                dve.tensor_tensor(Dt[:, :, :], Dt[:, :, :], eye_quad[:, :].unsqueeze(1).broadcast_to([P, G, CH]), ALU.add)\
                    .then_inc(s("Dt"), 1)
                for j in range(7):
                    fir_tap(2, j)
                dve.wait_ge(s("r3"), 4)
                src = banks(0, 4).rearrange("p (g c) -> p g c", c=64)
                dve.scalar_tensor_tensor(out=pt[:, :, :], in0=src[:, :, 0:32], scalar=-1.0,
                                         in1=eye_quad[:, :].unsqueeze(1).broadcast_to([P, G, DH]),
                                         op0=ALU.mult, op1=ALU.add).then_inc(s("pt"), 1)
                dve.tensor_tensor(qwT[:, :].rearrange("p (g i) -> p g i", g=G),
                                  kbq[:, 1, :].rearrange("p (g i) -> p g i", g=G), src[:, :, 32:64],
                                  ALU.subtract).then_inc(s("qwT"), 1)
                dve.wait_ge(s("gk"), 1)
                dve.tensor_copy(state[:, :, 1, :], gk[:, :, 0, :]).then_inc(s("state"), 1)
                for n in range(1, NC - 1):
                    fir_tap(3, n - 1)
                    dve.wait_ge(s("scan"), n)
                    dve.tensor_tensor(state[:, :, n + 1, :], banks(6)[:, 0:64].rearrange("p (b e) -> p b e", b=NB),
                                      gk[:, :, n, :], ALU.add).then_inc(s("state"), 1)
                fir_tap(3, 14)
                dve.wait_ge(s("logits"), 2)
                dve.tensor_scalar(sp[:, 0, :], banks(2, 2)[0:28], gb2[:, 0:1], 0.0, ALU.add, ALU.max).then_inc(s("sp_max"), 1)
                dve.wait_ge(s("sp_max"), 1)
                dve.wait_ge(s("sp_ln"), 1)
                dve.scalar_tensor_tensor(out=sp[:, 2, :], in0=sp[:, 1, :], scalar=0.02, in1=sp[:, 0, :],
                                         op0=ALU.add, op1=ALU.add).then_inc(s("wraw"), 1)
                dve.wait_ge(s("den"), 2)
                dve.reciprocal(sp[:, 0, :], banks(0, 2)[0:28]).then_inc(s("rden"), 1)
                dve.wait_ge(s("rden"), 1)
                dve.tensor_tensor(sp[:, 2, :], sp[:, 2, :], sp[:, 0, :], ALU.mult).then_inc(s("wts"), 1)
                for k in range(S7):
                    st = fir[:, k, :] if k < 5 else delta[:, :] if k == 5 else v_pad[:, :, PADF:]
                    dve.wait_ge(s("expand"), 2 * k + 2)
                    if k == 0:
                        dve.wait_ge(s("streams"), 7)
                    src = banks(4 + 2 * (k % 2), 2)
                    dst = acc[:, :] if k == 0 else ab[:, k % 2, :]
                    if k == 6:
                        src, dst = (z.rearrange("p (b t) -> p b t", b=NB) for z in (src, dst))
                    if k >= 3:
                        dve.wait_ge(s("o_sum"), k - 2)
                    dve.tensor_tensor(dst, src, st, ALU.mult).then_inc(s("prod"), 1)
                    if k:
                        dve.wait_ge(s("prod"), k + 1)
                        if k > 1:
                            dve.wait_ge(s("o_sum"), k - 1)
                        dve.tensor_tensor(acc[:, :], acc[:, :], ab[:, k % 2, :], ALU.add).then_inc(s("o_sum"), 1)
                dve.wait_ge(s("o_root"), 1)
                dve.reciprocal(ab[:, 1, :], ab[:, 1, :]).then_inc(s("o_rroot"), 1)
                dve.wait_ge(s("o_rroot"), 1)
                dve.tensor_tensor(acc[:, :], acc[:, :], ab[:, 1, :], ALU.mult).then_inc(s("o_n"), 1)
                dve.wait_ge(s("attn_out"), 2)
                dve.tensor_tensor(x1[:, :, :], banks(0, 2).rearrange("p (t d) -> p t d", d=D), x_tc[:, :, :],
                                  ALU.add).then_inc(s("res1"), 1)
                dve.wait_ge(s("res1"), 1)
                for t in range(NT):
                    dve.bn_stats(bn6[:, t, :], x1[:, t, :]).then_inc(s("ln1_stats"), 1)
                for t in range(NT):
                    if t == 0:
                        dve.wait_ge(s("ln1_stats"), NT)
                    dve.bn_aggr(bn2[:, t, :], bn6[:, t, :]).then_inc(s("ln1_var"), 1)
                dve.wait_ge(s("ln1_root"), 1)
                dve.reciprocal(rstd[:, :], rstd[:, :]).then_inc(s("ln1_rstd"), 1)
                dve.wait_ge(s("ln1_rstd"), 1)
                for t in range(NT):
                    dve.tensor_scalar(x1[:, t, :], x1[:, t, :], bn2[:, t, 0:1], rstd[:, t:t + 1],
                                      ALU.subtract, ALU.mult).then_inc(s("x1"), 1)
                dve.wait_ge(s("x1T"), 2)
                for b in range(NB):
                    dve.tensor_scalar(pooled_b[:, b, :], ones[:, :], pooled[:, b:b + 1], 1 / L, ALU.mult, ALU.mult)\
                        .then_inc(s("pooled_b"), 1)
                e8 = lambda n: rt[:, n, :].rearrange("p (b e) -> p b e", b=NB)
                e1 = lambda n: rt[:, n, 0:NB]
                wide = lambda ap: ap.unsqueeze(2).broadcast_to([P, NB, E])
                dve.wait_ge(s("gate8"), 1)
                dve.tensor_reduce(e1(0), banks(6)[:, 0:2 * E].rearrange("p (b e) -> p b e", b=NB), AX.X, ALU.max)\
                    .then_inc(s("choice"), 1)
                dve.wait_ge(s("choice"), 1)
                dve.tensor_tensor(e8(1), banks(6)[:, 0:2 * E].rearrange("p (b e) -> p b e", b=NB), wide(e1(0)),
                                  ALU.subtract).then_inc(s("choice"), 1)
                dve.wait_ge(s("gate_exp"), 1)
                dve.tensor_reduce(e1(2), e8(1), AX.X, ALU.add).then_inc(s("choice"), 1)
                dve.wait_ge(s("choice"), 3)
                dve.reciprocal(e1(3), e1(2)).then_inc(s("choice"), 1)
                dve.wait_ge(s("choice"), 4)
                dve.tensor_tensor(e8(4), e8(1), wide(e1(3)), ALU.mult).then_inc(s("choice"), 1)
                dve.wait_ge(s("choice"), 5)
                mine = e8(4).unsqueeze(3).broadcast_to([P, NB, E, E])
                others = e8(4).unsqueeze(2).broadcast_to([P, NB, E, E])
                dve.tensor_tensor(pair8[:, :, :, :], others, mine, ALU.is_gt).then_inc(s("choice"), 1)
                dve.tensor_tensor(eq8[:, :, :, :], others, mine, ALU.is_equal).then_inc(s("choice"), 1)
                dve.wait_ge(s("choice"), 7)
                dve.tensor_tensor(eq8[:, :, :, :], eq8[:, :, :, :], eight_low[:, :, :].unsqueeze(1).broadcast_to([P, NB, E, E]),
                                  ALU.mult).then_inc(s("choice"), 1)
                dve.wait_ge(s("choice"), 8)
                dve.tensor_tensor(pair8[:, :, :, :], pair8[:, :, :, :], eq8[:, :, :, :], ALU.add).then_inc(s("choice"), 1)
                dve.wait_ge(s("choice"), 9)
                dve.tensor_reduce(e8(5), pair8[:, :, :, :], AX.X, ALU.add).then_inc(s("choice"), 1)
                dve.wait_ge(s("choice"), 10)
                dve.scalar_tensor_tensor(out=e8(5), in0=e8(5), scalar=1.5, in1=e8(4), op0=ALU.is_lt, op1=ALU.mult)\
                    .then_inc(s("choice"), 1)
                dve.wait_ge(s("choice"), 11)
                dve.tensor_reduce(e1(2), e8(5), AX.X, ALU.add).then_inc(s("choice"), 1)
                dve.wait_ge(s("choice"), 12)
                dve.tensor_scalar(e1(2), e1(2), 1e-8, None, ALU.add).then_inc(s("choice"), 1)
                dve.wait_ge(s("choice"), 13)
                dve.reciprocal(e1(3), e1(2)).then_inc(s("choice"), 1)
                dve.wait_ge(s("choice"), 14)
                dve.tensor_tensor(e8(6), e8(5), wide(e1(3)), ALU.mult).then_inc(s("choice"), 1)
                dve.wait_ge(s("choice"), 15)
                for b in range(NB):
                    dve.tensor_tensor(pair8[:, b, 0:4, :], e8(6)[:, b:b + 1, :].broadcast_to([P, 4, E]), pick[:, :, :],
                                      ALU.mult).then_inc(s("choice"), 1)
                dve.tensor_tensor(cdiag[:, :, :], e8(6)[0:E], ident[0:E, 0:E].unsqueeze(1).broadcast_to([E, NB, E]),
                                  ALU.mult).then_inc(s("choice"), 1)
                dve.wait_ge(s("choice"), 18)
                dve.tensor_reduce(cvec[:, :, :], pair8[:, :, 0:4, :], AX.X, ALU.add).then_inc(s("choice"), 1)
                dve.tensor_reduce(cd[:, :], cdiag[:, :, :], AX.X, ALU.add).then_inc(s("choice"), 1)
                dve.wait_ge(s("choice"), 20)
                for b in range(NB):
                    for m in range(4):
                        dve.tensor_scalar(ups[:, b, m, :], upT[:, m, :], cvec[:, b, m:m + 1], None, ALU.mult).then_inc(s("ups"), 1)
                    dve.tensor_scalar(c_rows[:, b, :], ones[0:E, :], cd[:, b:b + 1], None, ALU.mult).then_inc(s("ups"), 1)

                def norm(name, psum, resid, dst):
                    dve.wait_ge(s(name + "_out"), 2)
                    dve.tensor_tensor(dst[:, :, :], psum.rearrange("p (t d) -> p t d", d=D), resid[:, :, :],
                                      ALU.add).then_inc(s(name + "_res"), 1)
                    dve.wait_ge(s(name + "_res"), 1)
                    for t in range(NT):
                        dve.bn_stats(bn6[:, t, :], dst[:, t, :]).then_inc(s(name + "_stats"), 1)
                    dve.wait_ge(s(name + "_stats"), NT)
                    for t in range(NT):
                        dve.bn_aggr(bn2[:, t, :], bn6[:, t, :]).then_inc(s(name + "_var"), 1)
                    dve.wait_ge(s(name + "_root"), 1)
                    dve.reciprocal(rstd[:, :], rstd[:, :]).then_inc(s(name + "_rstd"), 1)
                    dve.wait_ge(s(name + "_rstd"), 1)
                    for t in range(NT):
                        dve.tensor_scalar(dst[:, t, :], dst[:, t, :], bn2[:, t, 0:1], rstd[:, t:t + 1],
                                          ALU.subtract, ALU.mult).then_inc(s(name), 1)

                norm("x2", banks(2, 2), x1, x2)
                for half in range(2):
                    dve.wait_ge(s("v_proj2"), 2 * half + 2)
                    dve.tensor_copy(ve[:, 8 * half:8 * half + 8, :, 0:DH],
                                    banks((6, 0)[half], 2).rearrange("p (j h d) -> p j h d", h=H, d=DH)).then_inc(s("ve"), 1)
                for b in range(NB):
                    for m in range(2):
                        dve.wait_ge(s("scores"), 4 * b + 2 * m + 2)
                        bank = ((2, 4), (6, 0))[b][m]
                        dve.tensor_tensor(sc[b][:, 8 * m:8 * m + 8, :], banks(bank, 2).rearrange("p (n k) -> p n k", k=P),
                                          wmask[:, :].unsqueeze(1).broadcast_to([P, 8, P]), ALU.add).then_inc(s("masked"), 1)
                    dve.wait_ge(s("masked"), 2 * b + 2)
                    dve.tensor_reduce(mx[:, b, :], sc[b], AX.X, ALU.max).then_inc(s("row_max"), 1)
                    dve.wait_ge(s("row_max"), b + 1)
                    dve.tensor_tensor(sc[b], sc[b], mx[:, b, :].unsqueeze(2).broadcast_to([P, 16, P]), ALU.subtract)\
                        .then_inc(s("shifted"), 1)
                for t in range(NT):
                    if t % 4 == 0:
                        dve.wait_ge(s("pv"), t // 4 + 1)
                    at = banks(2 + t // 2)[:, (t % 2) * 132:(t % 2) * 132 + 132].rearrange("p (h e) -> p h e", h=H)
                    dve.reciprocal(ri[:, t, :].unsqueeze(2), at[:, :, DH:DH + 1]).then_inc(s("ri"), 1)
                    dve.wait_ge(s("ri"), t + 1)
                    dve.tensor_tensor(ao[:, t, :].rearrange("p (h e) -> p h e", h=H), at[:, :, 0:DH],
                                      ri[:, t, :].unsqueeze(2).broadcast_to([P, H, DH]), ALU.mult).then_inc(s("ao"), 1)
                dve.wait_ge(s("pred"), 2)
                dve.wait_ge(s("swaT"), 1)
                dve.scalar_tensor_tensor(out=eT.rearrange("p b t -> p (b t)"), in0=banks(2, 2), scalar=b2c[:, 0:1], in1=swaT,
                                         op0=ALU.add, op1=ALU.subtract).then_inc(s("eT"), 1)
                for t in range(NT):
                    o = t % 2
                    if t >= 2:
                        dve.wait_ge(s("dw"), t - 1)
                    dve.wait_ge(s("z"), t + 1)
                    dve.tensor_tensor(zb[:, o, :], banks((6, 0)[o]), b1r[:, :], ALU.add).then_inc(s("zb"), 1)
                    if t == 0:
                        dve.wait_ge(s("eT"), 1)
                        dve.tensor_reduce(esum[:, :], eT.rearrange("p b t -> p (b t)"), AX.X, ALU.add).then_inc(s("esum"), 1)
                        dve.wait_ge(s("esum"), 1)
                        dve.tensor_tensor(gb2s[:, :], gb2s[:, :], esum[:, :], ALU.add).then_inc(s("gb2"), 1)
                    dve.wait_ge(s("a_th"), 2 * t + 2)
                    if t >= 2:
                        dve.wait_ge(s("dzsum"), t - 1)
                    dve.scalar_tensor_tensor(out=t1[:, o, :], in0=zb[:, o, :], scalar=1.0, in1=a_tc[:, o, :], op0=ALU.add,
                                             op1=ALU.subtract).then_inc(s("dz_steps"), 1)
                    dve.wait_ge(s("dz_steps"), 2 * t + 1)
                    dve.scalar_tensor_tensor(out=t1[:, o, :], in0=th[:, o, :], scalar=1.0, in1=t1[:, o, :], op0=ALU.add,
                                             op1=ALU.mult).then_inc(s("dz_steps"), 1)
                    dve.wait_ge(s("dz_steps"), 2 * t + 2)
                    dve.wait_ge(s("da"), t + 1)
                    dve.scalar_tensor_tensor(out=dz[:, o, :], in0=t1[:, o, :], scalar=0.5, in1=banks((7, 1)[o]), op0=ALU.mult,
                                             op1=ALU.mult).then_inc(s("dz"), 1)
                dve.wait_ge(s("dw"), NT)
                dve.tensor_tensor(gW2[:, :], gW2[:, :], banks(2), ALU.add).then_inc(s("gw"), 1)
                dve.tensor_tensor(gW1[:, :], gW1[:, :], banks(3), ALU.add).then_inc(s("gw"), 1)
                dve.wait_ge(s("gw"), 2)
                dve.wait_ge(s("gb2"), 1)
                dve.sem_inc(s("step_done"), 1)
                dve.wait_ge(step_go, i + 1)

            dve.tensor_scalar(keep_lr[:, 0:1], keep_lr[:, 0:1], -1.0, 1.0, ALU.mult, ALU.add).then_inc(s2("lr"), 1)
            dve.tensor_scalar(keep_lr[:, 1:2], keep_lr[:, 1:2], -1.0, None, ALU.mult).then_inc(s2("lr"), 1)
            dve.wait_ge(s2("lr"), 2)
            one_less, step = keep_lr[:, 0:1], keep_lr[:, 1:2]
            w1flat = w1T[:, :, :].rearrange("p m c -> p (m c)")
            dve.wait_ge(s2("db1"), 1)
            for grad, g_in in ((gW2[:, :], gW2[:, :]), (gW1[:, :], gW1[:, :]), (gb2s[:, :], gb2s[:, :]), (rt[:, 0, 0:4], banks(7)[:, 0:4])):
                dve.tensor_scalar(grad, g_in, step, None, ALU.mult).then_inc(s2("stepped"), 1)
            for n, (w, grad) in enumerate(((w2[:, :], gW2[:, :]), (w1flat, gW1[:, :]), (b2c[:, :], gb2s[:, :]), (b1c[:, :], rt[:, 0, 0:4]))):
                dve.wait_ge(s2("stepped"), n + 1)
                dve.scalar_tensor_tensor(out=w, in0=w, scalar=one_less, in1=grad, op0=ALU.mult, op1=ALU.add)\
                    .then_inc(s2("updated"), 1)
            for n in range(0, 16, 2):
                dve.wait_ge(s2("e_turned"), n + 1)
                dst = w1eT[:, n, :, :] if n < 8 else w2eT[:, n - 8, :, :]
                dve.tensor_copy(dst, banks(n % 8).rearrange("p (m c) -> p m c", m=4)).then_inc(s2("e_even"), 1)
            dve.wait_ge(s2("w2_turned"), 1)
            dve.tensor_copy(w2T[:, :, :], banks(0).rearrange("p (m c) -> p m c", m=4)).then_inc(s2("ready2"), 1)
            dve.wait_ge(s2("w2_turned"), 2)
            dve.tensor_copy(lT[:, :, :], banks(1)[:, 0:2 * D].rearrange("p (m c) -> p m c", m=2)).then_inc(s2("ready2"), 1)
            dve.wait_ge(s2("updated"), 4)
            dve.wait_ge(s2("ready2"), 2)
            dve.sem_inc(once("step2_done"), 1)
            dve.wait_ge(once("step2_go"), 1)
            with dve.Fori(0, PAIRS) as i:
                dve.wait_ge(s2("tg"), 1)
                dve.scalar_tensor_tensor(out=mT, in0=tg[:, 0, :], scalar=1.0, in1=bswaT, op0=ALU.add, op1=ALU.mult)\
                    .then_inc(s2("merge"), 1)
                dve.wait_ge(s2("tg"), 2)
                dve.scalar_tensor_tensor(out=tg[:, 1, :], in0=tg[:, 1, :], scalar=1.0, in1=omT, op0=ALU.add, op1=ALU.mult)\
                    .then_inc(s2("merge"), 1)
                dve.wait_ge(s2("merge"), 2)
                dve.tensor_tensor(mT, mT, tg[:, 1, :], ALU.add).then_inc(s2("merged"), 1)

                def norm2(name, src, dst):
                    for t in range(NT):
                        dve.bn_stats(bn6[:, t, :], src[:, t * D:(t + 1) * D]).then_inc(s2(name + "_stats"), 1)
                    dve.wait_ge(s2(name + "_stats"), NT)
                    for t in range(NT):
                        dve.bn_aggr(bn2[:, t, :], bn6[:, t, :]).then_inc(s2(name + "_var"), 1)
                    dve.wait_ge(s2(name + "_root"), 1)
                    dve.reciprocal(rstd[:, :], rstd[:, :]).then_inc(s2(name + "_rstd"), 1)
                    dve.wait_ge(s2(name + "_rstd"), 1)
                    for t in range(NT):
                        dve.tensor_scalar(dst[:, t * D:(t + 1) * D], src[:, t * D:(t + 1) * D], bn2[:, t, 0:1], rstd[:, t:t + 1],
                                          ALU.subtract, ALU.mult).then_inc(s2(name), 1)

                dve.wait_ge(s2("in_x2"), 16)
                dve.wait_ge(s2("m_turned"), 2)
                dve.scalar_tensor_tensor(out=x3, in0=banks(0, 2), scalar=0.5, in1=bx2, op0=ALU.mult, op1=ALU.add)\
                    .then_inc(s2("x3_res"), 1)
                dve.wait_ge(s2("x3_res"), 1)
                norm2("x3", x3, x3)
                dve.wait_ge(s2("r_logits"), 1)
                wide3 = lambda ap: ap.unsqueeze(2).broadcast_to([P, NT, E])
                col = lambda n: rw[:, 4, n, 0:NT]
                dve.tensor_tensor(rw[:, 0], banks(4)[:, 0:NT * E].rearrange("p (t e) -> p t e", e=E),
                                  brr[:, :].unsqueeze(1).broadcast_to([P, NT, E]), ALU.add).then_inc(s2("route"), 1)
                dve.wait_ge(s2("route"), 1)
                dve.tensor_reduce(col(0), rw[:, 0], AX.X, ALU.max).then_inc(s2("route"), 1)
                dve.wait_ge(s2("route"), 2)
                dve.tensor_tensor(rw[:, 1], rw[:, 0], wide3(col(0)), ALU.subtract).then_inc(s2("route"), 1)
                tp = tok_pair.rearrange("p (t e) f -> p t e f", e=E)
                mine = rw[:, 0].unsqueeze(3).broadcast_to([P, NT, E, E])
                others = rw[:, 0].unsqueeze(2).broadcast_to([P, NT, E, E])
                tq = tg[:, 0, 0:NT * E * E].rearrange("p (t e f) -> p t e f", e=E, f=E)
                dve.tensor_tensor(tp, others, mine, ALU.is_gt).then_inc(s2("route"), 1)
                dve.tensor_tensor(tq, others, mine, ALU.is_equal).then_inc(s2("route"), 1)
                dve.wait_ge(s2("route"), 5)
                dve.tensor_tensor(tq, tq, eight_low[:, :, :].unsqueeze(1).broadcast_to([P, NT, E, E]), ALU.mult).then_inc(s2("route"), 1)
                dve.wait_ge(s2("route"), 6)
                dve.tensor_tensor(tp, tp, tq, ALU.add).then_inc(s2("route"), 1)
                dve.wait_ge(s2("route"), 7)
                dve.tensor_reduce(rw[:, 2], tp, AX.X, ALU.add).then_inc(s2("route"), 1)
                dve.wait_ge(s2("route"), 8)
                dve.wait_ge(s2("r_exp"), 1)
                dve.scalar_tensor_tensor(out=rw[:, 2], in0=rw[:, 2], scalar=1.5, in1=rw[:, 1], op0=ALU.is_lt, op1=ALU.mult)\
                    .then_inc(s2("route"), 1)
                dve.wait_ge(s2("route"), 9)
                dve.tensor_reduce(col(1), rw[:, 2], AX.X, ALU.add).then_inc(s2("route"), 1)
                dve.wait_ge(s2("route"), 10)
                dve.reciprocal(col(2), col(1)).then_inc(s2("route"), 1)
                dve.wait_ge(s2("route"), 11)
                dve.tensor_tensor(rw[:, 3], rw[:, 2], wide3(col(2)), ALU.mult).then_inc(s2("weights"), 1)
                dve.wait_ge(s2("y_bias"), 2)
                dve.tensor_tensor(y, banks(0, 2), x3, ALU.add).then_inc(s2("y"), 1)
                for e in range(E):
                    for t in range(NT):
                        if t % 4 == 0:
                            dve.wait_ge(s2("o"), 2 * e + t // 4 + 1)
                        dve.wait_ge(s2("y"), 1 + max(0, NT * (e - 1) + t + 1))
                        yt = y[:, t * D:(t + 1) * D]
                        bank = (6, 0)[e % 2] + t // 4
                        dve.scalar_tensor_tensor(out=yt, in0=banks(bank)[:, (t % 4) * D:(t % 4 + 1) * D], scalar=rw[:, 3, t, e:e + 1],
                                                 in1=yt, op0=ALU.mult, op1=ALU.add).then_inc(s2("y"), 1)
                dve.wait_ge(s2("y"), 1 + NT * E)
                norm2("yn", y, y)
                y3 = y.rearrange("p (t d) -> p t d", d=D)
                dve.wait_ge(s2("yn"), NT)
                dve.tensor_tensor(y3, y3, gamma_r[:, :].unsqueeze(1).broadcast_to([P, NT, D]), ALU.mult).then_inc(s2("scaled"), 1)
                dve.wait_ge(s2("scaled"), 1)
                dve.tensor_tensor(y3, y3, beta_r[:, :].unsqueeze(1).broadcast_to([P, NT, D]), ALU.add).then_inc(s2("scaled"), 1)
                dve.wait_ge(s2("scaled"), 2)
                dve.tensor_tensor(y, y, x3, ALU.add).then_inc(s2("scaled"), 1)
                dve.wait_ge(s2("scaled"), 3)
                norm2("x4", y, y)
                dve.wait_ge(s2("x4"), NT)
                dve.sem_inc(s2("step_done"), 1)
                dve.wait_ge(once("step2_go"), i + 2)

        @block.scalar
        def _(act):
            act.wait_ge(prepared, 3)
            act.wait_ge(once("m_dve"), 6)
            act.activation(m_sc[0:NM, :, :], m_sc[0:NM, :, :], ACT.Exp, scale=DH ** -0.5).then_inc(once("m_act"), 1)
            act.wait_ge(once("m_pe"), 7)
            for m in range(4):
                act.activation(m_aT[:, m, :], banks(2)[:, m * NM:(m + 1) * NM], ACT.Silu, bias=b1c[:, m:m + 1])\
                    .then_inc(once("m_act"), 1)
            act.wait_ge(once("m_dve"), 12)
            act.activation(m_a[0:NM, :], m_zb[0:NM, :], ACT.Silu).then_inc(once("m_act"), 1)
            act.activation(m_th[0:NM, :], m_zb[0:NM, :], ACT.Tanh, scale=0.5).then_inc(once("m_act"), 1)
            act.wait_ge(once("m_done"), 1)
            with act.Fori(0, PAIRS) as i:
                for b in range(NB):
                    act.wait_ge(s("x_turned"), b + 1)
                    act.activation(xT[:, b, :], banks(b), ACT.Copy).then_inc(s("xT"), 1)
                for name, dst, bank in (("k", k_raw, 4), ("q", q_raw, 2), ("v", v_raw, 6)):
                    for b in range(NB):
                        act.wait_ge(s(name + "_proj"), b + 1)
                        act.activation(dst[:, b, PADC:], banks(bank + b), ACT.Copy).then_inc(s(name + "_raw"), 1)
                act.wait_ge(s("b_proj"), 2)
                act.activation(beta[:, :], banks(0, 2), ACT.Tanh, scale=0.5).then_inc(s("beta_tanh"), 1)
                act.wait_ge(s("k_conv"), 4)
                act.activation(k_n[:, :], conv[:, 1].rearrange("p b t -> p (b t)"), ACT.Silu).then_inc(s("k_act"), 1)
                act.wait_ge(s("q_conv"), 4)
                act.activation(kbq[:, 1, :], conv[:, 0].rearrange("p b t -> p (b t)"), ACT.Silu).then_inc(s("q_act"), 1)
                act.wait_ge(s("v_conv"), 4)
                act.activation(v_pad[:, :, PADF:], conv[:, 2], ACT.Silu).then_inc(s("v_act"), 1)
                act.wait_ge(s("k_act"), 1)
                act.activation(sq[:, 1, :], k_n[:, :], ACT.Square).then_inc(s("k_sq"), 1)
                act.wait_ge(s("q_act"), 1)
                act.activation(sq[:, 0, :], kbq[:, 1, :], ACT.Square).then_inc(s("q_sq"), 1)
                act.wait_ge(s("k_ss"), 2)
                act.activation(nrm[:, 1, :], banks(4, 2), ACT.Sqrt, bias=eps6[:, 0:1]).then_inc(s("k_norm"), 1)
                act.wait_ge(s("q_ss"), 2)
                act.activation(nrm[:, 0, :], banks(2, 2), ACT.Sqrt, bias=eps6[:, 0:1]).then_inc(s("q_norm"), 1)
                act.wait_ge(s("v_act"), 1)
                act.activation(fir[:, 0, :].rearrange("p (b t) -> p b t", b=NB), v_pad[:, :, PADF:], ACT.Copy,
                               scale=fir_w[:, 0:1]).then_inc(s("fir1"), 1)

                def magnitude(n, src, k):
                    if n >= 2:
                        act.wait_ge(s("stat"), 2 * (n - 1))
                    dst = ab[:, n % 2, :]
                    if k == 6:
                        dst = dst.rearrange("p (b t) -> p b t", b=NB)
                    act.activation(dst, src, ACT.Abs).then_inc(s("streams"), 1)

                magnitude(0, v_pad[:, :, PADF:], 6)
                act.wait_ge(s("fir1"), 1)
                magnitude(1, fir[:, 0, :], 0)
                act.wait_ge(s("fir31_psum"), 2)
                act.activation(fir[:, 4, :], banks(2, 2), ACT.Copy).then_inc(s("fir31"), 1)
                for m in range(2):
                    act.wait_ge(s("r2"), 2 * m + 2)
                    act.activation(wu[:, 16 * m:16 * m + 16, :].rearrange("p g c -> p (g c)"), banks(4 + 2 * m, 2),
                                   ACT.Copy).then_inc(s("wu"), 1)
                act.wait_ge(s("r4"), 2)
                act.activation(gk[:, :, :, :].rearrange("p b n e -> p (b n e)"), banks(4, 2), ACT.Copy).then_inc(s("gk"), 1)
                act.wait_ge(s("delta_psum"), 1)
                act.activation(delta[:, :], banks(0, 2), ACT.Copy).then_inc(s("delta"), 1)
                act.wait_ge(s("fir3"), 3)
                magnitude(2, fir[:, 1, :], 1)
                act.wait_ge(s("fir31"), 1)
                magnitude(3, fir[:, 4, :], 4)
                act.wait_ge(s("fir7"), 7)
                magnitude(4, fir[:, 2, :], 2)
                act.wait_ge(s("fir15"), 15)
                magnitude(5, fir[:, 3, :], 3)
                act.wait_ge(s("delta"), 1)
                magnitude(6, delta[:, :], 5)
                act.wait_ge(s("stat"), 14)
                act.activation(stats[:, :], banks(4, 2)[0:28], ACT.Copy).then_inc(s("stats"), 1)
                for m in range(2):
                    act.wait_ge(s("gate_h"), 2 * m + 2)
                    act.activation(hmid[:, m, :], banks((6, 2)[m], 2), ACT.Gelu, bias=gb1[:, m:m + 1]).then_inc(s("hmid"), 1)
                act.wait_ge(s("logits"), 2)
                act.wait_ge(s("sp_max"), 1)
                act.activation(sp[:, 1, :], banks(2, 2)[0:28], ACT.Abs, bias=gb2[:, 0:1]).then_inc(s("sp_abs"), 1)
                act.wait_ge(s("sp_abs"), 1)
                act.activation(sp[:, 1, :], sp[:, 1, :], ACT.Exp, scale=-1.0).then_inc(s("sp_exp"), 1)
                act.wait_ge(s("sp_exp"), 1)
                act.activation(sp[:, 1, :], sp[:, 1, :], ACT.Ln, bias=one1[0:28, 0:1]).then_inc(s("sp_ln"), 1)
                act.wait_ge(s("o_sum"), 6)
                act.activation(ab[:, 1, :], acc[:, :], ACT.Square).then_inc(s("o_sq"), 1)
                act.wait_ge(s("o_ms"), 2)
                act.activation(ab[:, 1, :], banks(2, 2), ACT.Sqrt, bias=eps5[:, 0:1], scale=1 / DH).then_inc(s("o_root"), 1)
                act.wait_ge(s("ln1_var"), NT)
                act.activation(rstd[:, :], bn2[:, :, 1], ACT.Sqrt, bias=eps5[:, 0:1]).then_inc(s("ln1_root"), 1)
                for b in range(NB):
                    act.wait_ge(s("x1_turned"), b + 1)
                    act.activation(x1T[:, b, :], banks(4 + b), ACT.Copy, accum_out=pooled[:, b:b + 1]).then_inc(s("x1T"), 1)
                act.wait_ge(s("choice"), 2)
                act.activation(rt[:, 1, :], rt[:, 1, :], ACT.Exp).then_inc(s("gate_exp"), 1)
                for m in range(4):
                    act.wait_ge(s("down"), 2 * m + 2)
                    act.activation(hf[:, m, :], banks((2, 0, 4, 6)[m], 2), ACT.Gelu, bias=dnb[:, m:m + 1]).then_inc(s("hf"), 1)
                act.wait_ge(s("x2_var"), NT)
                act.activation(rstd[:, :], bn2[:, :, 1], ACT.Sqrt, bias=eps5[:, 0:1]).then_inc(s("x2_root"), 1)
                for b in range(NB):
                    act.wait_ge(s("x2_turned"), b + 1)
                    act.activation(xe[:, b, NM:], banks(b), ACT.Copy).then_inc(s("xe"), 1)
                act.wait_ge(s("q_proj2"), 2)
                act.activation(qs, banks(2, 2), ACT.Copy).then_inc(s("qs"), 1)
                act.wait_ge(s("k_proj2"), 2)
                act.activation(ke[:, :, NM:], banks(4, 2).rearrange("p (b t) -> p b t", b=NB), ACT.Copy).then_inc(s("ke"), 1)
                for b in range(NB):
                    act.wait_ge(s("shifted"), b + 1)
                    act.activation(sc[b], sc[b], ACT.Exp, scale=DH ** -0.5).then_inc(s("probs"), 1)
                    for m in range(2):
                        act.wait_ge(s("probs_turned"), 4 * b + 2 * m + 2)
                        bank = ((2, 4), (6, 0))[b][m]
                        act.activation(prT[b][:, 8 * m:8 * m + 8, :].rearrange("p n q -> p (n q)"), banks(bank, 2), ACT.Copy)\
                            .then_inc(s("prT"), 1)
                act.wait_ge(s("ao_turned"), 2)
                act.activation(aoT, banks(6, 2), ACT.Copy).then_inc(s("aoT"), 1)
                act.wait_ge(s("wo"), 2)
                act.activation(swaT, banks(0, 2), ACT.Copy).then_inc(s("swaT"), 1)
                for n in range(8):
                    b, m = n // 4, n % 4
                    act.wait_ge(s("zT"), n + 1)
                    act.activation(aT[:, m, b * L:(b + 1) * L], banks(4 + n % 2), ACT.Silu, bias=b1c[:, m:m + 1])\
                        .then_inc(s("aT"), 1)
                act.wait_ge(s("e_turned"), 2)
                act.activation(e_tc.rearrange("p t d -> p (t d)"), banks(4, 2), ACT.Copy).then_inc(s("e_tc"), 1)
                for t in range(NT):
                    o = t % 2
                    act.wait_ge(s("zb"), t + 1)
                    if t >= 2:
                        act.wait_ge(s("dw"), t - 1)
                    act.activation(a_tc[:, o, :], zb[:, o, :], ACT.Silu).then_inc(s("a_th"), 1)
                    act.activation(th[:, o, :], zb[:, o, :], ACT.Tanh, scale=0.5).then_inc(s("a_th"), 1)
                act.wait_ge(s("a_th"), 2 * NT)
                act.sem_inc(s("step_done"), 1)
                act.wait_ge(step_go, i + 1)

            for n in range(1, 16, 2):
                act.wait_ge(s2("e_turned"), n + 1)
                dst = w1eT[:, n, :, :] if n < 8 else w2eT[:, n - 8, :, :]
                act.activation(dst.rearrange("p m c -> p (m c)"), banks(n % 8), ACT.Copy).then_inc(s2("e_odd"), 1)
            act.wait_ge(s2("e_odd"), 8)
            act.sem_inc(once("step2_done"), 1)
            act.wait_ge(once("step2_go"), 1)
            with act.Fori(0, PAIRS) as i:
                for n in range(8):
                    b, m = n // 4, n % 4
                    act.wait_ge(s2("zT"), n + 1)
                    act.activation(baT[:, m, b * L:(b + 1) * L], banks(n % 2), ACT.Silu, bias=b1c[:, m:m + 1]).then_inc(s2("aT"), 1)
                act.wait_ge(s2("g1"), 2)
                act.activation(tg[:, 0, :], banks(4, 2), ACT.Tanh, scale=0.5).then_inc(s2("tg"), 1)
                act.wait_ge(s2("om"), 2)
                act.activation(omT, banks(2, 2), ACT.Identity, bias=b2c[:, 0:1]).then_inc(s2("omT"), 1)
                act.wait_ge(s2("g2"), 2)
                act.activation(tg[:, 1, :], banks(6, 2), ACT.Tanh, scale=0.5).then_inc(s2("tg"), 1)
                act.wait_ge(s2("x3_var"), NT)
                act.activation(rstd[:, :], bn2[:, :, 1], ACT.Sqrt, bias=eps5[:, 0:1]).then_inc(s2("x3_root"), 1)
                act.wait_ge(s2("x3_turned"), 2)
                act.activation(x3T, banks(2, 2), ACT.Copy).then_inc(s2("x3T"), 1)
                act.wait_ge(s2("route"), 3)
                act.activation(rw[:, 1], rw[:, 1], ACT.Exp).then_inc(s2("r_exp"), 1)
                for e in range(E):
                    if e == 1:
                        act.wait_ge(s2("rw_turned"), 1)
                        act.activation(rwT, banks(6, 2)[0:E], ACT.Copy).then_inc(s2("rwT"), 1)
                    for m in range(4):
                        n = 4 * e + m
                        act.wait_ge(s2("h"), 2 * n + 2)
                        if e >= 2:
                            act.wait_ge(s2("o"), 2 * (e - 1))
                        act.activation(hT[e % 2][:, m, :], banks((2, 4)[n % 2], 2), ACT.Relu, bias=b1e[:, e, m:m + 1])\
                            .then_inc(s2("hT"), 1)
                act.wait_ge(s2("yn_var"), NT)
                act.activation(rstd[:, :], bn2[:, :, 1], ACT.Sqrt, bias=eps5[:, 0:1]).then_inc(s2("yn_root"), 1)
                act.wait_ge(s2("x4_var"), NT)
                act.wait_ge(s2("yn"), NT)
                act.activation(rstd[:, :], bn2[:, :, 1], ACT.Sqrt, bias=eps5[:, 0:1]).then_inc(s2("x4_root"), 1)
                act.wait_ge(s2("x4_root"), 1)
                act.sem_inc(s2("step_done"), 1)
                act.wait_ge(once("step2_go"), i + 2)

        @block.tensor
        def _(pe):
            pe.wait_ge(prepared, 3)
            up_blocks = up_in.rearrange("p (m a) c -> p m (a c)", a=2)
            for n, block_of in enumerate((lambda m: dn_in[:, m, :], lambda m: up_blocks[:, m, :], lambda m: w1_in[:, m, :],
                                          lambda m: w2[:, m * P:(m + 1) * P], lambda m: sq_in[:, m, :])):
                for m in range(4):
                    mm = pe.transpose(banks(n)[:, m * P:(m + 1) * P], block_of(m), ident[:, :])
                mm.then_inc(once("turned"), 1)
            pe.transpose(banks(5)[:, 0:NM], mem_in[:, :], ident[0:NM, 0:NM]).then_inc(once("turned"), 1)
            pe.wait_ge(once("turned_sb"), 6)
            pe.matmul(banks(0)[:, 0:NM], aw[:, 0, :], memT[:, :], start=True, stop=True)
            pe.matmul(banks(0)[:, NM:2 * NM], aw[:, 1, :], memT[:, :], start=True, stop=True)
            pe.matmul(banks(0)[0:NM, P:P + D], memT[:, :], aw[:, 2, :], start=True, stop=True).then_inc(once("m_pe"), 1)
            pe.wait_ge(once("m_dve"), 3)
            for h in range(H):
                r = slice(DH * h, DH * h + DH)
                mm = pe.matmul(banks(2 + h)[0:NM, 0:NM], m_q[r, :], ke[r, 0, 0:NM], start=True, stop=True)
            mm.then_inc(once("m_pe"), 1)
            pe.wait_ge(once("m_act"), 1)
            for h in range(H):
                mm = pe.transpose(banks(6)[0:NM, h * NM:(h + 1) * NM], m_sc[0:NM, h, :], ident[0:NM, 0:NM])
            mm.then_inc(once("m_pe"), 1)
            pe.wait_ge(once("m_dve"), 7)
            for h in range(H):
                mm = pe.matmul(banks(7)[0:NM, h * 33:(h + 1) * 33], m_prT[0:NM, h, :], m_v[0:NM, h, :], start=True, stop=True)
            mm.then_inc(once("m_pe"), 1)
            pe.wait_ge(once("m_dve"), 9)
            pe.transpose(banks(0)[:, 0:NM], m_ao[0:NM, :], ident[0:NM, 0:NM]).then_inc(once("m_pe"), 1)
            pe.wait_ge(once("m_dve"), 10)
            pe.matmul(banks(1)[:, 0:NM], aw[:, 3, :], m_aoT, start=True, stop=True).then_inc(once("m_pe"), 1)
            for m in range(4):
                mm = pe.matmul(banks(2)[:, m * NM:(m + 1) * NM], w1T[:, m, :], memT[:, :], start=True, stop=True)
            mm.then_inc(once("m_pe"), 1)
            pe.matmul(banks(5)[0:NM], memT[:, :], w1T[:, :, :].rearrange("p m c -> p (m c)"), start=True, stop=True)\
                .then_inc(once("m_pe"), 1)
            pe.wait_ge(once("m_act"), 5)
            for m in range(4):
                mm = pe.matmul(banks(3)[:, 0:NM], w2T[:, m, :], m_aT[:, m, :], start=(m == 0), stop=(m == 3))
            mm.then_inc(once("m_pe"), 1)
            pe.wait_ge(once("m_dve"), 14)
            pe.transpose(banks(4)[0:NM, 0:P], m_eT, ident[:, :]).then_inc(once("m_pe"), 1)
            pe.matmul(banks(6)[0:NM], m_eT, w2[:, :], start=True, stop=True).then_inc(once("m_pe"), 1)
            pe.wait_ge(once("m_dve"), 15)
            pe.wait_ge(once("m_dve"), 18)
            pe.matmul(banks(7), m_e[0:NM, :], m_a[0:NM, :], start=True, stop=True)
            pe.matmul(banks(0), mem_in[:, :], m_t1[0:NM, :], start=True, stop=True).then_inc(once("m_pe"), 1)
            pe.wait_ge(once("m_done"), 1)
            with pe.Fori(0, PAIRS) as i:
                pe.wait_ge(s("x_in"), 16)
                for b in range(NB):
                    for t in range(4):
                        mm = pe.transpose(banks(b)[:, t * P:(t + 1) * P], x_tc[:, 4 * b + t, :], ident[:, :])
                    mm.then_inc(s("x_turned"), 1)

                def project(name, w, rhs, bank):
                    for b in range(NB):
                        pe.matmul(banks(bank + b), w, rhs(b), start=True, stop=True).then_inc(s(name), 1)

                pe.wait_ge(s("xT"), 2)
                of_x = lambda b: xT[:, b, :]
                project("k_proj", w_k[:, :], of_x, 4)
                project("q_proj", w_q[:, :], of_x, 2)
                project("v_proj", w_v[:, :], of_x, 6)
                project("b_proj", w_bx[:, :], of_x, 0)
                pe.wait_ge(s("k_sq"), 1)
                pe.wait_ge(s("k_raw"), 2)
                project("k_ss", headones[:, :], lambda b: sq[:, 1, b * L:(b + 1) * L], 4)
                pe.wait_ge(s("q_sq"), 1)
                pe.wait_ge(s("q_raw"), 2)
                project("q_ss", headones[:, :], lambda b: sq[:, 0, b * L:(b + 1) * L], 2)
                pe.wait_ge(s("kbq"), 2)
                pe.wait_ge(s("v_raw"), 2)
                pe.wait_ge(s("beta_tanh"), 1)
                for g in range(G):
                    at = banks((6, 7, 0, 1)[g // 8])[:, (g % 8) * 64:(g % 8) * 64 + 64]
                    for h in range(H):
                        r = slice(DH * h, DH * h + DH)
                        mm = pe.matmul(at[r].rearrange("p (a c) -> p a c", a=2), k_n[r, g * CH:(g + 1) * CH],
                                       kbq[r, :, g * CH:(g + 1) * CH], start=True, stop=True)
                    if g % 8 == 7:
                        mm.then_inc(s("r1"), 1)
                pe.wait_ge(s("q_norm"), 1)
                pe.wait_ge(s("v_act"), 1)
                for b in range(NB):
                    for j in range(31):
                        mm = pe.matmul(banks(2 + b), fir_diag[:, j, :], v_pad[:, b, j:j + L], start=(j == 0), stop=(j == 30))
                    mm.then_inc(s("fir31_psum"), 1)

                stat_order = (6, 0, 1, 4, 2, 3, 5)

                def stat(n, bank):
                    pe.wait_ge(s("streams"), n + 1)
                    for b in range(NB):
                        pe.matmul(banks(bank + b)[0:28], statsel[:, stat_order[n], :], ab[:, n % 2, b * L:(b + 1) * L],
                                  start=(n == 0), stop=(n == 6), skip_group_check=True).then_inc(s("stat"), 1)

                def small(name, g, at, lhs, rhs, inc=False, **kw):
                    for h in range(H):
                        r = slice(DH * h, DH * h + DH)
                        mm = pe.matmul(at[r], lhs[r], rhs[r], **kw)
                    if inc:
                        mm.then_inc(s(name), 1)

                pe.wait_ge(s("k_norm"), 1)
                pe.wait_ge(s("Dt"), 1)
                pe.wait_ge(s("kv"), 2)
                for g in range(G):
                    small("r2", g, banks(4 + g // 8)[:, (g % 8) * 64:(g % 8) * 64 + 64], Dt[:, g, :], kv[:, g, :],
                          inc=g % 8 == 7, start=True, stop=True)
                pe.wait_ge(s("fir31"), 1)
                pe.wait_ge(s("ka"), 3)
                for g in range(G):
                    if g % 16 == 0:
                        pe.wait_ge(s("wu"), g // 16 + 1)
                    small("r3", g, banks(g // 8)[:, (g % 8) * 64:(g % 8) * 64 + 64], wu[:, g, 0:32], ka[:, g, :],
                          inc=g % 8 == 7, start=True, stop=True)
                for g in range(G):
                    small("r4", g, banks(4 + g // 16)[:, (g % 16) * 32:(g % 16) * 32 + 32], ka[:, g, 0:32], wu[:, g, 32:64],
                          inc=g % 16 == 15, start=True, stop=True)

                def chunk_out(n):
                    for b in range(NB):
                        g = b * NC + n
                        at = banks(b)[:, n * CH:(n + 1) * CH]
                        for h in range(H):
                            r = slice(DH * h, DH * h + DH)
                            mm = pe.matmul(at[r], wu[r, g, 32:64], ka[r, g, 32:64], start=True, stop=(n == 0))
                            if n:
                                mm = pe.matmul(at[r], state[r, b, n, :], qwT[r, g * CH:(g + 1) * CH], start=False, stop=True)
                    return mm

                pe.wait_ge(s("pt"), 1)
                pe.wait_ge(s("qwT"), 1)
                for n in range(1, NC):
                    pe.wait_ge(s("state"), n)
                    if n < NC - 1:
                        for b in range(NB):
                            for h in range(H):
                                r = slice(DH * h, DH * h + DH)
                                mm = pe.matmul(banks(6)[r, b * DH:(b + 1) * DH], pt[r, b * NC + n, :], state[r, b, n, :],
                                               start=True, stop=True)
                        mm.then_inc(s("scan"), 1)
                    chunk_out(n - 1)
                chunk_out(NC - 1).then_inc(s("delta_psum"), 1)
                for n in range(S7):
                    stat(n, 4)
                for m in range(2):
                    for b in range(NB):
                        at = banks((6, 2)[m] + b)
                        pe.matmul(at, gw1a[:, m * P:(m + 1) * P], xT[:, b, :], start=True, stop=False)
                        if m == 0 and b == 0:
                            pe.wait_ge(s("stats"), 1)
                        pe.matmul(at, gw1b[:, m * P:(m + 1) * P], stats[:, b * L:(b + 1) * L], start=False,
                                  stop=True).then_inc(s("gate_h"), 1)
                pe.wait_ge(s("hmid"), 2)
                for b in range(NB):
                    for m in range(2):
                        mm = pe.matmul(banks(2 + b)[0:28], gw2[:, m, :], hmid[:, m, b * L:(b + 1) * L], start=(m == 0), stop=(m == 1))
                    mm.then_inc(s("logits"), 1)
                pe.wait_ge(s("wraw"), 1)
                pe.wait_ge(s("delta"), 1)
                for b in range(NB):
                    pe.matmul(banks(b)[0:28], den_sel[:, :], sp[:, 2, b * L:(b + 1) * L], start=True, stop=True).then_inc(s("den"), 1)
                pe.wait_ge(s("wts"), 1)
                for k in range(S7):
                    if k >= 2:
                        pe.wait_ge(s("prod"), k - 1)
                    for b in range(NB):
                        pe.matmul(banks(4 + 2 * (k % 2) + b), expand[:, k, :], sp[:, 2, b * L:(b + 1) * L],
                                  start=True, stop=True).then_inc(s("expand"), 1)
                pe.wait_ge(s("o_sq"), 1)
                project("o_ms", headones[:, :], lambda b: ab[:, 1, b * L:(b + 1) * L], 2)
                pe.wait_ge(s("o_n"), 1)
                for t in range(NT):
                    mm = pe.matmul(banks(t // 4)[:, (t % 4) * D:(t % 4 + 1) * D], acc[:, t * P:(t + 1) * P], w_on[:, :],
                                   start=True, stop=True)
                    if t % 4 == 3:
                        mm.then_inc(s("attn_out"), 1)
                def turn(name, src, bank):
                    for b in range(NB):
                        for t in range(4):
                            mm = pe.transpose(banks(bank + b)[:, t * P:(t + 1) * P], src[:, 4 * b + t, :], ident[:, :])
                        mm.then_inc(s(name), 1)

                pe.wait_ge(s("x1"), NT)
                pe.wait_ge(s("prod"), 7)
                turn("x1_turned", x1, 4)
                pe.wait_ge(s("pooled_b"), 2)
                for b in range(NB):
                    mm = pe.matmul(banks(6)[:, b * E:(b + 1) * E], pooled_b[:, b, :], gwT[:, :], start=True, stop=True)
                mm.then_inc(s("gate8"), 1)
                pe.wait_ge(s("x1T"), 2)
                for m in range(4):
                    if m == 3:
                        pe.wait_ge(s("choice"), 2)
                    project("down", dnT[:, m, :], lambda b: x1T[:, b, :], (2, 0, 4, 6)[m])
                pe.wait_ge(s("hf"), 4)
                pe.wait_ge(s("ups"), 10)
                for t in range(NT):
                    at = banks(2 + t // 4)[:, (t % 4) * D:(t % 4 + 1) * D]
                    for m in range(4):
                        pe.matmul(at, hf[:, m, t * P:(t + 1) * P], ups[:, t // 4, m, :], start=(m == 0), stop=False)
                    mm = pe.matmul(at, c_rows[:, t // 4, :], upb[:, :], start=False, stop=True)
                    if t % 4 == 3:
                        mm.then_inc(s("x2_out"), 1)
                pe.wait_ge(s("x2"), NT)
                turn("x2_turned", x2, 0)
                pe.wait_ge(s("xe"), 2)
                project("q_proj2", aw[:, 0, :], lambda b: xe[:, b, NM:], 2)
                project("k_proj2", aw[:, 1, :], lambda b: xe[:, b, NM:], 4)
                for j in range(2 * NT):
                    b, k = j // 8, j % 8
                    mm = pe.matmul(banks((6, 7, 0, 1)[j // 4])[:, (j % 4) * D:(j % 4 + 1) * D],
                                   xe[:, b, NM * k:NM * k + P], aw[:, 2, :], start=True, stop=True)
                    if j % 4 == 3:
                        mm.then_inc(s("v_proj2"), 1)
                pe.wait_ge(s("qs"), 1)
                pe.wait_ge(s("ke"), 1)
                for b in range(NB):
                    if b == 1:
                        pe.wait_ge(s("ve"), 2)
                    for t in range(4):
                        for half in range(2):
                            for h in range(H):
                                r = slice(DH * h, DH * h + DH)
                                k0 = t * P + NM * half
                                mm = pe.matmul(banks(((2, 3, 4, 5), (6, 7, 0, 1))[b][h])[NM * half:NM * half + NM, t * P:(t + 1) * P],
                                               qs[r, b * L + k0:b * L + k0 + NM], ke[r, b, k0:k0 + P], start=True, stop=True)
                                if t == 3 and half == 1:
                                    mm.then_inc(s("scores"), 1)
                pe.wait_ge(s("ones_column"), 1)
                for b in range(NB):
                    pe.wait_ge(s("probs"), b + 1)
                    for n in range(16):
                        mm = pe.transpose(banks(((2, 3, 4, 5), (6, 7, 0, 1))[b][n // 4])[:, (n % 4) * P:(n % 4 + 1) * P],
                                          sc[b][:, n, :], ident[:, :])
                        if n % 4 == 3:
                            mm.then_inc(s("probs_turned"), 1)
                for b in range(NB):
                    pe.wait_ge(s("prT"), 2 * b + 2)
                    for t in range(4):
                        for half in range(2):
                            for h in range(H):
                                c = (t % 2) * 132 + h * 33
                                mm = pe.matmul(banks(2 + (4 * b + t) // 2)[NM * half:NM * half + NM, c:c + 33],
                                               prT[b][:, 4 * h + t, NM * half:NM * half + NM], ve[:, 8 * b + 2 * t + half, h, :],
                                               start=True, stop=True)
                    mm.then_inc(s("pv"), 1)
                pe.wait_ge(s("prT"), 4)
                pe.wait_ge(s("ao"), NT)
                turn("ao_turned", ao, 6)
                pe.wait_ge(s("aoT"), 1)
                project("wo", aw[:, 3, :], lambda b: aoT[:, b * L:(b + 1) * L], 0)
                for n in range(8):
                    b, m = n // 4, n % 4
                    if n >= 2:
                        pe.wait_ge(s("aT"), n - 1)
                    pe.matmul(banks(4 + n % 2), w1T[:, m, :], xe[:, b, NM:], start=True, stop=True).then_inc(s("zT"), 1)
                for b in range(NB):
                    pe.wait_ge(s("aT"), 4 * b + 4)
                    for m in range(4):
                        mm = pe.matmul(banks(2 + b), w2T[:, m, :], aT[:, m, b * L:(b + 1) * L], start=(m == 0), stop=(m == 3))
                    mm.then_inc(s("pred"), 1)

                def z_and_da(t):
                    b, c = t // 4, t % 4
                    o = t % 2
                    if t >= 2:
                        pe.wait_ge(s("zb"), t - 1)
                    pe.matmul(banks((6, 0)[o]), xe[:, b, NM + c * P:NM + (c + 1) * P], w1T[:, :, :].rearrange("p m c -> p (m c)"),
                              start=True, stop=True).then_inc(s("z"), 1)
                    if t >= 2:
                        pe.wait_ge(s("dz"), t - 1)
                    if t == 0:
                        pe.wait_ge(s("eT"), 1)
                        for bb in range(NB):
                            for cc in range(4):
                                mm = pe.transpose(banks(4 + bb)[:, cc * P:(cc + 1) * P], eT[:, bb, cc * P:(cc + 1) * P], ident[:, :])
                            mm.then_inc(s("e_turned"), 1)
                    pe.matmul(banks((7, 1)[o]), eT[:, b, c * P:(c + 1) * P], w2[:, :], start=True, stop=True).then_inc(s("da"), 1)

                pe.wait_ge(s("swaT"), 1)
                z_and_da(0)
                for t in range(NT):
                    if t + 1 < NT:
                        z_and_da(t + 1)
                    o = t % 2
                    if t == 0:
                        pe.wait_ge(s("e_tc"), 1)
                    pe.wait_ge(s("a_th"), 2 * t + 2)
                    pe.matmul(banks(2), e_tc[:, t, :], a_tc[:, o, :], start=(t == 0), stop=(t == NT - 1))
                    pe.wait_ge(s("dz"), t + 1)
                    pe.matmul(banks(3), x2[:, t, :], dz[:, o, :], start=(t == 0), stop=(t == NT - 1)).then_inc(s("dw"), 1)
                pe.wait_ge(s("dw"), NT)
                pe.sem_inc(s("step_done"), 1)
                pe.wait_ge(step_go, i + 1)

            for m in range(4):
                mm = pe.matmul(banks(7)[:, m:m + 1], dzsum[:, m * P:(m + 1) * P], ones[:, 0:1], start=True, stop=True)
            mm.then_inc(s2("db1"), 1)
            pe.wait_ge(s2("e_loaded"), 16 * len(late_loads))
            for n in range(16):
                if n == 7:
                    pe.wait_ge(s2("stepped"), 4)
                if n >= 8:
                    pe.wait_ge(s2(("e_even", "e_odd")[n % 2]), (n - 8) // 2 + 1)
                for m in range(4):
                    src = w1n[:, n, m, :] if n < 8 else w2n[:, n - 8, m * P:(m + 1) * P]
                    mm = pe.transpose(banks(n % 8)[:, m * P:(m + 1) * P], src, ident[:, :])
                mm.then_inc(s2("e_turned"), 1)
            pe.wait_ge(s2("updated"), 1)
            pe.wait_ge(s2("e_even"), 5)
            for m in range(4):
                mm = pe.transpose(banks(0)[:, m * P:(m + 1) * P], w2[:, m * P:(m + 1) * P], ident[:, :])
            mm.then_inc(s2("w2_turned"), 1)
            pe.wait_ge(s2("e_odd"), 5)
            for m in range(2):
                mm = pe.transpose(banks(1)[:, m * P:(m + 1) * P], lin_in[:, m, :], ident[:, :])
            mm.then_inc(s2("w2_turned"), 1)
            pe.wait_ge(s2("w2_turned"), 2)
            pe.sem_inc(once("step2_done"), 1)
            pe.wait_ge(once("step2_go"), 1)
            with pe.Fori(0, PAIRS) as i:
                def project2(name, w, src, bank):
                    for b in range(NB):
                        pe.matmul(banks(bank + b), w, src[:, b * L:(b + 1) * L], start=True, stop=True).then_inc(s2(name), 1)

                def turn2(name, src, bank):
                    for t in range(NT):
                        mm = pe.transpose(banks(bank + t // 4)[:, (t % 4) * P:(t % 4 + 1) * P], src[:, t * P:(t + 1) * P], ident[:, :])
                        if t % 4 == 3:
                            mm.then_inc(s2(name), 1)

                pe.wait_ge(s2("in_x2T"), 16)
                for n in range(8):
                    b, m = n // 4, n % 4
                    if n >= 2:
                        pe.wait_ge(s2("aT"), n - 1)
                    pe.matmul(banks(n % 2), w1T[:, m, :], bx2T[:, b * L:(b + 1) * L], start=True, stop=True).then_inc(s2("zT"), 1)
                pe.wait_ge(s2("in_swaT"), 16)
                project2("g1", lT[:, 0, :], bswaT, 4)
                for b in range(NB):
                    pe.wait_ge(s2("aT"), 4 * b + 4)
                    for m in range(4):
                        mm = pe.matmul(banks(2 + b), w2T[:, m, :], baT[:, m, b * L:(b + 1) * L], start=(m == 0), stop=(m == 3))
                    mm.then_inc(s2("om"), 1)
                pe.wait_ge(s2("omT"), 1)
                project2("g2", lT[:, 1, :], omT, 6)
                pe.wait_ge(s2("merged"), 1)
                turn2("m_turned", mT, 0)
                pe.wait_ge(s2("x3"), NT)
                turn2("x3_turned", x3, 2)
                pe.wait_ge(s2("x3T"), 1)
                for t in range(NT):
                    mm = pe.matmul(banks(4)[:, t * E:(t + 1) * E], x3T[:, t * P:(t + 1) * P], wrT[:, :], start=True, stop=True)
                mm.then_inc(s2("r_logits"), 1)

                def hidden(e, m):
                    n = 4 * e + m
                    if n == 1:
                        pe.wait_ge(s2("route"), 1)
                    if n >= 2:
                        pe.wait_ge(s2("hT"), n - 1)
                    for b in range(NB):
                        pe.matmul(banks((2, 4)[n % 2] + b), w1eT[:, e, m, :], x3T[:, b * L:(b + 1) * L], start=True,
                                  stop=True).then_inc(s2("h"), 1)

                hidden(0, 0)
                hidden(0, 1)
                hidden(0, 2)
                hidden(0, 3)
                pe.wait_ge(s2("weights"), 1)
                for t in range(NT):
                    mm = pe.transpose(banks(6 + t // 4)[0:E, (t % 4) * P:(t % 4 + 1) * P], rw[:, 3, t, :], ident[:, :])
                mm.then_inc(s2("rw_turned"), 1)
                pe.wait_ge(s2("rwT"), 1)
                for t in range(NT):
                    mm = pe.matmul(banks(t // 4)[:, (t % 4) * D:(t % 4 + 1) * D], rwT[:, t * P:(t + 1) * P], b2e[:, :],
                                   start=True, stop=True)
                    if t % 4 == 3:
                        mm.then_inc(s2("y_bias"), 1)
                for e in range(E):
                    for t in range(NT):
                        if e + 1 < E and t % 2 == 0:
                            hidden(e + 1, t // 2)
                        if t == 0:
                            pe.wait_ge(s2("hT"), 4 * e + 4)
                            if e == 1:
                                pe.wait_ge(s2("y"), 1)
                            if e >= 2:
                                pe.wait_ge(s2("y"), 1 + NT * (e - 1))
                        at = banks((6, 0)[e % 2] + t // 4)[:, (t % 4) * D:(t % 4 + 1) * D]
                        for m in range(4):
                            mm = pe.matmul(at, hT[e % 2][:, m, t * P:(t + 1) * P], w2eT[:, e, m, :], start=(m == 0), stop=(m == 3))
                        if t % 4 == 3:
                            mm.then_inc(s2("o"), 1)
                pe.wait_ge(s2("o"), 2 * E)
                pe.sem_inc(s2("step_done"), 1)
                pe.wait_ge(once("step2_go"), i + 2)

        @block.sync
        def _(sp_):
            for dst, src in loads:
                sp_.dma_start(dst, src, allow_slow_non_contiguous=True).then_inc(loaded, 16)
            with sp_.Fori(0, PAIRS) as i:
                sp_.dma_start(x_tc[:, :, :].rearrange("p (b t) d -> p b t d", b=NB),
                              A["L0_attn_hidden_states"][bass.ds(i * NB, NB), :, :].rearrange("b (t p) d -> p b t d", p=P)
                              ).then_inc(s("x_in"), 16)
                sp_.wait_ge(s("x2"), NT)
                sp_.dma_start(x2_d[bass.ds(i, 1), :, :].rearrange("a p n -> p (a n)"), x2.rearrange("p t d -> p (t d)"))\
                    .then_inc(s("kept"), 16)
                sp_.wait_ge(s("xe"), 2)
                sp_.dma_start(x2T_d[bass.ds(i, 1), :, :].rearrange("a p (b t) -> p (a b) t", b=NB), xe[:, :, NM:])\
                    .then_inc(s("kept"), 16)
                sp_.wait_ge(s("swaT"), 1)
                sp_.dma_start(swaT_d[bass.ds(i, 1), :, :].rearrange("a p n -> p (a n)"), swaT).then_inc(s("kept"), 16)
                sp_.wait_ge(s("step_done"), 4)
                sp_.wait_ge(s("kept"), 48)
                sp_.sem_clear(range(min(z.num for z in sems.values()), max(z.num for z in sems.values()) + 1))
                sp_.sem_inc(step_go, 1)
            for dst, src in late_loads:
                sp_.dma_start(dst, src, allow_slow_non_contiguous=True).then_inc(s2("e_loaded"), 16)
            sp_.wait_ge(once("step2_done"), 3)
            for z in (s2(n) for n in ("lr", "db1", "stepped", "updated", "e_turned", "e_even", "e_odd", "w2_turned", "ready2", "e_loaded")):
                sp_.sem_clear(z)
            sp_.sem_inc(once("step2_go"), 1)
            with sp_.Fori(0, PAIRS) as i:
                sp_.dma_start(bx2T, x2T_d[bass.ds(i, 1), :, :].rearrange("a p n -> p (a n)")).then_inc(s2("in_x2T"), 16)
                sp_.dma_start(bswaT, swaT_d[bass.ds(i, 1), :, :].rearrange("a p n -> p (a n)")).then_inc(s2("in_swaT"), 16)
                sp_.dma_start(bx2, x2_d[bass.ds(i, 1), :, :].rearrange("a p n -> p (a n)")).then_inc(s2("in_x2"), 16)
                sp_.wait_ge(s2("x4"), NT)
                sp_.dma_start(out[bass.ds(i * NB, NB), :, :].rearrange("b (t p) d -> p b t d", p=P),
                              y.rearrange("p (b t d) -> p b t d", b=NB, d=D)).then_inc(s2("stored"), 16)
                sp_.wait_ge(s2("step_done"), 3)
                sp_.wait_ge(s2("stored"), 16)
                sp_.sem_clear(range(min(z.num for z in sems.values()), max(z.num for z in sems.values()) + 1))
                sp_.sem_inc(once("step2_go"), 1)


_INS = [
    "L0_attn_hidden_states", "L0_attn_w_q", "L0_attn_w_k", "L0_attn_w_v", "L0_attn_w_b", "L0_attn_conv_q_w",
    "L0_attn_conv_k_w", "L0_attn_conv_v_w", "L0_attn_fir1", "L0_attn_fir3", "L0_attn_fir7", "L0_attn_fir15",
    "L0_attn_fir31", "L0_attn_gate_w1", "L0_attn_gate_b1", "L0_attn_gate_w2", "L0_attn_gate_b2",
    "L0_attn_norm_w", "L0_attn_w_o", "L0_ffn_gate_w", "L0_ffn_down_w", "L0_ffn_down_b", "L0_ffn_up_w",
    "L0_ffn_up_b", "L1_attn_mem", "L1_attn_wq", "L1_attn_wk", "L1_attn_wv", "L1_attn_wo", "L1_attn_w1",
    "L1_attn_b1", "L1_attn_w2", "L1_attn_b2", "L1_attn_lin1", "L1_attn_lin2", "L1_attn_alpha",
    "L1_attn_theta", "L1_ffn_Wr", "L1_ffn_br", "L1_ffn_W1", "L1_ffn_b1", "L1_ffn_W2", "L1_ffn_b2",
    "L1_ffn_gamma", "L1_ffn_beta",
]
_OUTS = [((B, L, D), "float32")]


def kernel(**inputs):
    import numpy as _np
    import concourse.bacc as _bacc
    from concourse import mybir as _mybir
    from concourse.bass_utils import run_bass_kernel_spmd as _run

    nc = _bacc.Bacc("TRN2", target_bir_lowering=False, num_devices=1)
    arrays, args = {}, {}
    for name in _INS:
        a = _np.ascontiguousarray(inputs[name])
        if a.ndim == 0:
            a = a.reshape(1)
        arrays[f"in_{name}_dram"] = a
        args[name] = nc.dram_tensor(f"in_{name}_dram", a.shape, _mybir.dt.from_np(a.dtype), kind="ExternalInput").ap()
    outs = []
    for i, (shape, dtype) in enumerate(_OUTS):
        dt = _mybir.dt.from_np(_np.dtype(dtype))
        outs.append(nc.dram_tensor(f"out_{i}_dram", shape, dt, kind="ExternalOutput").ap())
    program(nc, args, outs[0])
    r = _run(nc, [arrays], core_ids=[0])
    got = tuple(r.results[0][f"out_{i}_dram"] for i in range(len(_OUTS)))
    return got[0]
```

```python
from contextlib import ExitStack

import numpy as np
import concourse.bass as bass
import concourse.mybir as mybir

F32 = mybir.dt.float32
F32R = mybir.dt.float32r
ACT = mybir.ActivationFunctionType
ALU = mybir.AluOpType
AX = mybir.AxisListType

P = 128
D = 128
B, L = 8, 512
H, DH = 4, 32
CH = 32
NB = 2
PAIRS = B // NB
T = NB * L
NT = T // P
NC = L // CH
G = NB * NC
S7 = 7
FIRS = (1, 3, 7, 15, 31)
FOFF = (0, 1, 4, 11, 26)
PADC, PADF = 3, 30
BANK = 512
E = 8
NM = 64
FH = 512
NEG = -1e30


def program(nc, A, out):
    ctx = ExitStack()
    with ctx:
        def sb(name, shape, dt=F32):
            return ctx.enter_context(nc.sbuf_tensor(name, shape, dt))

        PS = ctx.enter_context(nc.psum_tensor("PS", [P, 8 * BANK], F32))

        def banks(first, n=1):
            return PS[:, first * BANK:(first + n) * BANK]

        arena = {"front": sb("front", [P, 9 * T]), "middle": sb("middle", [P, 23 * T + 256])}
        used = {"front": 0, "middle": 0}

        def part(where, name, *shape):
            size = int(np.prod(shape))
            at = used[where]
            used[where] = at + size
            assert at + size <= arena[where].shape[1], (name, at + size)
            v = arena[where][:, at:at + size]
            if len(shape) == 2:
                v = v.rearrange("p (a b) -> p a b", a=shape[0])
            if len(shape) == 3:
                v = v.rearrange("p (a b c) -> p a b c", a=shape[0], b=shape[1])
            return v

        def part_in(name, *shape):
            return part("middle", name, *shape)

        ident = sb("ident", [P, P])
        ones = sb("ones", [P, P])
        headones = sb("headones", [P, P])
        statsel = sb("statsel", [P, S7, 28])
        den_sel = sb("den_sel", [64, 28], F32R)
        expand = sb("expand", [64, S7, P], F32R)
        keep_j_le_i = sb("keep_j_le_i", [P, CH])
        low_free = sb("low_free", [P, CH, CH])
        eye_quad = sb("eye_quad", [P, DH])
        eps6 = sb("eps6", [P, 1])
        eps5 = sb("eps5", [P, 1])
        one1 = sb("one1", [P, 1])
        w_q, w_k, w_v = sb("w_q", [D, D]), sb("w_k", [D, D]), sb("w_v", [D, D])
        w_b = sb("w_b", [D, H])
        w_bx = sb("w_bx", [D, D])
        conv_w = sb("conv_w", [P, 3, 4])
        fir_w = sb("fir_w", [P, 57])
        fir_diag = sb("fir_diag", [P, 31, P])
        gw1a = sb("gw1a", [D, 256])
        gw1b = sb("gw1b", [28, 256])
        gb1 = sb("gb1", [P, 2])
        gw2 = sb("gw2", [P, 2, 28])
        gb2 = sb("gb2", [28, 1])
        norm_col = sb("norm_col", [P, 1])
        w_o = sb("w_o", [P, D])
        w_on = sb("w_on", [P, D])

        gwT = sb("gwT", [D, E])
        dn_in = part_in("dn_in", 4, P)
        up_in = part_in("up_in", E, 64)
        w1_in = part_in("w1_in", 4, D)
        sq_in = part_in("sq_in", 4, D)
        mem_in = sb("mem_in", [NM, D])
        m_q = part("middle", "m_q", NM)
        m_v = part("middle", "m_v", H, DH + 1)
        m_sc = part("middle", "m_sc", H, NM)
        m_st = part("middle", "m_st", 2, H)
        m_prT = part("middle", "m_prT", H, NM)
        m_ao = part("middle", "m_ao", D)
        m_aoT = part("middle", "m_aoT", NM)
        m_swaT = part("middle", "m_swaT", NM)
        m_aT = part("middle", "m_aT", 4, NM)
        m_eT = part("middle", "m_eT", NM)
        m_e = part("middle", "m_e", D)
        m_zb, m_a, m_th, m_t1 = (part("middle", n, FH) for n in ("m_zb", "m_a", "m_th", "m_t1"))
        zero_in, den_in, expand_in = part("middle", "zero_in", T)[0:64], part("middle", "den_in", 28)[0:64], part("middle", "expand_in", S7, P)[0:64]
        dnT = sb("dnT", [P, 4, P])
        upT = sb("upT", [P, 4, D])
        dnb = sb("dnb", [P, 4])
        upb = sb("upb", [E, D])
        w1T = sb("w1T", [P, 4, P])
        w2 = sb("w2", [P, FH])
        w2T = sb("w2T", [P, 4, D])
        aw = sb("aw", [P, 4, D])
        memT = sb("memT", [P, NM])
        b1c = sb("b1c", [P, 4])
        b1r = sb("b1r", [P, FH])
        b2c = sb("b2c", [P, 1])
        eight_low = sb("eight_low", [P, E, E])
        pick = sb("pick", [P, 4, E])
        wmask = sb("wmask", [P, P])
        gW1, gW2, dzsum = sb("gW1", [P, FH]), sb("gW2", [P, FH]), sb("dzsum", [P, FH])
        gb2s = sb("gb2s", [P, 1])
        esum = sb("esum", [P, 1])

        arena["late"] = fir_diag[:, :, :].rearrange("p k c -> p (k c)")
        used["late"] = 0
        lin_in = part("late", "lin_in", 2, D)
        lT = part("late", "lT", 2, D)
        keep_lr = sb("keep_lr", [P, 2])
        wrT = part("late", "wrT", E)
        brr = part("late", "brr", E)
        b1e = part("late", "b1e", E, 4)
        b2e = part("late", "b2e", D)[0:E]
        gamma_r, beta_r = part("late", "gamma_r", D), part("late", "beta_r", D)

        used["middle"] = 0
        x_tc = sb("x_tc", [P, NT, D])
        xe = sb("xe", [P, NB, NM + L])
        xT = xe[:, :, NM:]
        v_pad = sb("v_pad", [P, NB, PADF + L])
        conv = part("front", "conv", 3, NB, L)
        sq = part("front", "sq", 2, T)
        nrm = sq
        beta = part("front", "beta", T)
        ab = part("front", "ab", 2, T)
        acc = part("front", "acc", T)
        used["front"] = 0
        hmid = part("front", "hmid", 2, T)
        sp = part("front", "sp", 3, T)
        sp = sp[0:28]
        halves = sb("halves", [64, T], F32R)
        stats = part("front", "stats", T)[0:28]

        kbq = part("middle", "kbq", 2, T)
        k_n = part("middle", "k_n", T)
        vb = part("middle", "vb", T)
        Dm = part("middle", "Dm", CH, CH)
        Dt = part("middle", "Dt", G, CH)
        tmp = part("middle", "tmp", 256)
        ka = part("middle", "ka", G, 64)
        kv = part("middle", "kv", G, 64)
        before = used["middle"]
        q_raw, k_raw, v_raw = (part("middle", n, NB, PADC + L) for n in ("q_raw", "k_raw", "v_raw"))
        used["middle"] = before
        wu = part("middle", "wu", G, 64)
        pt = part("middle", "pt", G, DH)
        gk = part("middle", "gk", NB, NC, DH)
        qwT = part("middle", "qwT", T)
        fir = part("middle", "fir", 5, T)
        delta = part("middle", "delta", T)
        state = part("middle", "state", NB, NC, DH)
        used["middle"] = 0
        x1T = part("middle", "x1T", NB, L)
        hf = part("middle", "hf", 4, T)
        ups = part("middle", "ups", NB, 4, D)
        x1 = part("middle", "x1", NT, D)
        x2 = part("middle", "x2", NT, D)
        qs = part("middle", "qs", T)
        ve = part("middle", "ve", 2 * NT, H, DH + 1)
        sc = [part("middle", f"sc{b}", H * 4, P) for b in range(NB)]
        prT = [part("middle", f"prT{b}", H * 4, P) for b in range(NB)]
        ao = part("middle", "ao", NT, D)
        aoT = part("middle", "aoT", T)
        swaT = part("middle", "swaT", T)
        pooled_b = part("middle", "pooled_b", NB, P)
        c_rows = part("middle", "c_rows", NB, P)[0:E]
        pair8, eq8 = (part("middle", n, NB * E, E).rearrange("p (b e) f -> p b e f", b=NB) for n in ("pair8", "eq8"))
        used["middle"], used["front"] = 0, 0
        eT = part("middle", "eT", NB, L)
        e_tc = part("middle", "e_tc", NT, D)
        aT = part("front", "aT", 4, T)
        zb, a_tc, th, t1, dz = (part("front", n, 2, FH) for n in ("zb", "a_tc", "th", "t1", "dz"))
        ke = sb("ke", [P, NB, NM + L])
        bn6 = sb("bn6", [P, NT, 6])
        bn2 = sb("bn2", [P, NT, 2])
        rstd = sb("rstd", [P, NT])
        used["middle"], used["front"] = 0, 0
        w1eT = part("middle", "w1eT", E, 4, P)
        w2eT = part("middle", "w2eT", E, 4, D)
        before = used["middle"]
        hT = [part("middle", f"hT{o}", 4, T) for o in range(2)]
        used["middle"] = before
        w1n = part("middle", "w1n", E, 4, D)
        w2n = part("middle", "w2n", E, FH)
        bx2T, bswaT, bx2, omT, mT, x3, x3T = (part("middle", n, T) for n in ("bx2T", "bswaT", "bx2", "omT", "mT", "x3", "x3T"))
        baT = part("front", "baT", 4, T)
        tg = part("front", "tg", 2, T)
        tok_pair, tok_equal = (tg[:, n, 0:NT * E * E].rearrange("p (t e f) -> p t e f", e=E, f=E) for n in range(2))
        y = part("front", "y", T)
        x3_keep = part("front", "x3_keep", T)
        rwT = part("front", "rwT", T)[0:E]
        x3T_keep = x_tc[:, :, :].rearrange("p t d -> p (t d)")
        rw = part("late", "rw", 5, NT, E)
        rw_keep = part("late", "rw_keep", NT, E)
        pooled = sb("pooled", [P, NB])
        rt = sb("rt", [P, 8, 2 * E])
        cvec = sb("cvec", [P, NB, 4])
        cdiag = sb("cdiag", [E, NB, E])
        cd = sb("cd", [E, NB])
        mx = sb("mx", [P, NB, H * 4])
        ri = sb("ri", [P, NT, H])

        sems = {}

        def s(name):
            if name not in sems:
                sems[name] = ctx.enter_context(nc.semaphore(name))
            return sems[name]

        second = {}

        def s2(name):
            if name not in second:
                second[name] = list(sems.values())[len(second)]
            return second[name]

        single = {}

        def once(name):
            if name not in single:
                single[name] = ctx.enter_context(nc.semaphore(name))
            return single[name]

        loaded, masks, prepared, step_go = (
            once(n) for n in ("loaded", "masks", "prepared", "step_go"))
        for n in ("turned", "turned_sb", "m_pe", "m_dve", "m_act", "m_done", "step2_done", "step2_go"):
            once(n)
        loads = [
            (w_q[:, :], A["L0_attn_w_q"]), (w_k[:, :], A["L0_attn_w_k"]), (w_v[:, :], A["L0_attn_w_v"]),
            (w_b[:, :], A["L0_attn_w_b"]), (conv_w[:, 0, :], A["L0_attn_conv_q_w"]),
            (conv_w[:, 1, :], A["L0_attn_conv_k_w"]), (conv_w[:, 2, :], A["L0_attn_conv_v_w"]),
            (gw1a[:, :], A["L0_attn_gate_w1"][0:D, :]), (gw1b[:, :], A["L0_attn_gate_w1"][D:D + 28, :]),
            (gb1[:, :], A["L0_attn_gate_b1"].rearrange("(m p) -> p m", p=P)),
            (gw2[:, :, :], A["L0_attn_gate_w2"].rearrange("(m p) c -> p m c", p=P)),
            (gb2[:, :], A["L0_attn_gate_b2"].rearrange("(p a) -> p a", a=1)),
            (w_o[:, :], A["L0_attn_w_o"]),
        ]
        loads += [(fir_w[:, FOFF[n]:FOFF[n] + k], A[f"L0_attn_fir{k}"]) for n, k in enumerate(FIRS)]
        loads += [(norm_col[DH * h:DH * h + DH, :], A["L0_attn_norm_w"].rearrange("(p a) -> p a", a=1)) for h in range(H)]
        loads += [
            (gwT[:, :], A["L0_ffn_gate_w"].rearrange("e d -> d e")),
            (dn_in, A["L0_ffn_down_w"].rearrange("e c d -> (e c) d").rearrange("(m p) d -> p m d", p=P)),
            (up_in, A["L0_ffn_up_w"].rearrange("e d c -> d e c")),
            (dnb[:, :], A["L0_ffn_down_b"].rearrange("(m a) c -> (a c) m", a=2)),
            (upb[:, :], A["L0_ffn_up_b"]),
            (w1_in, A["L1_attn_w1"].rearrange("(m p) d -> p m d", p=P)),
            (w2[:, :], A["L1_attn_w2"]),
            (mem_in[:, :], A["L1_attn_mem"]),
            (b1c[:, :], A["L1_attn_b1"].rearrange("(m p) -> p m", p=P)),
            (b2c[:, :], A["L1_attn_b2"].rearrange("(p a) -> p a", a=1)),
            (b1r[:, :], A["L1_attn_b1"].partition_broadcast(P)),
        ]
        late_loads = [
            (lin_in[:, 0, :], A["L1_attn_lin1"]), (lin_in[:, 1, :], A["L1_attn_lin2"]),
            (wrT, A["L1_ffn_Wr"].rearrange("e d -> d e")),
            (brr, A["L1_ffn_br"].partition_broadcast(P)),
            (b1e, A["L1_ffn_b1"].rearrange("e (m p) -> p e m", p=P)),
            (b2e, A["L1_ffn_b2"]),
            (gamma_r, A["L1_ffn_gamma"].partition_broadcast(P)),
            (beta_r, A["L1_ffn_beta"].partition_broadcast(P)),
            (w1n, A["L1_ffn_W1"].rearrange("e (m p) d -> p e m d", p=P)),
            (w2n, A["L1_ffn_W2"].rearrange("e d f -> d e f")),
        ]
        loads += [
            (keep_lr[:, 0:1], A["L1_attn_alpha"].partition_broadcast(P)),
            (keep_lr[:, 1:2], A["L1_attn_theta"].partition_broadcast(P)),
        ]
        loads += [(sq_in[:, n, :], A[f"L1_attn_w{c}"]) for n, c in enumerate("qkvo")]
        x2T_d = nc.dram_tensor("x2T_d", [PAIRS, P, T], F32).ap()
        swaT_d = nc.dram_tensor("swaT_d", [PAIRS, P, T], F32).ap()
        x2_d = nc.dram_tensor("x2_d", [PAIRS, P, T], F32).ap()
        block = ctx.enter_context(nc.Block())

        @block.gpsimd
        def _(pool):
            n = 0

            def fill(t, v):
                nonlocal n
                if n:
                    pool.wait_ge(masks, n)
                pool.memset(t, v).then_inc(masks, 1)
                n += 1

            def keep(t, op, pattern, base, mult, value):
                nonlocal n
                pool.wait_ge(masks, n)
                pool.affine_select(out=t, in_=t, compare_op=op, fill=value, base=base, pattern=pattern,
                                   channel_multiplier=mult).then_inc(masks, 1)
                n += 1

            fill(ident[:, :], 0.0)
            keep(ident[:, :], ALU.not_equal, [[-1, P]], 0, 1, 1.0)
            fill(ones[:, :], 1.0)
            for t, v in ((headones, 1.0),):
                fill(t[:, :], v)
                keep(t[:, :].rearrange("p (h d) -> p h d", h=H), ALU.is_ge, [[-DH, H], [0, DH]], 0, 1, 0.0)
                keep(t[:, :].rearrange("p (h d) -> p h d", h=H), ALU.is_ge, [[DH, H], [0, DH]], DH - 1, -1, 0.0)
            fill(statsel[:, :, :], 0.0)
            for k in range(S7):
                pool.wait_ge(masks, n)
                for h in range(H):
                    fill(statsel[DH * h:DH * h + DH, k, 4 * k + h:4 * k + h + 1], 1 / DH)
            fill(zero_in, 0.0)
            fill(den_in, 0.0)
            fill(expand_in, 0.0)
            for r in (slice(0, 28), slice(32, 60)):
                v = den_in[r, :].rearrange("p (h k) -> p h k", h=H)
                fill(v, 1.0)
                keep(v, ALU.is_ge, [[-S7, H], [0, S7]], 0, 1, 0.0)
                keep(v, ALU.is_ge, [[S7, H], [0, S7]], S7 - 1, -1, 0.0)
                keep(expand_in[r, :, :].rearrange("p k (h d) -> p k h d", h=H), ALU.not_equal,
                     [[-1, S7], [-S7, H], [0, DH]], 0, 1, 1.0)
            for h in range(H):
                fill(keep_j_le_i[DH * h:DH * h + DH, :], 1.0)
                keep(keep_j_le_i[DH * h:DH * h + DH, :], ALU.is_ge, [[1, CH]], 0, -1, 0.0)
                fill(eye_quad[DH * h:DH * h + DH, :], 0.0)
                keep(eye_quad[DH * h:DH * h + DH, :], ALU.not_equal, [[-1, CH]], 0, 1, 1.0)
            fill(low_free[:, :, :], -1.0)
            keep(low_free[:, :, :], ALU.is_gt, [[1, CH], [-1, CH]], 0, 0, 0.0)
            fill(eps6[:, :], 1e-6)
            fill(eps5[:, :], 1e-5)
            fill(one1[:, :], 1.0)
            fill(eight_low[:, :, :], 1.0)
            keep(eight_low[:, :, :], ALU.is_gt, [[1, E], [-1, E]], 0, 0, 0.0)
            for half in range(2):
                v = pick[64 * half:64 * half + 64, :, :]
                fill(v, 0.0)
                keep(v, ALU.not_equal, [[-2, 4], [1, E]], -half, 0, 1.0)
                v = wmask[64 * half:64 * half + 64, :]
                fill(v, 0.0)
                keep(v, ALU.is_gt, [[1, P]], 0, -1, NEG)
                keep(v, ALU.is_ge, [[-1, P]], NM, 1, NEG)
            fill(v_pad[:, :, 0:PADF], 0.0)
            pool.wait_ge(masks, n)
            pool.wait_ge(loaded, 16 * len(loads))
            for j in range(31):
                pool.tensor_scalar(fir_diag[:, j, :], ident[:, :], fir_w[:, FOFF[4] + j:FOFF[4] + j + 1], None,
                                   ALU.mult).then_inc(masks, 1)
                n += 1
            pool.wait_ge(masks, n)
            pool.sem_inc(prepared, 1)
            pool.wait_ge(once("m_done"), 1)
            with pool.Fori(0, PAIRS) as i:
                for t in (q_raw, k_raw, v_raw):
                    pool.memset(t[:, :, 0:PADC], 0.0).then_inc(s("pads"), 1)
                pool.wait_ge(s("x1"), NT)
                pool.memset(ve[:, :, :, DH:DH + 1], 1.0).then_inc(s("ones_column"), 1)
                for t in range(NT):
                    pool.wait_ge(s("dz"), t + 1)
                    if t:
                        pool.wait_ge(s("dzsum"), t)
                    pool.tensor_tensor(dzsum[:, :], dzsum[:, :], dz[:, t % 2, :], ALU.add).then_inc(s("dzsum"), 1)
                pool.wait_ge(s("dzsum"), NT)
                pool.sem_inc(s("step_done"), 1)
                pool.wait_ge(step_go, i + 1)

        @block.vector
        def _(dve):
            dve.wait_ge(loaded, 16 * len(loads))
            dve.tensor_copy(w_bx[:, :].rearrange("p (h d) -> p h d", h=H),
                            w_b[:, :].unsqueeze(2).broadcast_to([P, H, DH])).then_inc(prepared, 1)
            dve.tensor_scalar(w_on[:, :], w_o[:, :], norm_col[:, 0:1], None, ALU.mult).then_inc(prepared, 1)
            dve.wait_ge(prepared, 3)
            for dst, src in ((halves[:, :], zero_in), (den_sel[:, :], den_in), (expand[:, :, :], expand_in)):
                dve.tensor_copy(dst, src).then_inc(prepared, 1)
            for n, dst in enumerate((dnT, upT, w1T, w2T, aw)):
                dve.wait_ge(once("turned"), n + 1)
                dve.tensor_copy(dst[:, :, :], banks(n).rearrange("p (m c) -> p m c", c=P)).then_inc(once("turned_sb"), 1)
            dve.wait_ge(once("turned"), 6)
            dve.tensor_copy(memT[:, :], banks(5)[:, 0:NM]).then_inc(once("turned_sb"), 1)
            dve.tensor_copy(xe[:, :, 0:NM], banks(5)[:, 0:NM].unsqueeze(1).broadcast_to([P, NB, NM]))
            dve.memset(dzsum[NM:P, :], 0.0)
            dve.wait_ge(once("m_pe"), 1)
            dve.tensor_copy(m_q, banks(0)[:, 0:NM]).then_inc(once("m_dve"), 1)
            dve.tensor_copy(ke[:, :, 0:NM], banks(0)[:, NM:2 * NM].unsqueeze(1).broadcast_to([P, NB, NM])).then_inc(once("m_dve"), 1)
            dve.memset(m_v[0:NM, :, DH:DH + 1], 1.0)
            dve.tensor_copy(m_v[0:NM, :, 0:DH], banks(0)[0:NM, P:P + D].rearrange("p (h d) -> p h d", h=H)).then_inc(once("m_dve"), 1)
            dve.wait_ge(once("m_pe"), 2)
            dve.tensor_tensor(m_sc[0:NM, :, :], banks(2, 4)[0:NM].rearrange("p (h k) -> p h k", h=H)[:, :, 0:NM],
                              wmask[0:NM, NM:].unsqueeze(1).broadcast_to([NM, H, NM]), ALU.add).then_inc(once("m_dve"), 1)
            dve.wait_ge(once("m_dve"), 4)
            dve.tensor_reduce(m_st[0:NM, 0, :], m_sc[0:NM, :, :], AX.X, ALU.max).then_inc(once("m_dve"), 1)
            dve.wait_ge(once("m_dve"), 5)
            dve.tensor_tensor(m_sc[0:NM, :, :], m_sc[0:NM, :, :], m_st[0:NM, 0, :].unsqueeze(2).broadcast_to([NM, H, NM]),
                              ALU.subtract).then_inc(once("m_dve"), 1)
            dve.wait_ge(once("m_pe"), 3)
            dve.tensor_copy(m_prT[0:NM, :, :], banks(6)[0:NM, 0:H * NM].rearrange("p (h q) -> p h q", h=H)).then_inc(once("m_dve"), 1)
            dve.wait_ge(once("m_pe"), 4)
            pv = banks(7)[0:NM, 0:H * 33].rearrange("p (h e) -> p h e", h=H)
            dve.reciprocal(m_st[0:NM, 1, :].unsqueeze(2), pv[:, :, DH:DH + 1]).then_inc(once("m_dve"), 1)
            dve.wait_ge(once("m_dve"), 8)
            dve.tensor_tensor(m_ao[0:NM, :].rearrange("p (h e) -> p h e", h=H), pv[:, :, 0:DH],
                              m_st[0:NM, 1, :].unsqueeze(2).broadcast_to([NM, H, DH]), ALU.mult).then_inc(once("m_dve"), 1)
            dve.wait_ge(once("m_pe"), 5)
            dve.tensor_copy(m_aoT, banks(0)[:, 0:NM]).then_inc(once("m_dve"), 1)
            dve.wait_ge(once("m_pe"), 6)
            dve.tensor_copy(m_swaT, banks(1)[:, 0:NM]).then_inc(once("m_dve"), 1)
            dve.wait_ge(once("m_pe"), 8)
            dve.tensor_tensor(m_zb[0:NM, :], banks(5)[0:NM], b1r[0:NM, :], ALU.add).then_inc(once("m_dve"), 1)
            dve.wait_ge(once("m_pe"), 9)
            dve.wait_ge(once("m_dve"), 11)
            dve.scalar_tensor_tensor(out=m_eT, in0=banks(3)[:, 0:NM], scalar=b2c[:, 0:1], in1=m_swaT, op0=ALU.add,
                                     op1=ALU.subtract).then_inc(once("m_dve"), 1)
            dve.wait_ge(once("m_dve"), 13)
            dve.tensor_scalar(m_eT, m_eT, float(B), None, ALU.mult).then_inc(once("m_dve"), 1)
            dve.wait_ge(once("m_dve"), 14)
            dve.tensor_reduce(gb2s[:, :], m_eT, AX.X, ALU.add)
            dve.wait_ge(once("m_pe"), 10)
            dve.tensor_copy(m_e[0:NM, :], banks(4)[0:NM, 0:P]).then_inc(once("m_dve"), 1)
            dve.wait_ge(once("m_act"), 7)
            dve.scalar_tensor_tensor(out=m_t1[0:NM, :], in0=m_zb[0:NM, :], scalar=1.0, in1=m_a[0:NM, :], op0=ALU.add,
                                     op1=ALU.subtract).then_inc(once("m_dve"), 1)
            dve.wait_ge(once("m_dve"), 16)
            dve.scalar_tensor_tensor(out=m_t1[0:NM, :], in0=m_th[0:NM, :], scalar=1.0, in1=m_t1[0:NM, :], op0=ALU.add,
                                     op1=ALU.mult).then_inc(once("m_dve"), 1)
            dve.wait_ge(once("m_dve"), 17)
            dve.wait_ge(once("m_pe"), 11)
            dve.scalar_tensor_tensor(out=m_t1[0:NM, :], in0=m_t1[0:NM, :], scalar=0.5, in1=banks(6)[0:NM], op0=ALU.mult,
                                     op1=ALU.mult).then_inc(once("m_dve"), 1)
            dve.wait_ge(once("m_dve"), 18)
            dve.tensor_copy(dzsum[0:NM, :], m_t1[0:NM, :])
            dve.wait_ge(once("m_pe"), 12)
            dve.tensor_copy(gW2[:, :], banks(7))
            dve.tensor_copy(gW1[:, :], banks(0)).then_inc(once("m_done"), 1)
            dve.wait_ge(once("m_done"), 1)
            with dve.Fori(0, PAIRS) as i:
                def convolve(name, src, dst):
                    dve.wait_ge(s(name + "_raw"), 2)
                    c = {"q": 0, "k": 1, "v": 2}[name]
                    for j in range(4):
                        sh, w = src[:, :, j:j + L], conv_w[:, c, j:j + 1]
                        if j == 0:
                            ins = dve.tensor_scalar(dst, sh, w, None, ALU.mult)
                        else:
                            dve.wait_ge(s(name + "_conv"), j)
                            ins = dve.scalar_tensor_tensor(out=dst, in0=sh, scalar=w, in1=dst, op0=ALU.mult, op1=ALU.add)
                        ins.then_inc(s(name + "_conv"), 1)

                def fir_tap(n, j):
                    k = FIRS[n]
                    dst = fir[:, n, :].rearrange("p (b t) -> p b t", b=NB)
                    sh = v_pad[:, :, PADF - k + 1 + j:PADF - k + 1 + j + L]
                    w = fir_w[:, FOFF[n] + j:FOFF[n] + j + 1]
                    if j == 0:
                        dve.wait_ge(s("v_act"), 1)
                        ins = dve.tensor_scalar(dst, sh, w, None, ALU.mult)
                    else:
                        dve.wait_ge(s(f"fir{k}"), j)
                        ins = dve.scalar_tensor_tensor(out=dst, in0=sh, scalar=w, in1=dst, op0=ALU.mult, op1=ALU.add)
                    ins.then_inc(s(f"fir{k}"), 1)

                dve.wait_ge(s("pads"), 3)
                convolve("v", v_raw, conv[:, 2])
                convolve("k", k_raw, conv[:, 1])
                convolve("q", q_raw, conv[:, 0])
                dve.wait_ge(s("beta_tanh"), 1)
                dve.tensor_scalar(beta[:, :], beta[:, :], 0.5, 0.5, ALU.mult, ALU.add).then_inc(s("beta"), 1)
                dve.wait_ge(s("k_rnorm"), 1)
                dve.tensor_tensor(k_n[:, :], k_n[:, :], nrm[:, 1, :], ALU.mult).then_inc(s("k_n"), 1)
                dve.wait_ge(s("q_rnorm"), 1)
                dve.tensor_tensor(kbq[:, 1, :], kbq[:, 1, :], nrm[:, 0, :], ALU.mult).then_inc(s("kbq"), 1)
                dve.wait_ge(s("k_n"), 1)
                dve.wait_ge(s("beta"), 1)
                dve.tensor_tensor(kbq[:, 0, :], k_n[:, :], beta[:, :], ALU.mult).then_inc(s("kbq"), 1)
                dve.wait_ge(s("v_act"), 1)
                dve.tensor_tensor(vb[:, :].rearrange("p (b t) -> p b t", b=NB), v_pad[:, :, PADF:],
                                  beta[:, :].rearrange("p (b t) -> p b t", b=NB), ALU.mult).then_inc(s("vb"), 1)
                dve.transpose(ka[:, :, 0:32], k_n[:, :].rearrange("p (g i) -> p g i", g=G)).then_inc(s("ka"), 1)
                dve.wait_ge(s("kbq"), 2)
                dve.transpose(kv[:, :, 0:32], kbq[:, 0, :].rearrange("p (g i) -> p g i", g=G)).then_inc(s("kv"), 1)
                dve.wait_ge(s("vb"), 1)
                dve.transpose(kv[:, :, 32:64], vb[:, :].rearrange("p (g i) -> p g i", g=G)).then_inc(s("kv"), 1)
                for j in range(3):
                    fir_tap(1, j)
                dve.wait_ge(s("r1"), 4)
                for half in range(2):
                    src = banks(6 if half == 0 else 0, 2).rearrange("p (g c) -> p g c", c=64)
                    dve.tensor_tensor(ka[:, 16 * half:16 * half + 16, 32:64], src[:, :, 32:64],
                                      keep_j_le_i[:, :].unsqueeze(1).broadcast_to([P, 16, CH]),
                                      ALU.mult).then_inc(s("ka"), 1)
                    dve.tensor_copy(wu[:, 16 * half:16 * half + 16, 0:32], src[:, :, 0:32]).then_inc(s("a_copy"), 1)
                dve.wait_ge(s("a_copy"), 2)
                dve.transpose(Dm[:, :, :], wu[:, :, 0:32].rearrange("p g i -> p i g")).then_inc(s("inv"), 1)
                dve.wait_ge(s("inv"), 1)
                dve.tensor_tensor(Dm[:, :, :], Dm[:, :, :], low_free[:, :, :], ALU.mult).then_inc(s("inv"), 1)
                for j in range(1, CH - 1):
                    r = CH - 1 - j
                    dve.wait_ge(s("inv"), 2 * j)
                    t2 = tmp[:, 0:r * j].rearrange("p (r c) -> p r c", c=j)
                    dve.tensor_tensor(t2, Dm[:, j + 1:, j:j + 1].broadcast_to([P, r, j]),
                                      Dm[:, j:j + 1, 0:j].broadcast_to([P, r, j]), ALU.mult).then_inc(s("inv"), 1)
                    dve.wait_ge(s("inv"), 1 + 2 * j)
                    dve.tensor_tensor(Dm[:, j + 1:, 0:j], Dm[:, j + 1:, 0:j], t2, ALU.add).then_inc(s("inv"), 1)
                dve.wait_ge(s("inv"), 2 + 2 * 30)
                dve.transpose(Dt[:, :, :].rearrange("p g i -> p i g"), Dm[:, :, :]).then_inc(s("inv"), 1)
                dve.wait_ge(s("inv"), 3 + 2 * 30)
                dve.tensor_tensor(Dt[:, :, :], Dt[:, :, :], eye_quad[:, :].unsqueeze(1).broadcast_to([P, G, CH]), ALU.add)\
                    .then_inc(s("Dt"), 1)
                for j in range(7):
                    fir_tap(2, j)
                dve.wait_ge(s("r3"), 4)
                src = banks(0, 4).rearrange("p (g c) -> p g c", c=64)
                dve.scalar_tensor_tensor(out=pt[:, :, :], in0=src[:, :, 0:32], scalar=-1.0,
                                         in1=eye_quad[:, :].unsqueeze(1).broadcast_to([P, G, DH]),
                                         op0=ALU.mult, op1=ALU.add).then_inc(s("pt"), 1)
                dve.tensor_tensor(qwT[:, :].rearrange("p (g i) -> p g i", g=G),
                                  kbq[:, 1, :].rearrange("p (g i) -> p g i", g=G), src[:, :, 32:64],
                                  ALU.subtract).then_inc(s("qwT"), 1)
                dve.wait_ge(s("gk"), 1)
                dve.tensor_copy(state[:, :, 1, :], gk[:, :, 0, :]).then_inc(s("state"), 1)
                for n in range(1, NC - 1):
                    fir_tap(3, n - 1)
                    dve.wait_ge(s("scan"), n)
                    dve.tensor_tensor(state[:, :, n + 1, :], banks(6)[:, 0:64].rearrange("p (b e) -> p b e", b=NB),
                                      gk[:, :, n, :], ALU.add).then_inc(s("state"), 1)
                fir_tap(3, 14)
                dve.wait_ge(s("logits"), 2)
                dve.tensor_scalar(sp[:, 0, :], banks(2, 2)[0:28], gb2[:, 0:1], 0.0, ALU.add, ALU.max).then_inc(s("sp_max"), 1)
                dve.wait_ge(s("sp_max"), 1)
                dve.wait_ge(s("sp_ln"), 1)
                dve.scalar_tensor_tensor(out=sp[:, 2, :], in0=sp[:, 1, :], scalar=0.02, in1=sp[:, 0, :],
                                         op0=ALU.add, op1=ALU.add).then_inc(s("wraw"), 1)

                def in_halves(n):
                    dve.tensor_copy(halves[0:28], sp[:, 2, :]).then_inc(s("halves"), 1)
                    dve.wait_ge(s("halves"), 2 * n + 1)
                    dve.tensor_tensor(halves[32:60], sp[:, 2, :], halves[0:28].bitcast(F32), ALU.subtract).then_inc(s("halves"), 1)

                dve.wait_ge(s("wraw"), 1)
                in_halves(0)
                dve.wait_ge(s("rden"), 1)
                dve.tensor_tensor(sp[:, 2, :], sp[:, 2, :], sp[:, 0, :], ALU.mult).then_inc(s("wts"), 1)
                dve.wait_ge(s("wts"), 1)
                in_halves(1)
                for k in range(S7):
                    st = fir[:, k, :] if k < 5 else delta[:, :] if k == 5 else v_pad[:, :, PADF:]
                    dve.wait_ge(s("expand"), 2 * k + 2)
                    if k == 0:
                        dve.wait_ge(s("streams"), 7)
                    src = banks(4 + 2 * (k % 2), 2)
                    dst = acc[:, :] if k == 0 else ab[:, k % 2, :]
                    if k == 6:
                        src, dst = (z.rearrange("p (b t) -> p b t", b=NB) for z in (src, dst))
                    if k >= 3:
                        dve.wait_ge(s("o_sum"), k - 2)
                    dve.tensor_tensor(dst, src, st, ALU.mult).then_inc(s("prod"), 1)
                    if k:
                        dve.wait_ge(s("prod"), k + 1)
                        if k > 1:
                            dve.wait_ge(s("o_sum"), k - 1)
                        dve.tensor_tensor(acc[:, :], acc[:, :], ab[:, k % 2, :], ALU.add).then_inc(s("o_sum"), 1)
                dve.wait_ge(s("o_rroot"), 1)
                dve.tensor_tensor(acc[:, :], acc[:, :], ab[:, 1, :], ALU.mult).then_inc(s("o_n"), 1)
                dve.wait_ge(s("attn_out"), 2)
                dve.tensor_tensor(x1[:, :, :], banks(0, 2).rearrange("p (t d) -> p t d", d=D), x_tc[:, :, :],
                                  ALU.add).then_inc(s("ln_res"), 1)
                dve.wait_ge(s("ln_res"), 1)
                for t in range(NT):
                    dve.bn_stats(bn6[:, t, :], x1[:, t, :]).then_inc(s("ln_stats"), 1)
                for t in range(NT):
                    if t == 0:
                        dve.wait_ge(s("ln_stats"), NT)
                    dve.bn_aggr(bn2[:, t, :], bn6[:, t, :]).then_inc(s("ln_var"), 1)
                dve.wait_ge(s("ln_root"), 1)
                dve.reciprocal(rstd[:, :], rstd[:, :]).then_inc(s("ln_rstd"), 1)
                dve.wait_ge(s("ln_rstd"), 1)
                for t in range(NT):
                    dve.tensor_scalar(x1[:, t, :], x1[:, t, :], bn2[:, t, 0:1], rstd[:, t:t + 1],
                                      ALU.subtract, ALU.mult).then_inc(s("x1"), 1)
                dve.wait_ge(s("x1T"), 2)
                for b in range(NB):
                    dve.tensor_scalar(pooled_b[:, b, :], ones[:, :], pooled[:, b:b + 1], 1 / L, ALU.mult, ALU.mult)\
                        .then_inc(s("pooled_b"), 1)
                e8 = lambda n: rt[:, n, :].rearrange("p (b e) -> p b e", b=NB)
                e1 = lambda n: rt[:, n, 0:NB]
                wide = lambda ap: ap.unsqueeze(2).broadcast_to([P, NB, E])
                dve.wait_ge(s("gate8"), 1)
                dve.tensor_reduce(e1(0), banks(6)[:, 0:2 * E].rearrange("p (b e) -> p b e", b=NB), AX.X, ALU.max)\
                    .then_inc(s("choice"), 1)
                dve.wait_ge(s("choice"), 1)
                dve.tensor_tensor(e8(1), banks(6)[:, 0:2 * E].rearrange("p (b e) -> p b e", b=NB), wide(e1(0)),
                                  ALU.subtract).then_inc(s("choice"), 1)
                dve.wait_ge(s("gate_exp"), 1)
                dve.tensor_reduce(e1(2), e8(1), AX.X, ALU.add).then_inc(s("choice"), 1)
                dve.wait_ge(s("choice"), 3)
                dve.reciprocal(e1(3), e1(2)).then_inc(s("choice"), 1)
                dve.wait_ge(s("choice"), 4)
                dve.tensor_tensor(e8(4), e8(1), wide(e1(3)), ALU.mult).then_inc(s("choice"), 1)
                dve.wait_ge(s("choice"), 5)
                mine = e8(4).unsqueeze(3).broadcast_to([P, NB, E, E])
                others = e8(4).unsqueeze(2).broadcast_to([P, NB, E, E])
                dve.tensor_tensor(pair8[:, :, :, :], others, mine, ALU.is_gt).then_inc(s("choice"), 1)
                dve.tensor_tensor(eq8[:, :, :, :], others, mine, ALU.is_equal).then_inc(s("choice"), 1)
                dve.wait_ge(s("choice"), 7)
                dve.tensor_tensor(eq8[:, :, :, :], eq8[:, :, :, :], eight_low[:, :, :].unsqueeze(1).broadcast_to([P, NB, E, E]),
                                  ALU.mult).then_inc(s("choice"), 1)
                dve.wait_ge(s("choice"), 8)
                dve.tensor_tensor(pair8[:, :, :, :], pair8[:, :, :, :], eq8[:, :, :, :], ALU.add).then_inc(s("choice"), 1)
                dve.wait_ge(s("choice"), 9)
                dve.tensor_reduce(e8(5), pair8[:, :, :, :], AX.X, ALU.add).then_inc(s("choice"), 1)
                dve.wait_ge(s("choice"), 10)
                dve.scalar_tensor_tensor(out=e8(5), in0=e8(5), scalar=1.5, in1=e8(4), op0=ALU.is_lt, op1=ALU.mult)\
                    .then_inc(s("choice"), 1)
                dve.wait_ge(s("choice"), 11)
                dve.tensor_reduce(e1(2), e8(5), AX.X, ALU.add).then_inc(s("choice"), 1)
                dve.wait_ge(s("choice"), 12)
                dve.tensor_scalar(e1(2), e1(2), 1e-8, None, ALU.add).then_inc(s("choice"), 1)
                dve.wait_ge(s("choice"), 13)
                dve.reciprocal(e1(3), e1(2)).then_inc(s("choice"), 1)
                dve.wait_ge(s("choice"), 14)
                dve.tensor_tensor(e8(6), e8(5), wide(e1(3)), ALU.mult).then_inc(s("choice"), 1)
                dve.wait_ge(s("choice"), 15)
                for b in range(NB):
                    dve.tensor_tensor(pair8[:, b, 0:4, :], e8(6)[:, b:b + 1, :].broadcast_to([P, 4, E]), pick[:, :, :],
                                      ALU.mult).then_inc(s("choice"), 1)
                dve.tensor_tensor(cdiag[:, :, :], e8(6)[0:E], ident[0:E, 0:E].unsqueeze(1).broadcast_to([E, NB, E]),
                                  ALU.mult).then_inc(s("choice"), 1)
                dve.wait_ge(s("choice"), 18)
                dve.tensor_reduce(cvec[:, :, :], pair8[:, :, 0:4, :], AX.X, ALU.add).then_inc(s("choice"), 1)
                dve.tensor_reduce(cd[:, :], cdiag[:, :, :], AX.X, ALU.add).then_inc(s("choice"), 1)
                dve.wait_ge(s("choice"), 20)
                for b in range(NB):
                    for m in range(4):
                        dve.tensor_scalar(ups[:, b, m, :], upT[:, m, :], cvec[:, b, m:m + 1], None, ALU.mult).then_inc(s("ups"), 1)
                    dve.tensor_scalar(c_rows[:, b, :], ones[0:E, :], cd[:, b:b + 1], None, ALU.mult).then_inc(s("ups"), 1)

                def norm(name, psum, resid, dst):
                    dve.wait_ge(s(name + "_out"), 2)
                    dve.tensor_tensor(dst[:, :, :], psum.rearrange("p (t d) -> p t d", d=D), resid[:, :, :],
                                      ALU.add).then_inc(s("ln_res"), 1)
                    dve.wait_ge(s("ln_res"), 2)
                    for t in range(NT):
                        dve.bn_stats(bn6[:, t, :], dst[:, t, :]).then_inc(s("ln_stats"), 1)
                    dve.wait_ge(s("ln_stats"), 2 * NT)
                    for t in range(NT):
                        dve.bn_aggr(bn2[:, t, :], bn6[:, t, :]).then_inc(s("ln_var"), 1)
                    dve.wait_ge(s("ln_root"), 2)
                    dve.reciprocal(rstd[:, :], rstd[:, :]).then_inc(s("ln_rstd"), 1)
                    dve.wait_ge(s("ln_rstd"), 2)
                    for t in range(NT):
                        dve.tensor_scalar(dst[:, t, :], dst[:, t, :], bn2[:, t, 0:1], rstd[:, t:t + 1],
                                          ALU.subtract, ALU.mult).then_inc(s(name), 1)

                norm("x2", banks(2, 2), x1, x2)
                for half in range(2):
                    dve.wait_ge(s("v_proj2"), 2 * half + 2)
                    dve.tensor_copy(ve[:, 8 * half:8 * half + 8, :, 0:DH],
                                    banks((6, 0)[half], 2).rearrange("p (j h d) -> p j h d", h=H, d=DH)).then_inc(s("ve"), 1)
                for b in range(NB):
                    for m in range(2):
                        dve.wait_ge(s("scores"), 4 * b + 2 * m + 2)
                        bank = ((2, 4), (6, 0))[b][m]
                        dve.tensor_tensor(sc[b][:, 8 * m:8 * m + 8, :], banks(bank, 2).rearrange("p (n k) -> p n k", k=P),
                                          wmask[:, :].unsqueeze(1).broadcast_to([P, 8, P]), ALU.add).then_inc(s("masked"), 1)
                    dve.wait_ge(s("masked"), 2 * b + 2)
                    dve.tensor_reduce(mx[:, b, :], sc[b], AX.X, ALU.max).then_inc(s("row_max"), 1)
                    dve.wait_ge(s("row_max"), b + 1)
                    dve.tensor_tensor(sc[b], sc[b], mx[:, b, :].unsqueeze(2).broadcast_to([P, 16, P]), ALU.subtract)\
                        .then_inc(s("shifted"), 1)
                for t in range(NT):
                    if t % 4 == 0:
                        dve.wait_ge(s("pv"), t // 4 + 1)
                    at = banks(2 + t // 2)[:, (t % 2) * 132:(t % 2) * 132 + 132].rearrange("p (h e) -> p h e", h=H)
                    dve.reciprocal(ri[:, t, :].unsqueeze(2), at[:, :, DH:DH + 1]).then_inc(s("ri"), 1)
                    dve.wait_ge(s("ri"), t + 1)
                    dve.tensor_tensor(ao[:, t, :].rearrange("p (h e) -> p h e", h=H), at[:, :, 0:DH],
                                      ri[:, t, :].unsqueeze(2).broadcast_to([P, H, DH]), ALU.mult).then_inc(s("ao"), 1)
                dve.wait_ge(s("pred"), 2)
                dve.wait_ge(s("swaT"), 1)
                dve.scalar_tensor_tensor(out=eT.rearrange("p b t -> p (b t)"), in0=banks(2, 2), scalar=b2c[:, 0:1], in1=swaT,
                                         op0=ALU.add, op1=ALU.subtract).then_inc(s("eT"), 1)
                def z_bias(t):
                    dve.wait_ge(s("z"), t + 1)
                    dve.tensor_tensor(zb[:, t % 2, :], banks((6, 0)[t % 2]), b1r[:, :], ALU.add).then_inc(s("zb"), 1)

                z_bias(0)
                for t in range(NT):
                    o = t % 2
                    if t + 1 < NT:
                        z_bias(t + 1)
                    if t >= 2:
                        dve.wait_ge(s("dw"), t - 1)
                    if t == 0:
                        dve.wait_ge(s("eT"), 1)
                        dve.tensor_reduce(esum[:, :], eT.rearrange("p b t -> p (b t)"), AX.X, ALU.add).then_inc(s("esum"), 1)
                        dve.wait_ge(s("esum"), 1)
                        dve.tensor_tensor(gb2s[:, :], gb2s[:, :], esum[:, :], ALU.add).then_inc(s("gb2"), 1)
                    dve.wait_ge(s("a_th"), 2 * t + 2)
                    if t >= 2:
                        dve.wait_ge(s("dzsum"), t - 1)
                    dve.scalar_tensor_tensor(out=t1[:, o, :], in0=zb[:, o, :], scalar=1.0, in1=a_tc[:, o, :], op0=ALU.add,
                                             op1=ALU.subtract).then_inc(s("dz_steps"), 1)
                    dve.wait_ge(s("dz_steps"), 2 * t + 1)
                    dve.scalar_tensor_tensor(out=t1[:, o, :], in0=th[:, o, :], scalar=1.0, in1=t1[:, o, :], op0=ALU.add,
                                             op1=ALU.mult).then_inc(s("dz_steps"), 1)
                    dve.wait_ge(s("dz_steps"), 2 * t + 2)
                    dve.wait_ge(s("da"), t + 1)
                    dve.scalar_tensor_tensor(out=dz[:, o, :], in0=t1[:, o, :], scalar=0.5, in1=banks((7, 1)[o]), op0=ALU.mult,
                                             op1=ALU.mult).then_inc(s("dz"), 1)
                dve.wait_ge(s("dw"), NT)
                dve.tensor_tensor(gW2[:, :], gW2[:, :], banks(2), ALU.add).then_inc(s("gw"), 1)
                dve.tensor_tensor(gW1[:, :], gW1[:, :], banks(3), ALU.add).then_inc(s("gw"), 1)
                dve.wait_ge(s("gw"), 2)
                dve.wait_ge(s("gb2"), 1)
                dve.sem_inc(s("step_done"), 1)
                dve.wait_ge(step_go, i + 1)

            dve.tensor_scalar(keep_lr[:, 0:1], keep_lr[:, 0:1], -1.0, 1.0, ALU.mult, ALU.add).then_inc(s2("lr"), 1)
            dve.tensor_scalar(keep_lr[:, 1:2], keep_lr[:, 1:2], -1.0, None, ALU.mult).then_inc(s2("lr"), 1)
            dve.wait_ge(s2("lr"), 2)
            one_less, step = keep_lr[:, 0:1], keep_lr[:, 1:2]
            w1flat = w1T[:, :, :].rearrange("p m c -> p (m c)")
            dve.wait_ge(s2("db1"), 1)
            for grad, g_in in ((gW2[:, :], gW2[:, :]), (gW1[:, :], gW1[:, :]), (gb2s[:, :], gb2s[:, :]), (rt[:, 0, 0:4], banks(7)[:, 0:4])):
                dve.tensor_scalar(grad, g_in, step, None, ALU.mult).then_inc(s2("stepped"), 1)
            for n, (w, grad) in enumerate(((w2[:, :], gW2[:, :]), (w1flat, gW1[:, :]), (b2c[:, :], gb2s[:, :]), (b1c[:, :], rt[:, 0, 0:4]))):
                dve.wait_ge(s2("stepped"), n + 1)
                dve.scalar_tensor_tensor(out=w, in0=w, scalar=one_less, in1=grad, op0=ALU.mult, op1=ALU.add)\
                    .then_inc(s2("updated"), 1)
            for n in range(0, 16, 2):
                dve.wait_ge(s2("e_turned"), n + 1)
                dst = w1eT[:, n, :, :] if n < 8 else w2eT[:, n - 8, :, :]
                dve.tensor_copy(dst, banks(n % 8).rearrange("p (m c) -> p m c", m=4)).then_inc(s2("e_even"), 1)
            dve.wait_ge(s2("w2_turned"), 1)
            dve.tensor_copy(w2T[:, :, :], banks(0).rearrange("p (m c) -> p m c", m=4)).then_inc(s2("ready2"), 1)
            dve.wait_ge(s2("w2_turned"), 2)
            dve.tensor_copy(lT[:, :, :], banks(1)[:, 0:2 * D].rearrange("p (m c) -> p m c", m=2)).then_inc(s2("ready2"), 1)
            dve.wait_ge(s2("updated"), 4)
            dve.wait_ge(s2("ready2"), 2)
            dve.sem_inc(once("step2_done"), 1)
            dve.wait_ge(once("step2_go"), 1)

            def norm2(name, src, dst):
                for t in range(NT):
                    dve.bn_stats(bn6[:, t, :], src[:, t * D:(t + 1) * D]).then_inc(s2(name + "_stats"), 1)
                dve.wait_ge(s2(name + "_stats"), NT)
                for t in range(NT):
                    dve.bn_aggr(bn2[:, t, :], bn6[:, t, :]).then_inc(s2(name + "_var"), 1)
                dve.wait_ge(s2(name + "_root"), 1)
                dve.reciprocal(rstd[:, :], rstd[:, :]).then_inc(s2(name + "_rstd"), 1)
                dve.wait_ge(s2(name + "_rstd"), 1)
                for t in range(NT):
                    dve.tensor_scalar(dst[:, t * D:(t + 1) * D], src[:, t * D:(t + 1) * D], bn2[:, t, 0:1], rstd[:, t:t + 1],
                                      ALU.subtract, ALU.mult).then_inc(s2(name), 1)

            def merge():
                dve.wait_ge(s2("tg"), 1)
                dve.scalar_tensor_tensor(out=mT, in0=tg[:, 0, :], scalar=1.0, in1=bswaT, op0=ALU.add, op1=ALU.mult)\
                    .then_inc(s2("merge"), 1)
                dve.wait_ge(s2("tg"), 2)
                dve.scalar_tensor_tensor(out=tg[:, 1, :], in0=tg[:, 1, :], scalar=1.0, in1=omT, op0=ALU.add, op1=ALU.mult)\
                    .then_inc(s2("merge"), 1)
                dve.wait_ge(s2("merge"), 2)
                dve.tensor_tensor(mT, mT, tg[:, 1, :], ALU.add).then_inc(s2("merged"), 1)

            def third_norm():
                dve.wait_ge(s2("in_x2"), 16)
                dve.wait_ge(s2("m_turned"), 2)
                dve.scalar_tensor_tensor(out=x3, in0=banks(4, 2), scalar=0.5, in1=bx2, op0=ALU.mult, op1=ALU.add)\
                    .then_inc(s2("x3_res"), 1)
                dve.wait_ge(s2("x3_res"), 1)
                norm2("x3", x3, x3)

            def route():
                dve.wait_ge(s2("r_logits"), 1)
                wide3 = lambda ap: ap.unsqueeze(2).broadcast_to([P, NT, E])
                col = lambda n: rw[:, 4, n, 0:NT]
                dve.tensor_tensor(rw[:, 0], banks(4)[:, 0:NT * E].rearrange("p (t e) -> p t e", e=E),
                                  brr[:, :].unsqueeze(1).broadcast_to([P, NT, E]), ALU.add).then_inc(s2("route"), 1)
                dve.wait_ge(s2("route"), 1)
                dve.tensor_reduce(col(0), rw[:, 0], AX.X, ALU.max).then_inc(s2("route"), 1)
                dve.wait_ge(s2("route"), 2)
                dve.tensor_tensor(rw[:, 1], rw[:, 0], wide3(col(0)), ALU.subtract).then_inc(s2("route"), 1)
                mine = rw[:, 0].unsqueeze(3).broadcast_to([P, NT, E, E])
                others = rw[:, 0].unsqueeze(2).broadcast_to([P, NT, E, E])
                dve.tensor_tensor(tok_pair, others, mine, ALU.is_gt).then_inc(s2("route"), 1)
                dve.tensor_tensor(tok_equal, others, mine, ALU.is_equal).then_inc(s2("route"), 1)
                dve.wait_ge(s2("route"), 5)
                dve.tensor_tensor(tok_equal, tok_equal, eight_low[:, :, :].unsqueeze(1).broadcast_to([P, NT, E, E]),
                                  ALU.mult).then_inc(s2("route"), 1)
                dve.wait_ge(s2("route"), 6)
                dve.tensor_tensor(tok_pair, tok_pair, tok_equal, ALU.add).then_inc(s2("route"), 1)
                dve.wait_ge(s2("route"), 7)
                dve.tensor_reduce(rw[:, 2], tok_pair, AX.X, ALU.add).then_inc(s2("route"), 1)
                dve.wait_ge(s2("route"), 8)
                dve.wait_ge(s2("r_exp"), 1)
                dve.scalar_tensor_tensor(out=rw[:, 2], in0=rw[:, 2], scalar=1.5, in1=rw[:, 1], op0=ALU.is_lt, op1=ALU.mult)\
                    .then_inc(s2("route"), 1)
                dve.wait_ge(s2("route"), 9)
                dve.tensor_reduce(col(1), rw[:, 2], AX.X, ALU.add).then_inc(s2("route"), 1)
                dve.wait_ge(s2("route"), 10)
                dve.reciprocal(col(2), col(1)).then_inc(s2("route"), 1)
                dve.wait_ge(s2("route"), 11)
                dve.tensor_tensor(rw[:, 3], rw[:, 2], wide3(col(2)), ALU.mult).then_inc(s2("weights"), 1)

            def fourth_norm(yn, scaled, x4):
                norm2(yn, y, y)
                y3 = y.rearrange("p (t d) -> p t d", d=D)
                dve.wait_ge(s2(yn), NT)
                dve.tensor_tensor(y3, y3, gamma_r[:, :].unsqueeze(1).broadcast_to([P, NT, D]), ALU.mult).then_inc(s2(scaled), 1)
                dve.wait_ge(s2(scaled), 1)
                dve.tensor_tensor(y3, y3, beta_r[:, :].unsqueeze(1).broadcast_to([P, NT, D]), ALU.add).then_inc(s2(scaled), 1)
                dve.wait_ge(s2(scaled), 2)
                dve.tensor_tensor(y, y, x3_keep, ALU.add).then_inc(s2(scaled), 1)
                dve.wait_ge(s2(scaled), 3)
                norm2(x4, y, x3_keep)

            def experts(first, last):
                dve.tensor_copy(rw_keep, rw[:, 3]).then_inc(s2("rw_keep"), 1)
                if not first:
                    fourth_norm("yn", "scaled", "x4")
                    dve.wait_ge(s2("x4"), NT)
                dve.wait_ge(s2("y_bias"), 2)
                dve.tensor_tensor(y, banks(0, 2), x3, ALU.add).then_inc(s2("y"), 1)
                dve.wait_ge(s2("rw_keep"), 1)
                for e in range(E):
                    for t in range(NT):
                        if t % 4 == 0:
                            dve.wait_ge(s2("o"), 2 * e + t // 4 + 1)
                        dve.wait_ge(s2("y"), 1 + max(0, NT * (e - 1) + t + 1))
                        yt = y[:, t * D:(t + 1) * D]
                        bank = (6, 0)[e % 2] + t // 4
                        dve.scalar_tensor_tensor(out=yt, in0=banks(bank)[:, (t % 4) * D:(t % 4 + 1) * D], scalar=rw_keep[:, t, e:e + 1],
                                                 in1=yt, op0=ALU.mult, op1=ALU.add).then_inc(s2("y"), 1)
                    if e == 3 and not last:
                        merge()
                    if e == 4:
                        if not first:
                            dve.wait_ge(s2("stored"), 16)
                        dve.tensor_copy(x3_keep, x3).then_inc(s2("x3_keep"), 1)
                        if not last:
                            dve.wait_ge(s2("x3_keep"), 1)
                            third_norm()
                    if e == 6 and not last:
                        route()
                dve.wait_ge(s2("y"), 1 + NT * E)
                dve.wait_ge(s2("x3_keep"), 1)

            merge()
            third_norm()
            route()
            dve.wait_ge(s2("weights"), 1)
            dve.sem_inc(s2("step_done"), 1)
            dve.wait_ge(once("step2_go"), 2)
            experts(True, False)
            dve.sem_inc(s2("step_done"), 1)
            dve.wait_ge(once("step2_go"), 3)
            with dve.Fori(1, PAIRS - 1) as i:
                experts(False, False)
                dve.wait_ge(s2("weights"), 1)
                dve.sem_inc(s2("step_done"), 1)
                dve.wait_ge(once("step2_go"), i + 3)
            experts(False, True)
            fourth_norm("last_yn", "last_scaled", "last_x4")

        @block.scalar
        def _(act):
            act.wait_ge(prepared, 3)
            act.wait_ge(once("m_dve"), 6)
            act.activation(m_sc[0:NM, :, :], m_sc[0:NM, :, :], ACT.Exp, scale=DH ** -0.5).then_inc(once("m_act"), 1)
            act.wait_ge(once("m_pe"), 7)
            for m in range(4):
                act.activation(m_aT[:, m, :], banks(2)[:, m * NM:(m + 1) * NM], ACT.Silu, bias=b1c[:, m:m + 1])\
                    .then_inc(once("m_act"), 1)
            act.wait_ge(once("m_dve"), 12)
            act.activation(m_a[0:NM, :], m_zb[0:NM, :], ACT.Silu).then_inc(once("m_act"), 1)
            act.activation(m_th[0:NM, :], m_zb[0:NM, :], ACT.Tanh, scale=0.5).then_inc(once("m_act"), 1)
            act.wait_ge(once("m_done"), 1)
            with act.Fori(0, PAIRS) as i:
                for b in range(NB):
                    act.wait_ge(s("x_turned"), b + 1)
                    act.activation(xT[:, b, :], banks(b), ACT.Copy).then_inc(s("xT"), 1)
                for name, dst, bank in (("v", v_raw, 6), ("k", k_raw, 4), ("q", q_raw, 2)):
                    for b in range(NB):
                        act.wait_ge(s(name + "_proj"), b + 1)
                        act.activation(dst[:, b, PADC:], banks(bank + b), ACT.Copy).then_inc(s(name + "_raw"), 1)
                act.wait_ge(s("b_proj"), 2)
                act.activation(beta[:, :], banks(0, 2), ACT.Tanh, scale=0.5).then_inc(s("beta_tanh"), 1)
                act.wait_ge(s("v_conv"), 4)
                act.activation(v_pad[:, :, PADF:], conv[:, 2], ACT.Silu).then_inc(s("v_act"), 1)
                act.wait_ge(s("k_conv"), 4)
                act.activation(k_n[:, :], conv[:, 1].rearrange("p b t -> p (b t)"), ACT.Silu).then_inc(s("k_act"), 1)
                act.wait_ge(s("k_act"), 1)
                act.activation(sq[:, 1, :], k_n[:, :], ACT.Square).then_inc(s("k_sq"), 1)
                act.wait_ge(s("q_conv"), 4)
                act.activation(kbq[:, 1, :], conv[:, 0].rearrange("p b t -> p (b t)"), ACT.Silu).then_inc(s("q_act"), 1)
                act.wait_ge(s("q_act"), 1)
                act.activation(sq[:, 0, :], kbq[:, 1, :], ACT.Square).then_inc(s("q_sq"), 1)
                act.wait_ge(s("k_ss"), 2)
                act.activation(nrm[:, 1, :], banks(4, 2), ACT.Ln, bias=eps6[:, 0:1]).then_inc(s("k_norm"), 1)
                act.wait_ge(s("q_ss"), 2)
                act.activation(nrm[:, 0, :], banks(0, 2), ACT.Ln, bias=eps6[:, 0:1]).then_inc(s("q_norm"), 1)
                act.wait_ge(s("k_norm"), 1)
                act.activation(nrm[:, 1, :], nrm[:, 1, :], ACT.Exp, scale=-0.5).then_inc(s("k_rnorm"), 1)
                act.wait_ge(s("q_norm"), 1)
                act.activation(nrm[:, 0, :], nrm[:, 0, :], ACT.Exp, scale=-0.5).then_inc(s("q_rnorm"), 1)
                act.wait_ge(s("v_act"), 1)
                act.activation(fir[:, 0, :].rearrange("p (b t) -> p b t", b=NB), v_pad[:, :, PADF:], ACT.Copy,
                               scale=fir_w[:, 0:1]).then_inc(s("fir1"), 1)

                def magnitude(n, src, k):
                    if n >= 2:
                        act.wait_ge(s("stat"), 2 * (n - 1))
                    dst = ab[:, n % 2, :]
                    if k == 6:
                        dst = dst.rearrange("p (b t) -> p b t", b=NB)
                    act.activation(dst, src, ACT.Abs).then_inc(s("streams"), 1)

                magnitude(0, v_pad[:, :, PADF:], 6)
                act.wait_ge(s("fir1"), 1)
                magnitude(1, fir[:, 0, :], 0)
                act.wait_ge(s("fir31_psum"), 2)
                act.activation(fir[:, 4, :], banks(2, 2), ACT.Copy).then_inc(s("fir31"), 1)
                for m in range(2):
                    act.wait_ge(s("r2"), 2 * m + 2)
                    act.activation(wu[:, 16 * m:16 * m + 16, :].rearrange("p g c -> p (g c)"), banks(4 + 2 * m, 2),
                                   ACT.Copy).then_inc(s("wu"), 1)
                act.wait_ge(s("r4"), 2)
                act.activation(gk[:, :, :, :].rearrange("p b n e -> p (b n e)"), banks(4, 2), ACT.Copy).then_inc(s("gk"), 1)
                act.wait_ge(s("delta_psum"), 1)
                act.activation(delta[:, :], banks(0, 2), ACT.Copy).then_inc(s("delta"), 1)
                act.wait_ge(s("fir3"), 3)
                magnitude(2, fir[:, 1, :], 1)
                act.wait_ge(s("fir31"), 1)
                magnitude(3, fir[:, 4, :], 4)
                act.wait_ge(s("fir7"), 7)
                magnitude(4, fir[:, 2, :], 2)
                act.wait_ge(s("fir15"), 15)
                magnitude(5, fir[:, 3, :], 3)
                act.wait_ge(s("delta"), 1)
                magnitude(6, delta[:, :], 5)
                act.wait_ge(s("stat"), 14)
                act.activation(stats[:, :], banks(4, 2)[0:28], ACT.Copy).then_inc(s("stats"), 1)
                for m in range(2):
                    act.wait_ge(s("gate_h"), 2 * m + 2)
                    act.activation(hmid[:, m, :], banks((6, 2)[m], 2), ACT.Gelu, bias=gb1[:, m:m + 1]).then_inc(s("hmid"), 1)
                act.wait_ge(s("logits"), 2)
                act.wait_ge(s("sp_max"), 1)
                act.activation(sp[:, 1, :], banks(2, 2)[0:28], ACT.Abs, bias=gb2[:, 0:1]).then_inc(s("sp_abs"), 1)
                act.wait_ge(s("sp_abs"), 1)
                act.activation(sp[:, 1, :], sp[:, 1, :], ACT.Exp, scale=-1.0).then_inc(s("sp_exp"), 1)
                act.wait_ge(s("sp_exp"), 1)
                act.activation(sp[:, 1, :], sp[:, 1, :], ACT.Ln, bias=one1[0:28, 0:1]).then_inc(s("sp_ln"), 1)
                act.wait_ge(s("den"), 2)
                act.activation(sp[:, 0, :], banks(0, 2)[0:28], ACT.Ln).then_inc(s("ln_den"), 1)
                act.wait_ge(s("ln_den"), 1)
                act.activation(sp[:, 0, :], sp[:, 0, :], ACT.Exp, scale=-1.0).then_inc(s("rden"), 1)
                act.wait_ge(s("o_sum"), 6)
                act.activation(ab[:, 1, :], acc[:, :], ACT.Square).then_inc(s("o_sq"), 1)
                act.wait_ge(s("o_ms"), 2)
                act.activation(ab[:, 1, :], banks(2, 2), ACT.Ln, bias=eps5[:, 0:1], scale=1 / DH).then_inc(s("o_root"), 1)
                act.wait_ge(s("o_root"), 1)
                act.activation(ab[:, 1, :], ab[:, 1, :], ACT.Exp, scale=-0.5).then_inc(s("o_rroot"), 1)
                act.wait_ge(s("ln_var"), NT)
                act.activation(rstd[:, :], bn2[:, :, 1], ACT.Sqrt, bias=eps5[:, 0:1]).then_inc(s("ln_root"), 1)
                for b in range(NB):
                    act.wait_ge(s("x1_turned"), b + 1)
                    act.activation(x1T[:, b, :], banks(4 + b), ACT.Copy, accum_out=pooled[:, b:b + 1]).then_inc(s("x1T"), 1)
                act.wait_ge(s("choice"), 2)
                act.activation(rt[:, 1, :], rt[:, 1, :], ACT.Exp).then_inc(s("gate_exp"), 1)
                for m in range(4):
                    act.wait_ge(s("down"), 2 * m + 2)
                    act.activation(hf[:, m, :], banks((2, 0, 4, 6)[m], 2), ACT.Gelu, bias=dnb[:, m:m + 1]).then_inc(s("hf"), 1)
                act.wait_ge(s("ln_var"), 2 * NT)
                act.activation(rstd[:, :], bn2[:, :, 1], ACT.Sqrt, bias=eps5[:, 0:1]).then_inc(s("ln_root"), 1)
                for b in range(NB):
                    act.wait_ge(s("x2_turned"), b + 1)
                    act.activation(xe[:, b, NM:], banks(b), ACT.Copy).then_inc(s("xe"), 1)
                act.wait_ge(s("q_proj2"), 2)
                act.activation(qs, banks(2, 2), ACT.Copy).then_inc(s("qs"), 1)
                act.wait_ge(s("k_proj2"), 2)
                act.activation(ke[:, :, NM:], banks(4, 2).rearrange("p (b t) -> p b t", b=NB), ACT.Copy).then_inc(s("ke"), 1)
                for b in range(NB):
                    act.wait_ge(s("shifted"), b + 1)
                    act.activation(sc[b], sc[b], ACT.Exp, scale=DH ** -0.5).then_inc(s("probs"), 1)
                    for m in range(2):
                        act.wait_ge(s("probs_turned"), 4 * b + 2 * m + 2)
                        bank = ((2, 4), (6, 0))[b][m]
                        act.activation(prT[b][:, 8 * m:8 * m + 8, :].rearrange("p n q -> p (n q)"), banks(bank, 2), ACT.Copy)\
                            .then_inc(s("prT"), 1)
                act.wait_ge(s("ao_turned"), 2)
                act.activation(aoT, banks(6, 2), ACT.Copy).then_inc(s("aoT"), 1)
                act.wait_ge(s("wo"), 2)
                act.activation(swaT, banks(0, 2), ACT.Copy).then_inc(s("swaT"), 1)
                for n in range(8):
                    b, m = n // 4, n % 4
                    act.wait_ge(s("zT"), n + 1)
                    act.activation(aT[:, m, b * L:(b + 1) * L], banks(4 + n % 2), ACT.Silu, bias=b1c[:, m:m + 1])\
                        .then_inc(s("aT"), 1)
                act.wait_ge(s("e_turned"), 2)
                act.activation(e_tc.rearrange("p t d -> p (t d)"), banks(4, 2), ACT.Copy).then_inc(s("e_tc"), 1)
                for t in range(NT):
                    o = t % 2
                    act.wait_ge(s("zb"), t + 1)
                    if t >= 2:
                        act.wait_ge(s("dw"), t - 1)
                    act.activation(a_tc[:, o, :], zb[:, o, :], ACT.Silu).then_inc(s("a_th"), 1)
                    act.activation(th[:, o, :], zb[:, o, :], ACT.Tanh, scale=0.5).then_inc(s("a_th"), 1)
                act.wait_ge(s("a_th"), 2 * NT)
                act.sem_inc(s("step_done"), 1)
                act.wait_ge(step_go, i + 1)

            for n in range(1, 16, 2):
                act.wait_ge(s2("e_turned"), n + 1)
                dst = w1eT[:, n, :, :] if n < 8 else w2eT[:, n - 8, :, :]
                act.activation(dst.rearrange("p m c -> p (m c)"), banks(n % 8), ACT.Copy).then_inc(s2("e_odd"), 1)
            act.wait_ge(s2("e_odd"), 8)
            act.sem_inc(once("step2_done"), 1)
            act.wait_ge(once("step2_go"), 1)

            def memory_hidden(n):
                b, m = n // 4, n % 4
                act.wait_ge(s2("zT"), n + 1)
                act.activation(baT[:, m, b * L:(b + 1) * L], banks(4 + n % 2), ACT.Silu, bias=b1c[:, m:m + 1]).then_inc(s2("aT"), 1)

            def memory_out():
                act.wait_ge(s2("om"), 2)
                act.activation(omT, banks(4, 2), ACT.Identity, bias=b2c[:, 0:1]).then_inc(s2("omT"), 1)

            def gate(n):
                act.wait_ge(s2(f"g{n + 1}"), 2)
                act.activation(tg[:, n, :], banks(4, 2), ACT.Tanh, scale=0.5).then_inc(s2("tg"), 1)

            def root(name):
                act.wait_ge(s2(name + "_var"), NT)
                act.activation(rstd[:, :], bn2[:, :, 1], ACT.Sqrt, bias=eps5[:, 0:1]).then_inc(s2(name + "_root"), 1)

            def x3_transposed():
                act.wait_ge(s2("x3_turned"), 2)
                act.activation(x3T, banks(4, 2), ACT.Copy).then_inc(s2("x3T"), 1)

            def route_exp():
                act.wait_ge(s2("route"), 3)
                act.activation(rw[:, 1], rw[:, 1], ACT.Exp).then_inc(s2("r_exp"), 1)

            def weights_transposed():
                act.wait_ge(s2("rw_turned"), 1)
                act.activation(rwT, banks(4, 2)[0:E], ACT.Copy).then_inc(s2("rwT"), 1)

            def hidden(e, m):
                for b in range(NB):
                    act.wait_ge(s2("h"), 2 * (4 * e + m) + b + 1)
                    if e >= 2:
                        act.wait_ge(s2("o"), 2 * (e - 1))
                    act.activation(hT[e % 2][:, m, b * L:(b + 1) * L], banks(2 + b), ACT.Relu, bias=b1e[:, e, m:m + 1])\
                        .then_inc(s2("hT"), 1)

            def experts(first, last):
                for m in range(4):
                    hidden(0, m)
                    if m == 1:
                        if not first:
                            root("yn")
                        act.activation(x3T_keep, x3T, ACT.Copy).then_inc(s2("x3T_keep"), 1)
                for e in range(E):
                    for m in range(4):
                        if e + 1 < E:
                            hidden(e + 1, m)
                        if e == 0 and m == 0 and not first:
                            root("x4")
                        if e == 0 and not last:
                            memory_hidden(2 * m)
                            memory_hidden(2 * m + 1)
                    if last:
                        continue
                    if e == 1:
                        memory_out()
                    if e == 2:
                        gate(0)
                    if e == 3:
                        gate(1)
                    if e == 4:
                        root("x3")
                    if e == 5:
                        x3_transposed()
                    if e == 6:
                        route_exp()
                    if e == 7:
                        weights_transposed()

            for n in range(8):
                memory_hidden(n)
            memory_out()
            gate(0)
            gate(1)
            root("x3")
            x3_transposed()
            route_exp()
            weights_transposed()
            act.wait_ge(s2("rwT"), 1)
            act.sem_inc(s2("step_done"), 1)
            act.wait_ge(once("step2_go"), 2)
            experts(True, False)
            act.wait_ge(s2("rwT"), 1)
            act.sem_inc(s2("step_done"), 1)
            act.wait_ge(once("step2_go"), 3)
            with act.Fori(1, PAIRS - 1) as i:
                experts(False, False)
                act.wait_ge(s2("rwT"), 1)
                act.sem_inc(s2("step_done"), 1)
                act.wait_ge(once("step2_go"), i + 3)
            experts(False, True)
            root("last_yn")
            root("last_x4")

        @block.tensor
        def _(pe):
            pe.wait_ge(prepared, 3)
            up_blocks = up_in.rearrange("p (m a) c -> p m (a c)", a=2)
            for n, block_of in enumerate((lambda m: dn_in[:, m, :], lambda m: up_blocks[:, m, :], lambda m: w1_in[:, m, :],
                                          lambda m: w2[:, m * P:(m + 1) * P], lambda m: sq_in[:, m, :])):
                for m in range(4):
                    mm = pe.transpose(banks(n)[:, m * P:(m + 1) * P], block_of(m), ident[:, :])
                mm.then_inc(once("turned"), 1)
            pe.transpose(banks(5)[:, 0:NM], mem_in[:, :], ident[0:NM, 0:NM]).then_inc(once("turned"), 1)
            pe.wait_ge(once("turned_sb"), 6)
            pe.matmul(banks(0)[:, 0:NM], aw[:, 0, :], memT[:, :], start=True, stop=True)
            pe.matmul(banks(0)[:, NM:2 * NM], aw[:, 1, :], memT[:, :], start=True, stop=True)
            pe.matmul(banks(0)[0:NM, P:P + D], memT[:, :], aw[:, 2, :], start=True, stop=True).then_inc(once("m_pe"), 1)
            pe.wait_ge(once("m_dve"), 3)
            for h in range(H):
                r = slice(DH * h, DH * h + DH)
                mm = pe.matmul(banks(2 + h)[0:NM, 0:NM], m_q[r, :], ke[r, 0, 0:NM], start=True, stop=True)
            mm.then_inc(once("m_pe"), 1)
            pe.wait_ge(once("m_act"), 1)
            for h in range(H):
                mm = pe.transpose(banks(6)[0:NM, h * NM:(h + 1) * NM], m_sc[0:NM, h, :], ident[0:NM, 0:NM])
            mm.then_inc(once("m_pe"), 1)
            pe.wait_ge(once("m_dve"), 7)
            for h in range(H):
                mm = pe.matmul(banks(7)[0:NM, h * 33:(h + 1) * 33], m_prT[0:NM, h, :], m_v[0:NM, h, :], start=True, stop=True)
            mm.then_inc(once("m_pe"), 1)
            pe.wait_ge(once("m_dve"), 9)
            pe.transpose(banks(0)[:, 0:NM], m_ao[0:NM, :], ident[0:NM, 0:NM]).then_inc(once("m_pe"), 1)
            pe.wait_ge(once("m_dve"), 10)
            pe.matmul(banks(1)[:, 0:NM], aw[:, 3, :], m_aoT, start=True, stop=True).then_inc(once("m_pe"), 1)
            for m in range(4):
                mm = pe.matmul(banks(2)[:, m * NM:(m + 1) * NM], w1T[:, m, :], memT[:, :], start=True, stop=True)
            mm.then_inc(once("m_pe"), 1)
            pe.matmul(banks(5)[0:NM], memT[:, :], w1T[:, :, :].rearrange("p m c -> p (m c)"), start=True, stop=True)\
                .then_inc(once("m_pe"), 1)
            pe.wait_ge(once("m_act"), 5)
            for m in range(4):
                mm = pe.matmul(banks(3)[:, 0:NM], w2T[:, m, :], m_aT[:, m, :], start=(m == 0), stop=(m == 3))
            mm.then_inc(once("m_pe"), 1)
            pe.wait_ge(once("m_dve"), 14)
            pe.transpose(banks(4)[0:NM, 0:P], m_eT, ident[:, :]).then_inc(once("m_pe"), 1)
            pe.matmul(banks(6)[0:NM], m_eT, w2[:, :], start=True, stop=True).then_inc(once("m_pe"), 1)
            pe.wait_ge(once("m_dve"), 15)
            pe.wait_ge(once("m_dve"), 18)
            pe.matmul(banks(7), m_e[0:NM, :], m_a[0:NM, :], start=True, stop=True)
            pe.matmul(banks(0), mem_in[:, :], m_t1[0:NM, :], start=True, stop=True).then_inc(once("m_pe"), 1)
            pe.wait_ge(once("m_done"), 1)
            with pe.Fori(0, PAIRS) as i:
                pe.wait_ge(s("x_in"), 16)
                for b in range(NB):
                    for t in range(4):
                        mm = pe.transpose(banks(b)[:, t * P:(t + 1) * P], x_tc[:, 4 * b + t, :], ident[:, :])
                    mm.then_inc(s("x_turned"), 1)

                def project(name, w, rhs, bank):
                    for b in range(NB):
                        pe.matmul(banks(bank + b), w, rhs(b), start=True, stop=True).then_inc(s(name), 1)

                pe.wait_ge(s("xT"), 2)
                of_x = lambda b: xT[:, b, :]
                project("v_proj", w_v[:, :], of_x, 6)
                project("k_proj", w_k[:, :], of_x, 4)
                project("q_proj", w_q[:, :], of_x, 2)
                project("b_proj", w_bx[:, :], of_x, 0)

                def fir31_taps(b, first, last):
                    for j in range(first, last):
                        mm = pe.matmul(banks(2 + b), fir_diag[:, j, :], v_pad[:, b, j:j + L], start=(j == 0), stop=(j == 30))
                    if last == 31:
                        mm.then_inc(s("fir31_psum"), 1)

                pe.wait_ge(s("q_raw"), 2)
                pe.wait_ge(s("v_act"), 1)
                fir31_taps(0, 0, 4)
                pe.wait_ge(s("k_sq"), 1)
                pe.wait_ge(s("k_raw"), 2)
                project("k_ss", headones[:, :], lambda b: sq[:, 1, b * L:(b + 1) * L], 4)
                fir31_taps(0, 4, 8)
                pe.wait_ge(s("q_sq"), 1)
                pe.wait_ge(s("beta_tanh"), 1)
                project("q_ss", headones[:, :], lambda b: sq[:, 0, b * L:(b + 1) * L], 0)
                fir31_taps(0, 8, 18)
                pe.wait_ge(s("kbq"), 2)
                pe.wait_ge(s("v_raw"), 2)
                for g in range(G):
                    at = banks((6, 7, 0, 1)[g // 8])[:, (g % 8) * 64:(g % 8) * 64 + 64]
                    for h in range(H):
                        r = slice(DH * h, DH * h + DH)
                        mm = pe.matmul(at[r].rearrange("p (a c) -> p a c", a=2), k_n[r, g * CH:(g + 1) * CH],
                                       kbq[r, :, g * CH:(g + 1) * CH], start=True, stop=True)
                    if g % 8 == 7:
                        mm.then_inc(s("r1"), 1)
                fir31_taps(0, 18, 31)
                fir31_taps(1, 0, 31)

                stat_order = (6, 0, 1, 4, 2, 3, 5)

                def stat(n, bank):
                    pe.wait_ge(s("streams"), n + 1)
                    for b in range(NB):
                        pe.matmul(banks(bank + b)[0:28], statsel[:, stat_order[n], :], ab[:, n % 2, b * L:(b + 1) * L],
                                  start=(n == 0), stop=(n == 6), skip_group_check=True).then_inc(s("stat"), 1)

                def small(name, g, at, lhs, rhs, inc=False, **kw):
                    for h in range(H):
                        r = slice(DH * h, DH * h + DH)
                        mm = pe.matmul(at[r], lhs[r], rhs[r], **kw)
                    if inc:
                        mm.then_inc(s(name), 1)

                pe.wait_ge(s("k_norm"), 1)
                pe.wait_ge(s("Dt"), 1)
                pe.wait_ge(s("kv"), 2)
                for g in range(G):
                    small("r2", g, banks(4 + g // 8)[:, (g % 8) * 64:(g % 8) * 64 + 64], Dt[:, g, :], kv[:, g, :],
                          inc=g % 8 == 7, start=True, stop=True)
                pe.wait_ge(s("fir31"), 1)
                pe.wait_ge(s("ka"), 3)
                for g in range(G):
                    if g % 16 == 0:
                        pe.wait_ge(s("wu"), g // 16 + 1)
                    small("r3", g, banks(g // 8)[:, (g % 8) * 64:(g % 8) * 64 + 64], wu[:, g, 0:32], ka[:, g, :],
                          inc=g % 8 == 7, start=True, stop=True)
                for g in range(G):
                    small("r4", g, banks(4 + g // 16)[:, (g % 16) * 32:(g % 16) * 32 + 32], ka[:, g, 0:32], wu[:, g, 32:64],
                          inc=g % 16 == 15, start=True, stop=True)

                def chunk_out(n):
                    for b in range(NB):
                        g = b * NC + n
                        at = banks(b)[:, n * CH:(n + 1) * CH]
                        for h in range(H):
                            r = slice(DH * h, DH * h + DH)
                            mm = pe.matmul(at[r], wu[r, g, 32:64], ka[r, g, 32:64], start=True, stop=(n == 0))
                            if n:
                                mm = pe.matmul(at[r], state[r, b, n, :], qwT[r, g * CH:(g + 1) * CH], start=False, stop=True)
                    return mm

                pe.wait_ge(s("pt"), 1)
                pe.wait_ge(s("qwT"), 1)
                for n in range(1, NC):
                    pe.wait_ge(s("state"), n)
                    if n < NC - 1:
                        for b in range(NB):
                            for h in range(H):
                                r = slice(DH * h, DH * h + DH)
                                mm = pe.matmul(banks(6)[r, b * DH:(b + 1) * DH], pt[r, b * NC + n, :], state[r, b, n, :],
                                               start=True, stop=True)
                        mm.then_inc(s("scan"), 1)
                    chunk_out(n - 1)
                chunk_out(NC - 1).then_inc(s("delta_psum"), 1)
                for n in range(S7):
                    stat(n, 4)
                for m in range(2):
                    for b in range(NB):
                        at = banks((6, 2)[m] + b)
                        pe.matmul(at, gw1a[:, m * P:(m + 1) * P], xT[:, b, :], start=True, stop=False)
                        if m == 0 and b == 0:
                            pe.wait_ge(s("stats"), 1)
                        pe.matmul(at, gw1b[:, m * P:(m + 1) * P], stats[:, b * L:(b + 1) * L], start=False,
                                  stop=True).then_inc(s("gate_h"), 1)
                pe.wait_ge(s("hmid"), 2)
                for b in range(NB):
                    for m in range(2):
                        mm = pe.matmul(banks(2 + b)[0:28], gw2[:, m, :], hmid[:, m, b * L:(b + 1) * L], start=(m == 0), stop=(m == 1))
                    mm.then_inc(s("logits"), 1)
                pe.wait_ge(s("halves"), 2)
                pe.wait_ge(s("delta"), 1)
                for b in range(NB):
                    pe.matmul(banks(b)[0:28], den_sel[0:60, :], halves[0:60, b * L:(b + 1) * L], start=True, stop=True).then_inc(s("den"), 1)
                pe.wait_ge(s("halves"), 4)
                for k in range(S7):
                    if k >= 2:
                        pe.wait_ge(s("prod"), k - 1)
                    for b in range(NB):
                        pe.matmul(banks(4 + 2 * (k % 2) + b), expand[0:60, k, :], halves[0:60, b * L:(b + 1) * L],
                                  start=True, stop=True).then_inc(s("expand"), 1)
                pe.wait_ge(s("o_sq"), 1)
                project("o_ms", headones[:, :], lambda b: ab[:, 1, b * L:(b + 1) * L], 2)
                pe.wait_ge(s("o_n"), 1)
                for t in range(NT):
                    mm = pe.matmul(banks(t // 4)[:, (t % 4) * D:(t % 4 + 1) * D], acc[:, t * P:(t + 1) * P], w_on[:, :],
                                   start=True, stop=True)
                    if t % 4 == 3:
                        mm.then_inc(s("attn_out"), 1)
                def turn(name, src, bank):
                    for b in range(NB):
                        for t in range(4):
                            mm = pe.transpose(banks(bank + b)[:, t * P:(t + 1) * P], src[:, 4 * b + t, :], ident[:, :])
                        mm.then_inc(s(name), 1)

                pe.wait_ge(s("x1"), NT)
                pe.wait_ge(s("prod"), 7)
                turn("x1_turned", x1, 4)
                pe.wait_ge(s("pooled_b"), 2)
                for b in range(NB):
                    mm = pe.matmul(banks(6)[:, b * E:(b + 1) * E], pooled_b[:, b, :], gwT[:, :], start=True, stop=True)
                mm.then_inc(s("gate8"), 1)
                pe.wait_ge(s("x1T"), 2)
                for m in range(4):
                    if m == 3:
                        pe.wait_ge(s("choice"), 2)
                    project("down", dnT[:, m, :], lambda b: x1T[:, b, :], (2, 0, 4, 6)[m])
                pe.wait_ge(s("hf"), 4)
                pe.wait_ge(s("ups"), 10)
                for t in range(NT):
                    at = banks(2 + t // 4)[:, (t % 4) * D:(t % 4 + 1) * D]
                    for m in range(4):
                        pe.matmul(at, hf[:, m, t * P:(t + 1) * P], ups[:, t // 4, m, :], start=(m == 0), stop=False)
                    mm = pe.matmul(at, c_rows[:, t // 4, :], upb[:, :], start=False, stop=True)
                    if t % 4 == 3:
                        mm.then_inc(s("x2_out"), 1)
                pe.wait_ge(s("x2"), NT)
                turn("x2_turned", x2, 0)
                pe.wait_ge(s("xe"), 2)
                project("q_proj2", aw[:, 0, :], lambda b: xe[:, b, NM:], 2)
                project("k_proj2", aw[:, 1, :], lambda b: xe[:, b, NM:], 4)
                for j in range(2 * NT):
                    b, k = j // 8, j % 8
                    mm = pe.matmul(banks((6, 7, 0, 1)[j // 4])[:, (j % 4) * D:(j % 4 + 1) * D],
                                   xe[:, b, NM * k:NM * k + P], aw[:, 2, :], start=True, stop=True)
                    if j % 4 == 3:
                        mm.then_inc(s("v_proj2"), 1)
                pe.wait_ge(s("qs"), 1)
                pe.wait_ge(s("ke"), 1)
                for b in range(NB):
                    if b == 1:
                        pe.wait_ge(s("ve"), 2)
                    for t in range(4):
                        for half in range(2):
                            for h in range(H):
                                r = slice(DH * h, DH * h + DH)
                                k0 = t * P + NM * half
                                mm = pe.matmul(banks(((2, 3, 4, 5), (6, 7, 0, 1))[b][h])[NM * half:NM * half + NM, t * P:(t + 1) * P],
                                               qs[r, b * L + k0:b * L + k0 + NM], ke[r, b, k0:k0 + P], start=True, stop=True)
                                if t == 3 and half == 1:
                                    mm.then_inc(s("scores"), 1)
                pe.wait_ge(s("ones_column"), 1)
                for b in range(NB):
                    pe.wait_ge(s("probs"), b + 1)
                    for n in range(16):
                        mm = pe.transpose(banks(((2, 3, 4, 5), (6, 7, 0, 1))[b][n // 4])[:, (n % 4) * P:(n % 4 + 1) * P],
                                          sc[b][:, n, :], ident[:, :])
                        if n % 4 == 3:
                            mm.then_inc(s("probs_turned"), 1)
                for b in range(NB):
                    pe.wait_ge(s("prT"), 2 * b + 2)
                    for t in range(4):
                        for half in range(2):
                            for h in range(H):
                                c = (t % 2) * 132 + h * 33
                                mm = pe.matmul(banks(2 + (4 * b + t) // 2)[NM * half:NM * half + NM, c:c + 33],
                                               prT[b][:, 4 * h + t, NM * half:NM * half + NM], ve[:, 8 * b + 2 * t + half, h, :],
                                               start=True, stop=True)
                    mm.then_inc(s("pv"), 1)
                pe.wait_ge(s("prT"), 4)
                pe.wait_ge(s("ao"), NT)
                turn("ao_turned", ao, 6)
                pe.wait_ge(s("aoT"), 1)
                project("wo", aw[:, 3, :], lambda b: aoT[:, b * L:(b + 1) * L], 0)
                for n in range(8):
                    b, m = n // 4, n % 4
                    if n >= 2:
                        pe.wait_ge(s("aT"), n - 1)
                    pe.matmul(banks(4 + n % 2), w1T[:, m, :], xe[:, b, NM:], start=True, stop=True).then_inc(s("zT"), 1)
                for b in range(NB):
                    pe.wait_ge(s("aT"), 4 * b + 4)
                    for m in range(4):
                        mm = pe.matmul(banks(2 + b), w2T[:, m, :], aT[:, m, b * L:(b + 1) * L], start=(m == 0), stop=(m == 3))
                    mm.then_inc(s("pred"), 1)

                def z_of(t):
                    b, c = t // 4, t % 4
                    o = t % 2
                    if t >= 2:
                        pe.wait_ge(s("zb"), t - 1)
                    pe.matmul(banks((6, 0)[o]), xe[:, b, NM + c * P:NM + (c + 1) * P], w1T[:, :, :].rearrange("p m c -> p (m c)"),
                              start=True, stop=True).then_inc(s("z"), 1)

                def da_of(t):
                    b, c = t // 4, t % 4
                    o = t % 2
                    if t >= 2:
                        pe.wait_ge(s("dz"), t - 1)
                    if t == 0:
                        pe.wait_ge(s("eT"), 1)
                        for bb in range(NB):
                            for cc in range(4):
                                mm = pe.transpose(banks(4 + bb)[:, cc * P:(cc + 1) * P], eT[:, bb, cc * P:(cc + 1) * P], ident[:, :])
                            mm.then_inc(s("e_turned"), 1)
                    pe.matmul(banks((7, 1)[o]), eT[:, b, c * P:(c + 1) * P], w2[:, :], start=True, stop=True).then_inc(s("da"), 1)

                pe.wait_ge(s("swaT"), 1)
                z_of(0)
                z_of(1)
                da_of(0)
                for t in range(NT):
                    if t + 2 < NT:
                        z_of(t + 2)
                    if t + 1 < NT:
                        da_of(t + 1)
                    o = t % 2
                    if t == 0:
                        pe.wait_ge(s("e_tc"), 1)
                    pe.wait_ge(s("a_th"), 2 * t + 2)
                    pe.matmul(banks(2), e_tc[:, t, :], a_tc[:, o, :], start=(t == 0), stop=(t == NT - 1))
                    pe.wait_ge(s("dz"), t + 1)
                    pe.matmul(banks(3), x2[:, t, :], dz[:, o, :], start=(t == 0), stop=(t == NT - 1)).then_inc(s("dw"), 1)
                pe.wait_ge(s("dw"), NT)
                pe.sem_inc(s("step_done"), 1)
                pe.wait_ge(step_go, i + 1)

            for m in range(4):
                mm = pe.matmul(banks(7)[:, m:m + 1], dzsum[:, m * P:(m + 1) * P], ones[:, 0:1], start=True, stop=True)
            mm.then_inc(s2("db1"), 1)
            pe.wait_ge(s2("e_loaded"), 16 * len(late_loads))
            for n in range(16):
                if n == 7:
                    pe.wait_ge(s2("stepped"), 4)
                if n >= 8:
                    pe.wait_ge(s2(("e_even", "e_odd")[n % 2]), (n - 8) // 2 + 1)
                for m in range(4):
                    src = w1n[:, n, m, :] if n < 8 else w2n[:, n - 8, m * P:(m + 1) * P]
                    mm = pe.transpose(banks(n % 8)[:, m * P:(m + 1) * P], src, ident[:, :])
                mm.then_inc(s2("e_turned"), 1)
            pe.wait_ge(s2("updated"), 1)
            pe.wait_ge(s2("e_even"), 5)
            for m in range(4):
                mm = pe.transpose(banks(0)[:, m * P:(m + 1) * P], w2[:, m * P:(m + 1) * P], ident[:, :])
            mm.then_inc(s2("w2_turned"), 1)
            pe.wait_ge(s2("e_odd"), 5)
            for m in range(2):
                mm = pe.transpose(banks(1)[:, m * P:(m + 1) * P], lin_in[:, m, :], ident[:, :])
            mm.then_inc(s2("w2_turned"), 1)
            pe.wait_ge(s2("w2_turned"), 2)
            pe.sem_inc(once("step2_done"), 1)
            pe.wait_ge(once("step2_go"), 1)

            def memory_z(n):
                b, m = n // 4, n % 4
                if n == 0:
                    pe.wait_ge(s2("in_x2T"), 16)
                if n >= 2:
                    pe.wait_ge(s2("aT"), n - 1)
                pe.matmul(banks(4 + n % 2), w1T[:, m, :], bx2T[:, b * L:(b + 1) * L], start=True, stop=True).then_inc(s2("zT"), 1)

            def memory_answer(n):
                b, m = n // 4, n % 4
                if n == 0:
                    pe.wait_ge(s2("aT"), 8)
                mm = pe.matmul(banks(4 + b), w2T[:, m, :], baT[:, m, b * L:(b + 1) * L], start=(m == 0), stop=(m == 3))
                if m == 3:
                    mm.then_inc(s2("om"), 1)

            def gate(n):
                if n == 0:
                    pe.wait_ge(s2("in_swaT"), 16)
                    pe.wait_ge(s2("omT"), 1)
                else:
                    pe.wait_ge(s2("tg"), 1)
                for b in range(NB):
                    pe.matmul(banks(4 + b), lT[:, n, :], (bswaT, omT)[n][:, b * L:(b + 1) * L], start=True, stop=True)\
                        .then_inc(s2(f"g{n + 1}"), 1)

            def turn2(name, src, t):
                mm = pe.transpose(banks(4 + t // 4)[:, (t % 4) * P:(t % 4 + 1) * P], src[:, t * P:(t + 1) * P], ident[:, :])
                if t % 4 == 3:
                    mm.then_inc(s2(name), 1)

            def turn_merged():
                pe.wait_ge(s2("tg"), 2)
                pe.wait_ge(s2("merged"), 1)
                for t in range(NT):
                    turn2("m_turned", mT, t)

            def turn_x3():
                pe.wait_ge(s2("x3"), NT)
                for t in range(NT):
                    turn2("x3_turned", x3, t)

            def route():
                pe.wait_ge(s2("x3T"), 1)
                for t in range(NT):
                    mm = pe.matmul(banks(4)[:, t * E:(t + 1) * E], x3T[:, t * P:(t + 1) * P], wrT[:, :], start=True, stop=True)
                mm.then_inc(s2("r_logits"), 1)

            def turn_weights():
                pe.wait_ge(s2("weights"), 1)
                for t in range(NT):
                    mm = pe.transpose(banks(4 + t // 4)[0:E, (t % 4) * P:(t % 4 + 1) * P], rw[:, 3, t, :], ident[:, :])
                mm.then_inc(s2("rw_turned"), 1)

            def hidden(e, m):
                n = 4 * e + m
                src = x3T if e < 2 else x3T_keep
                for b in range(NB):
                    if n >= 1:
                        pe.wait_ge(s2("hT"), 2 * (n - 1) + b + 1)
                    pe.matmul(banks(2 + b), w1eT[:, e, m, :], src[:, b * L:(b + 1) * L], start=True, stop=True).then_inc(s2("h"), 1)

            def experts(last):
                for m in range(4):
                    hidden(0, m)
                for t in range(NT):
                    mm = pe.matmul(banks(t // 4)[:, (t % 4) * D:(t % 4 + 1) * D], rwT[:, t * P:(t + 1) * P], b2e[:, :],
                                   start=True, stop=True)
                    if t % 4 == 3:
                        mm.then_inc(s2("y_bias"), 1)
                for e in range(E):
                    if e == 1:
                        pe.wait_ge(s2("x3T_keep"), 1)
                    for t in range(NT):
                        if e + 1 < E and t % 2 == 0:
                            hidden(e + 1, t // 2)
                        if t == 0:
                            pe.wait_ge(s2("hT"), 8 * e + 8)
                            if e == 1:
                                pe.wait_ge(s2("y"), 1)
                            if e >= 2:
                                pe.wait_ge(s2("y"), 1 + NT * (e - 1))
                        at = banks((6, 0)[e % 2] + t // 4)[:, (t % 4) * D:(t % 4 + 1) * D]
                        for m in range(4):
                            mm = pe.matmul(at, hT[e % 2][:, m, t * P:(t + 1) * P], w2eT[:, e, m, :], start=(m == 0), stop=(m == 3))
                        if t % 4 == 3:
                            mm.then_inc(s2("o"), 1)
                        if last:
                            continue
                        if e == 0:
                            memory_z(t)
                        if e == 1:
                            memory_answer(t)
                        if e == 2 and t == 5:
                            gate(0)
                        if e == 3 and t == 3:
                            gate(1)
                        if e == 4 and t == 5:
                            turn_merged()
                        if e == 5 and t == 6:
                            turn_x3()
                        if e == 6 and t == 5:
                            route()
                        if e == 7 and t == 7:
                            turn_weights()

            for n in range(8):
                memory_z(n)
            for n in range(8):
                memory_answer(n)
            gate(0)
            gate(1)
            turn_merged()
            turn_x3()
            route()
            turn_weights()
            pe.wait_ge(s2("rw_turned"), 1)
            pe.sem_inc(s2("step_done"), 1)
            pe.wait_ge(once("step2_go"), 2)
            experts(False)
            pe.wait_ge(s2("rw_turned"), 1)
            pe.sem_inc(s2("step_done"), 1)
            pe.wait_ge(once("step2_go"), 3)
            with pe.Fori(1, PAIRS - 1) as i:
                experts(False)
                pe.wait_ge(s2("rw_turned"), 1)
                pe.sem_inc(s2("step_done"), 1)
                pe.wait_ge(once("step2_go"), i + 3)
            experts(True)

        @block.sync
        def _(sp_):
            for dst, src in loads:
                sp_.dma_start(dst, src, allow_slow_non_contiguous=True).then_inc(loaded, 16)
            with sp_.Fori(0, PAIRS) as i:
                sp_.dma_start(x_tc[:, :, :].rearrange("p (b t) d -> p b t d", b=NB),
                              A["L0_attn_hidden_states"][bass.ds(i * NB, NB), :, :].rearrange("b (t p) d -> p b t d", p=P)
                              ).then_inc(s("x_in"), 16)
                sp_.wait_ge(s("x2"), NT)
                sp_.dma_start(x2_d[bass.ds(i, 1), :, :].rearrange("a p n -> p (a n)"), x2.rearrange("p t d -> p (t d)"))\
                    .then_inc(s("kept"), 16)
                sp_.wait_ge(s("xe"), 2)
                sp_.dma_start(x2T_d[bass.ds(i, 1), :, :].rearrange("a p (b t) -> p (a b) t", b=NB), xe[:, :, NM:])\
                    .then_inc(s("kept"), 16)
                sp_.wait_ge(s("swaT"), 1)
                sp_.dma_start(swaT_d[bass.ds(i, 1), :, :].rearrange("a p n -> p (a n)"), swaT).then_inc(s("kept"), 16)
                sp_.wait_ge(s("step_done"), 4)
                sp_.wait_ge(s("kept"), 48)
                sp_.sem_clear(range(min(z.num for z in sems.values()), max(z.num for z in sems.values()) + 1))
                sp_.sem_inc(step_go, 1)
            for dst, src in late_loads:
                sp_.dma_start(dst, src, allow_slow_non_contiguous=True).then_inc(s2("e_loaded"), 16)
            sp_.wait_ge(once("step2_done"), 3)
            for z in (s2(n) for n in ("lr", "db1", "stepped", "updated", "e_turned", "e_even", "e_odd", "w2_turned", "ready2", "e_loaded")):
                sp_.sem_clear(z)
            sp_.sem_inc(once("step2_go"), 1)

            def take(k):
                for name, dst, src in (("in_x2T", bx2T, x2T_d), ("in_swaT", bswaT, swaT_d), ("in_x2", bx2, x2_d)):
                    sp_.dma_start(dst, src[bass.ds(k, 1), :, :].rearrange("a p n -> p (a n)")).then_inc(s2(name), 16)

            def store(k, x4):
                sp_.wait_ge(s2(x4), NT)
                sp_.dma_start(out[bass.ds(k * NB, NB), :, :].rearrange("b (t p) d -> p b t d", p=P),
                              x3_keep.rearrange("p (b t d) -> p b t d", b=NB, d=D)).then_inc(s2("stored"), 16)

            def next_step():
                sp_.wait_ge(s2("step_done"), 3)
                sp_.sem_clear(range(min(z.num for z in sems.values()), max(z.num for z in sems.values()) + 1))
                sp_.sem_inc(once("step2_go"), 1)

            take(0)
            next_step()
            take(1)
            next_step()
            with sp_.Fori(1, PAIRS - 1) as i:
                take(i + 1)
                store(i - 1, "x4")
                sp_.wait_ge(s2("stored"), 16)
                next_step()
            store(PAIRS - 2, "x4")
            store(PAIRS - 1, "last_x4")
            sp_.wait_ge(s2("stored"), 32)


_INS = [
    "L0_attn_hidden_states", "L0_attn_w_q", "L0_attn_w_k", "L0_attn_w_v", "L0_attn_w_b", "L0_attn_conv_q_w",
    "L0_attn_conv_k_w", "L0_attn_conv_v_w", "L0_attn_fir1", "L0_attn_fir3", "L0_attn_fir7", "L0_attn_fir15",
    "L0_attn_fir31", "L0_attn_gate_w1", "L0_attn_gate_b1", "L0_attn_gate_w2", "L0_attn_gate_b2",
    "L0_attn_norm_w", "L0_attn_w_o", "L0_ffn_gate_w", "L0_ffn_down_w", "L0_ffn_down_b", "L0_ffn_up_w",
    "L0_ffn_up_b", "L1_attn_mem", "L1_attn_wq", "L1_attn_wk", "L1_attn_wv", "L1_attn_wo", "L1_attn_w1",
    "L1_attn_b1", "L1_attn_w2", "L1_attn_b2", "L1_attn_lin1", "L1_attn_lin2", "L1_attn_alpha",
    "L1_attn_theta", "L1_ffn_Wr", "L1_ffn_br", "L1_ffn_W1", "L1_ffn_b1", "L1_ffn_W2", "L1_ffn_b2",
    "L1_ffn_gamma", "L1_ffn_beta",
]
_OUTS = [((B, L, D), "float32")]


def kernel(**inputs):
    import numpy as _np
    import concourse.bacc as _bacc
    from concourse import mybir as _mybir
    from concourse.bass_utils import run_bass_kernel_spmd as _run

    nc = _bacc.Bacc("TRN2", target_bir_lowering=False, num_devices=1)
    arrays, args = {}, {}
    for name in _INS:
        a = _np.ascontiguousarray(inputs[name])
        if a.ndim == 0:
            a = a.reshape(1)
        arrays[f"in_{name}_dram"] = a
        args[name] = nc.dram_tensor(f"in_{name}_dram", a.shape, _mybir.dt.from_np(a.dtype), kind="ExternalInput").ap()
    outs = []
    for i, (shape, dtype) in enumerate(_OUTS):
        dt = _mybir.dt.from_np(_np.dtype(dtype))
        outs.append(nc.dram_tensor(f"out_{i}_dram", shape, dt, kind="ExternalOutput").ap())
    program(nc, args, outs[0])
    r = _run(nc, [arrays], core_ids=[0])
    got = tuple(r.results[0][f"out_{i}_dram"] for i in range(len(_OUTS)))
    return got[0]
```

```python
from contextlib import ExitStack

import numpy as np
import concourse.bass as bass
import concourse.mybir as mybir

F32 = mybir.dt.float32
F32R = mybir.dt.float32r
ACT = mybir.ActivationFunctionType
ALU = mybir.AluOpType
AX = mybir.AxisListType

P = 128
D = 128
B, L = 8, 512
H, DH = 4, 32
CH = 32
NB = 2
PAIRS = B // NB
T = NB * L
NT = T // P
NC = L // CH
G = NB * NC
S7 = 7
FIRS = (1, 3, 7, 15, 31)
FOFF = (0, 1, 4, 11, 26)
PADC, PADF = 3, 30
DVE_TAPS = 7
BANK = 512
E = 8
LATE_WORDS = 2304
NM = 64
FH = 512
NEG = -1e30


def program(nc, A, out):
    ctx = ExitStack()
    with ctx:
        at_byte = {}

        def sb(name, shape, dt=F32):
            at_byte[name] = -(-nc.sbuf_base // 32) * 32
            return ctx.enter_context(nc.sbuf_tensor(name, shape, dt))

        def over(name, host, words, *shape):
            return nc.alloc_sbuf_tensor_at(name, [P, *shape], F32R, offset=at_byte[host] + 4 * words)

        PS = ctx.enter_context(nc.psum_tensor("PS", [P, 8 * BANK], F32))

        def banks(first, n=1):
            return PS[:, first * BANK:(first + n) * BANK]

        arena = {"front": sb("front", [P, 9 * T]), "middle": sb("middle", [P, 23 * T + 256])}
        used = {"front": 0, "middle": 0}

        def part(where, name, *shape):
            size = int(np.prod(shape))
            at = used[where]
            used[where] = at + size
            assert at + size <= arena[where].shape[1], (name, at + size)
            v = arena[where][:, at:at + size]
            if len(shape) == 2:
                v = v.rearrange("p (a b) -> p a b", a=shape[0])
            if len(shape) == 3:
                v = v.rearrange("p (a b c) -> p a b c", a=shape[0], b=shape[1])
            return v

        def part_in(name, *shape):
            return part("middle", name, *shape)

        ident = sb("ident", [P, P])
        ones = sb("ones", [P, P])
        headones = sb("headones", [P, P])
        statsel = sb("statsel", [P, S7, 28])
        expand = sb("expand", [64, S7, P], F32R)
        keep_j_le_i = sb("keep_j_le_i", [P, CH])
        low_free = sb("low_free", [P, CH, CH])
        eye_quad = sb("eye_quad", [P, DH])
        eps6 = sb("eps6", [P, 1])
        eps5 = sb("eps5", [P, 1])
        one1 = sb("one1", [P, 1])
        w_q, w_k, w_v = sb("w_q", [D, D]), sb("w_k", [D, D]), sb("w_v", [D, D])
        w_b = sb("w_b", [D, H])
        w_bx = sb("w_bx", [D, D])
        conv_w = sb("conv_w", [P, 3, 4])
        fir_w = sb("fir_w", [P, 57])
        fir_diag = sb("fir_diag", [P, 31, P])
        gw1a = sb("gw1a", [D, 256])
        gw1b = sb("gw1b", [28, 256])
        gb1 = sb("gb1", [P, 2])
        gw2 = sb("gw2", [P, 2, 28])
        gb2 = sb("gb2", [P, 28])
        norm_col = sb("norm_col", [P, 1])
        w_o = sb("w_o", [P, D])
        w_on = sb("w_on", [P, D])

        gwT = sb("gwT", [D, E])
        dn_in = part_in("dn_in", 4, P)
        up_in = part_in("up_in", E, 64)
        w1_in = part_in("w1_in", 4, D)
        sq_in = part_in("sq_in", 4, D)
        mem_in = sb("mem_in", [NM, D])
        m_q = part("middle", "m_q", NM)
        m_v = part("middle", "m_v", H, DH + 1)
        m_sc = part("middle", "m_sc", H, NM)
        m_st = part("middle", "m_st", 2, H)
        m_prT = part("middle", "m_prT", H, NM)
        m_ao = part("middle", "m_ao", D)
        m_aoT = part("middle", "m_aoT", NM)
        m_swaT = part("middle", "m_swaT", NM)
        m_aT = part("middle", "m_aT", 4, NM)
        m_eT = part("middle", "m_eT", NM)
        m_e = part("middle", "m_e", D)
        m_zb, m_a, m_th, m_t1 = (part("middle", n, FH) for n in ("m_zb", "m_a", "m_th", "m_t1"))
        zero_in, expand_in = part("middle", "zero_in", T)[0:64], part("middle", "expand_in", S7, P)[0:64]
        dnT = sb("dnT", [P, 4, P])
        upT = sb("upT", [P, 4, D])
        dnb = sb("dnb", [P, 4])
        upb = sb("upb", [E, D])
        w1T = sb("w1T", [P, 4, P])
        w2 = sb("w2", [P, FH])
        w2T = sb("w2T", [P, 4, D])
        aw = sb("aw", [P, 4, D])
        memT = sb("memT", [P, NM])
        b1c = sb("b1c", [P, 4])
        b1r = sb("b1r", [P, FH])
        b2c = sb("b2c", [P, 1])
        eight_low = sb("eight_low", [P, E, E])
        pick = sb("pick", [P, 4, E])
        wmask = sb("wmask", [P, P])
        gW1, gW2, dzsum = sb("gW1", [P, FH]), sb("gW2", [P, FH]), sb("dzsum", [P, FH])
        gb2s = sb("gb2s", [P, 1])
        esum = sb("esum", [P, 1])

        arena["late"] = fir_diag[:, :, :].rearrange("p k c -> p (k c)")
        used["late"] = 0
        lin_in = part("late", "lin_in", 2, D)
        lT = part("late", "lT", 2, D)
        keep_lr = sb("keep_lr", [P, 2])
        wrT = part("late", "wrT", E)
        brr = part("late", "brr", E)
        b1e = part("late", "b1e", E, 4)
        b2e = part("late", "b2e", D)[0:E]
        gamma_r, beta_r = part("late", "gamma_r", D), part("late", "beta_r", D)

        turn_bank = lambda n: (0, 1, 2, 3, 6, 7)[n % 6]

        used["middle"] = 0
        x_tc = sb("x_tc", [P, NT, D])
        xe = sb("xe", [P, NB, NM + L])
        xT = xe[:, :, NM:]
        v_pad = sb("v_pad", [P, NB, PADF + L])
        conv = part("front", "conv", 3, NB, L)
        sq = part("front", "sq", 2, T)
        nrm = sq
        beta = part("front", "beta", T)
        ab = part("front", "ab", 2, T)
        acc = part("front", "acc", T)
        used["front"] = 0
        hmid = part("front", "hmid", 2, T)
        gl = part("front", "gl", 4, NT, 28)
        gden = part("front", "gden", 2, NT * H)
        halves = sb("halves", [64, T], F32R)
        stats = part("front", "stats", T)[0:28]

        kbq = part("middle", "kbq", 2, T)
        k_n = part("middle", "k_n", T)
        vb = part("middle", "vb", T)
        Dm = part("middle", "Dm", CH, CH)
        Dt = part("middle", "Dt", G, CH)
        tmp = part("middle", "tmp", 256)
        ka = part("middle", "ka", G, 64)
        kv = part("middle", "kv", G, 64)
        before = used["middle"]
        q_raw, k_raw, v_raw = (part("middle", n, NB, PADC + L) for n in ("q_raw", "k_raw", "v_raw"))
        used["middle"] = before
        wu = part("middle", "wu", G, 64)
        pt = part("middle", "pt", G, DH)
        gk = part("middle", "gk", NB, NC, DH)
        qwT = part("middle", "qwT", T)
        fir = part("middle", "fir", 5, T)
        delta = part("middle", "delta", T)
        state = part("middle", "state", NB, NC, DH)
        used["middle"] = 0
        x1T = part("middle", "x1T", NB, L)
        hf = part("middle", "hf", 4, T)
        ups = part("middle", "ups", NB, 4, D)
        x1 = part("middle", "x1", NT, D)
        x2 = part("middle", "x2", NT, D)
        qs = part("middle", "qs", T)
        ve = part("middle", "ve", 2 * NT, H, DH + 1)
        sc = [part("middle", f"sc{b}", H * 4, P) for b in range(NB)]
        prT = [part("middle", f"prT{b}", H * 4, P) for b in range(NB)]
        ao = part("middle", "ao", NT, D)
        aoT = part("middle", "aoT", T)
        swaT = part("middle", "swaT", T)
        pooled_b = part("middle", "pooled_b", NB, P)
        c_rows = part("middle", "c_rows", NB, P)[0:E]
        pair8, eq8 = (part("middle", n, NB * E, E).rearrange("p (b e) f -> p b e f", b=NB) for n in ("pair8", "eq8"))
        used["middle"], used["front"] = 0, 0
        eT = part("middle", "eT", NB, L)
        e_tc = part("middle", "e_tc", NT, D)
        aT = part("front", "aT", 4, T)
        zb, a_tc, th, t1, dz = (part("front", n, 2, FH) for n in ("zb", "a_tc", "th", "t1", "dz"))
        ke = sb("ke", [P, NB, NM + L])
        bn6 = sb("bn6", [P, NT, 6])
        bn2 = sb("bn2", [P, NT, 2])
        rstd = sb("rstd", [P, NT])
        used["middle"], used["front"] = 0, 0
        used["middle"] += 4 * T
        w1_high = over("w1_high", "middle", 0, E, 4, P)
        places = ([("ke", 0), ("ke", 4 * P), ("xe", 0), ("xe", 4 * P)] + [("fir_diag", LATE_WORDS + 4 * P * n) for n in range(3)]
                  + [("dzsum", 0)])
        w1_low = [over(f"w1_low{e}", host, words, 4, P) for e, (host, words) in enumerate(places)]
        x3_high, x3_low = over("x3_high", "x_tc", 0, T), over("x3_low", "v_pad", 0, T)
        w2eT = part("middle", "w2eT", E, 4, D)
        before = used["middle"]
        hT = [part("middle", f"hT{o}", 4, T) for o in range(2)]
        used["middle"] = before
        w1n = part("middle", "w1n", E, 4, D)
        w2n = part("middle", "w2n", E, FH)
        bx2T, bswaT, bx2, omT, mT, x3, x3T = (part("middle", n, T) for n in ("bx2T", "bswaT", "bx2", "omT", "mT", "x3", "x3T"))
        baT = part("front", "baT", 4, T)
        tg = part("front", "tg", 2, T)
        tok_pair, tok_equal = (tg[:, n, 0:NT * E * E].rearrange("p (t e f) -> p t e f", e=E, f=E) for n in range(2))
        y = part("front", "y", T)
        x3_keep = part("front", "x3_keep", T)
        rwT = part("front", "rwT", T)[0:E]
        rw = part("late", "rw", 5, NT, E)
        rw_keep = part("late", "rw_keep", NT, E)
        assert used["late"] <= LATE_WORDS
        pooled = sb("pooled", [P, NB])
        rt = sb("rt", [P, 8, 2 * E])
        cvec = sb("cvec", [P, NB, 4])
        cdiag = sb("cdiag", [E, NB, E])
        cd = sb("cd", [E, NB])
        mx = sb("mx", [P, NB, H * 4])
        ri = sb("ri", [P, NT, H])

        sems = {}

        def s(name):
            if name not in sems:
                sems[name] = ctx.enter_context(nc.semaphore(name))
            return sems[name]

        second = {}

        def s2(name):
            if name not in second:
                second[name] = list(sems.values())[len(second)]
            return second[name]

        single = {}

        def once(name):
            if name not in single:
                single[name] = ctx.enter_context(nc.semaphore(name))
            return single[name]

        loaded, masks, prepared, step_go, x_in = (
            once(n) for n in ("loaded", "masks", "prepared", "step_go", "x_in"))
        for n in ("turned", "turned_sb", "m_pe", "m_dve", "m_act", "m_done", "first_in", "step2_go", "filled", "diagonals", "e_loaded"):
            once(n)
        loads = [
            (w_q[:, :], A["L0_attn_w_q"]), (w_k[:, :], A["L0_attn_w_k"]), (w_v[:, :], A["L0_attn_w_v"]),
            (w_b[:, :], A["L0_attn_w_b"]), (conv_w[:, 0, :], A["L0_attn_conv_q_w"]),
            (conv_w[:, 1, :], A["L0_attn_conv_k_w"]), (conv_w[:, 2, :], A["L0_attn_conv_v_w"]),
            (gw1a[:, :], A["L0_attn_gate_w1"][0:D, :]), (gw1b[:, :], A["L0_attn_gate_w1"][D:D + 28, :]),
            (gb1[:, :], A["L0_attn_gate_b1"].rearrange("(m p) -> p m", p=P)),
            (gw2[:, :, :], A["L0_attn_gate_w2"].rearrange("(m p) c -> p m c", p=P)),
            (gb2[:, :], A["L0_attn_gate_b2"].partition_broadcast(P)),
            (w_o[:, :], A["L0_attn_w_o"]),
        ]
        loads += [(fir_w[:, FOFF[n]:FOFF[n] + k], A[f"L0_attn_fir{k}"]) for n, k in enumerate(FIRS)]
        loads += [(norm_col[DH * h:DH * h + DH, :], A["L0_attn_norm_w"].rearrange("(p a) -> p a", a=1)) for h in range(H)]
        loads += [
            (gwT[:, :], A["L0_ffn_gate_w"].rearrange("e d -> d e")),
            (dn_in, A["L0_ffn_down_w"].rearrange("e c d -> (e c) d").rearrange("(m p) d -> p m d", p=P)),
            (up_in, A["L0_ffn_up_w"].rearrange("e d c -> d e c")),
            (dnb[:, :], A["L0_ffn_down_b"].rearrange("(m a) c -> (a c) m", a=2)),
            (upb[:, :], A["L0_ffn_up_b"]),
            (w1_in, A["L1_attn_w1"].rearrange("(m p) d -> p m d", p=P)),
            (w2[:, :], A["L1_attn_w2"]),
            (mem_in[:, :], A["L1_attn_mem"]),
            (b1c[:, :], A["L1_attn_b1"].rearrange("(m p) -> p m", p=P)),
            (b2c[:, :], A["L1_attn_b2"].rearrange("(p a) -> p a", a=1)),
            (b1r[:, :], A["L1_attn_b1"].partition_broadcast(P)),
        ]
        small_late_loads = [
            (lin_in[:, 0, :], A["L1_attn_lin1"]), (lin_in[:, 1, :], A["L1_attn_lin2"]),
            (wrT, A["L1_ffn_Wr"].rearrange("e d -> d e")),
            (brr, A["L1_ffn_br"].partition_broadcast(P)),
            (b1e, A["L1_ffn_b1"].rearrange("e (m p) -> p e m", p=P)),
            (b2e, A["L1_ffn_b2"]),
            (gamma_r, A["L1_ffn_gamma"].partition_broadcast(P)),
            (beta_r, A["L1_ffn_beta"].partition_broadcast(P)),
        ]
        expert_loads = [
            (w1n, A["L1_ffn_W1"].rearrange("e (m p) d -> p e m d", p=P)),
            (w2n, A["L1_ffn_W2"].rearrange("e d f -> d e f")),
        ]
        loads += [
            (keep_lr[:, 0:1], A["L1_attn_alpha"].partition_broadcast(P)),
            (keep_lr[:, 1:2], A["L1_attn_theta"].partition_broadcast(P)),
        ]
        loads += [(sq_in[:, n, :], A[f"L1_attn_w{c}"]) for n, c in enumerate("qkvo")]
        x2T_d = nc.dram_tensor("x2T_d", [PAIRS, P, T], F32).ap()
        swaT_d = nc.dram_tensor("swaT_d", [PAIRS, P, T], F32).ap()
        x2_d = nc.dram_tensor("x2_d", [PAIRS, P, T], F32).ap()
        block = ctx.enter_context(nc.Block())

        @block.gpsimd
        def _(pool):
            n = 0

            def fill(t, v):
                nonlocal n
                if n:
                    pool.wait_ge(masks, n)
                pool.memset(t, v).then_inc(masks, 1)
                n += 1

            def keep(t, op, pattern, base, mult, value):
                nonlocal n
                pool.wait_ge(masks, n)
                pool.affine_select(out=t, in_=t, compare_op=op, fill=value, base=base, pattern=pattern,
                                   channel_multiplier=mult).then_inc(masks, 1)
                n += 1

            fill(ident[:, :], 0.0)
            keep(ident[:, :], ALU.not_equal, [[-1, P]], 0, 1, 1.0)
            pool.wait_ge(masks, n)
            pool.sem_inc(prepared, 1)
            fill(ones[:, :], 1.0)
            fill(headones[:, :], 1.0)
            by_head = headones[:, :].rearrange("p (h d) -> p h d", h=H)
            keep(by_head, ALU.is_ge, [[-DH, H], [0, DH]], 0, 1, 0.0)
            keep(by_head, ALU.is_ge, [[DH, H], [0, DH]], DH - 1, -1, 0.0)
            fill(statsel[:, :, :], 0.0)
            for k in range(S7):
                pool.wait_ge(masks, n)
                for h in range(H):
                    fill(statsel[DH * h:DH * h + DH, k, 4 * k + h:4 * k + h + 1], 1 / DH)
            fill(zero_in, 0.0)
            fill(expand_in, 0.0)
            for r in (slice(0, 28), slice(32, 60)):
                keep(expand_in[r, :, :].rearrange("p k (h d) -> p k h d", h=H), ALU.not_equal,
                     [[-1, S7], [-S7, H], [0, DH]], 0, 1, 1.0)
            for h in range(H):
                fill(keep_j_le_i[DH * h:DH * h + DH, :], 1.0)
                keep(keep_j_le_i[DH * h:DH * h + DH, :], ALU.is_ge, [[1, CH]], 0, -1, 0.0)
                fill(eye_quad[DH * h:DH * h + DH, :], 0.0)
                keep(eye_quad[DH * h:DH * h + DH, :], ALU.not_equal, [[-1, CH]], 0, 1, 1.0)
            fill(low_free[:, :, :], -1.0)
            keep(low_free[:, :, :], ALU.is_gt, [[1, CH], [-1, CH]], 0, 0, 0.0)
            fill(eps6[:, :], 1e-6)
            fill(eps5[:, :], 1e-5)
            fill(one1[:, :], 1.0)
            fill(eight_low[:, :, :], 1.0)
            keep(eight_low[:, :, :], ALU.is_gt, [[1, E], [-1, E]], 0, 0, 0.0)
            for half in range(2):
                v = pick[64 * half:64 * half + 64, :, :]
                fill(v, 0.0)
                keep(v, ALU.not_equal, [[-2, 4], [1, E]], -half, 0, 1.0)
                v = wmask[64 * half:64 * half + 64, :]
                fill(v, 0.0)
                keep(v, ALU.is_gt, [[1, P]], 0, -1, NEG)
                keep(v, ALU.is_ge, [[-1, P]], NM, 1, NEG)
            fill(v_pad[:, :, 0:PADF], 0.0)
            pool.wait_ge(masks, n)
            pool.sem_inc(once("filled"), 1)
            pool.wait_ge(once("m_done"), 1)
            with pool.Fori(0, PAIRS) as i:
                for t in (q_raw, k_raw, v_raw):
                    pool.memset(t[:, :, 0:PADC], 0.0).then_inc(s("pads"), 1)
                for n, k in enumerate((3, 5)):
                    pool.wait_ge(s("prod"), k + 1)
                    if n:
                        pool.wait_ge(s("pool_sum"), n)
                    pool.tensor_tensor(hmid[:, 0, :], hmid[:, 0, :], hmid[:, 1, :], ALU.add).then_inc(s("pool_sum"), 1)
                pool.wait_ge(s("x1"), NT)
                pool.memset(ve[:, :, :, DH:DH + 1], 1.0).then_inc(s("ones_column"), 1)
                for t in range(NT):
                    pool.wait_ge(s("dz"), t + 1)
                    if t:
                        pool.wait_ge(s("dzsum"), t)
                    pool.tensor_tensor(dzsum[:, :], dzsum[:, :], dz[:, t % 2, :], ALU.add).then_inc(s("dzsum"), 1)
                pool.wait_ge(s("dzsum"), NT)
                pool.sem_inc(s("step_done"), 1)
                pool.wait_ge(step_go, i + 1)

        @block.vector
        def _(dve):
            dve.wait_ge(loaded, 16 * len(loads))
            dve.tensor_copy(w_bx[:, :].rearrange("p (h d) -> p h d", h=H),
                            w_b[:, :].unsqueeze(2).broadcast_to([P, H, DH])).then_inc(prepared, 1)
            dve.tensor_scalar(w_on[:, :], w_o[:, :], norm_col[:, 0:1], None, ALU.mult).then_inc(prepared, 1)
            dve.wait_ge(prepared, 3)
            for n, dst in enumerate((dnT, upT, w1T, w2T, aw)):
                dve.wait_ge(once("turned"), n + 1)
                dve.tensor_copy(dst[:, :, :], banks(n).rearrange("p (m c) -> p m c", c=P)).then_inc(once("turned_sb"), 1)
            dve.wait_ge(once("turned"), 6)
            dve.tensor_copy(memT[:, :], banks(5)[:, 0:NM]).then_inc(once("turned_sb"), 1)
            dve.tensor_copy(xe[:, :, 0:NM], banks(5)[:, 0:NM].unsqueeze(1).broadcast_to([P, NB, NM]))
            dve.memset(dzsum[NM:P, :], 0.0)
            dve.wait_ge(once("m_pe"), 1)
            dve.tensor_copy(m_q, banks(0)[:, 0:NM]).then_inc(once("m_dve"), 1)
            dve.tensor_copy(ke[:, :, 0:NM], banks(0)[:, NM:2 * NM].unsqueeze(1).broadcast_to([P, NB, NM])).then_inc(once("m_dve"), 1)
            dve.memset(m_v[0:NM, :, DH:DH + 1], 1.0)
            dve.tensor_copy(m_v[0:NM, :, 0:DH], banks(0)[0:NM, P:P + D].rearrange("p (h d) -> p h d", h=H)).then_inc(once("m_dve"), 1)
            for j in range(DVE_TAPS, 31):
                dve.tensor_scalar(fir_diag[:, j, :], ident[:, :], fir_w[:, FOFF[4] + j:FOFF[4] + j + 1], None,
                                  ALU.mult).then_inc(once("diagonals"), 1)
            dve.wait_ge(once("filled"), 1)
            for dst, src in ((halves[:, :], zero_in), (expand[:, :, :], expand_in)):
                dve.tensor_copy(dst, src).then_inc(once("diagonals"), 1)
            dve.wait_ge(once("m_pe"), 2)
            dve.tensor_tensor(m_sc[0:NM, :, :], banks(2, 4)[0:NM].rearrange("p (h k) -> p h k", h=H)[:, :, 0:NM],
                              wmask[0:NM, NM:].unsqueeze(1).broadcast_to([NM, H, NM]), ALU.add).then_inc(once("m_dve"), 1)
            dve.wait_ge(once("m_dve"), 4)
            dve.tensor_reduce(m_st[0:NM, 0, :], m_sc[0:NM, :, :], AX.X, ALU.max).then_inc(once("m_dve"), 1)
            dve.wait_ge(once("m_dve"), 5)
            dve.tensor_tensor(m_sc[0:NM, :, :], m_sc[0:NM, :, :], m_st[0:NM, 0, :].unsqueeze(2).broadcast_to([NM, H, NM]),
                              ALU.subtract).then_inc(once("m_dve"), 1)
            dve.wait_ge(once("m_pe"), 3)
            dve.tensor_copy(m_prT[0:NM, :, :], banks(6)[0:NM, 0:H * NM].rearrange("p (h q) -> p h q", h=H)).then_inc(once("m_dve"), 1)
            dve.wait_ge(once("m_pe"), 4)
            pv = banks(7)[0:NM, 0:H * 33].rearrange("p (h e) -> p h e", h=H)
            dve.reciprocal(m_st[0:NM, 1, :].unsqueeze(2), pv[:, :, DH:DH + 1]).then_inc(once("m_dve"), 1)
            dve.wait_ge(once("m_dve"), 8)
            dve.tensor_tensor(m_ao[0:NM, :].rearrange("p (h e) -> p h e", h=H), pv[:, :, 0:DH],
                              m_st[0:NM, 1, :].unsqueeze(2).broadcast_to([NM, H, DH]), ALU.mult).then_inc(once("m_dve"), 1)
            dve.wait_ge(once("m_pe"), 5)
            dve.tensor_copy(m_aoT, banks(0)[:, 0:NM]).then_inc(once("m_dve"), 1)
            dve.wait_ge(once("m_pe"), 6)
            dve.tensor_copy(m_swaT, banks(1)[:, 0:NM]).then_inc(once("m_dve"), 1)
            dve.wait_ge(once("m_pe"), 8)
            dve.tensor_tensor(m_zb[0:NM, :], banks(5)[0:NM], b1r[0:NM, :], ALU.add).then_inc(once("m_dve"), 1)
            dve.wait_ge(once("m_pe"), 9)
            dve.wait_ge(once("m_dve"), 11)
            dve.scalar_tensor_tensor(out=m_eT, in0=banks(3)[:, 0:NM], scalar=b2c[:, 0:1], in1=m_swaT, op0=ALU.add,
                                     op1=ALU.subtract).then_inc(once("m_dve"), 1)
            dve.wait_ge(once("m_dve"), 13)
            dve.tensor_scalar(m_eT, m_eT, float(B), None, ALU.mult).then_inc(once("m_dve"), 1)
            dve.wait_ge(once("m_dve"), 14)
            dve.tensor_reduce(gb2s[:, :], m_eT, AX.X, ALU.add)
            dve.wait_ge(once("m_pe"), 10)
            dve.tensor_copy(m_e[0:NM, :], banks(4)[0:NM, 0:P]).then_inc(once("m_dve"), 1)
            dve.wait_ge(once("m_act"), 7)
            dve.scalar_tensor_tensor(out=m_t1[0:NM, :], in0=m_zb[0:NM, :], scalar=1.0, in1=m_a[0:NM, :], op0=ALU.add,
                                     op1=ALU.subtract).then_inc(once("m_dve"), 1)
            dve.wait_ge(once("m_dve"), 16)
            dve.scalar_tensor_tensor(out=m_t1[0:NM, :], in0=m_th[0:NM, :], scalar=1.0, in1=m_t1[0:NM, :], op0=ALU.add,
                                     op1=ALU.mult).then_inc(once("m_dve"), 1)
            dve.wait_ge(once("m_dve"), 17)
            dve.wait_ge(once("m_pe"), 11)
            dve.scalar_tensor_tensor(out=m_t1[0:NM, :], in0=m_t1[0:NM, :], scalar=0.5, in1=banks(6)[0:NM], op0=ALU.mult,
                                     op1=ALU.mult).then_inc(once("m_dve"), 1)
            dve.wait_ge(once("m_dve"), 18)
            dve.tensor_copy(dzsum[0:NM, :], m_t1[0:NM, :])
            dve.wait_ge(once("m_pe"), 12)
            dve.tensor_copy(gW2[:, :], banks(7))
            dve.tensor_copy(gW1[:, :], banks(0)).then_inc(once("m_done"), 1)
            dve.wait_ge(once("m_done"), 1)
            dve.wait_ge(once("diagonals"), 33 - DVE_TAPS)
            dve.wait_ge(x_in, 16)
            with dve.Fori(0, PAIRS) as i:
                def convolve(name, src, dst):
                    dve.wait_ge(s(name + "_raw"), 2)
                    c = {"q": 0, "k": 1, "v": 2}[name]
                    for j in range(4):
                        sh, w = src[:, :, j:j + L], conv_w[:, c, j:j + 1]
                        if j == 0:
                            ins = dve.tensor_scalar(dst, sh, w, None, ALU.mult)
                        else:
                            dve.wait_ge(s(name + "_conv"), j)
                            ins = dve.scalar_tensor_tensor(out=dst, in0=sh, scalar=w, in1=dst, op0=ALU.mult, op1=ALU.add)
                        ins.then_inc(s(name + "_conv"), 1)

                def fir_tap(n, j):
                    k = FIRS[n]
                    dst = fir[:, n, :].rearrange("p (b t) -> p b t", b=NB)
                    sh = v_pad[:, :, PADF - k + 1 + j:PADF - k + 1 + j + L]
                    w = fir_w[:, FOFF[n] + j:FOFF[n] + j + 1]
                    if j == 0:
                        dve.wait_ge(s("v_act"), 1)
                        ins = dve.tensor_scalar(dst, sh, w, None, ALU.mult)
                    else:
                        dve.wait_ge(s(f"fir{k}"), j)
                        ins = dve.scalar_tensor_tensor(out=dst, in0=sh, scalar=w, in1=dst, op0=ALU.mult, op1=ALU.add)
                    ins.then_inc(s(f"fir{k}"), 1)

                dve.wait_ge(s("pads"), 3)
                convolve("v", v_raw, conv[:, 2])
                convolve("k", k_raw, conv[:, 1])
                convolve("q", q_raw, conv[:, 0])
                dve.wait_ge(s("beta_tanh"), 1)
                dve.tensor_scalar(beta[:, :], beta[:, :], 0.5, 0.5, ALU.mult, ALU.add).then_inc(s("beta"), 1)
                dve.wait_ge(s("k_rnorm"), 1)
                dve.tensor_tensor(k_n[:, :], k_n[:, :], nrm[:, 1, :], ALU.mult).then_inc(s("k_n"), 1)
                dve.wait_ge(s("q_rnorm"), 1)
                dve.tensor_tensor(kbq[:, 1, :], kbq[:, 1, :], nrm[:, 0, :], ALU.mult).then_inc(s("kbq"), 1)
                dve.wait_ge(s("k_n"), 1)
                dve.wait_ge(s("beta"), 1)
                dve.tensor_tensor(kbq[:, 0, :], k_n[:, :], beta[:, :], ALU.mult).then_inc(s("kbq"), 1)
                dve.wait_ge(s("v_act"), 1)
                dve.tensor_tensor(vb[:, :].rearrange("p (b t) -> p b t", b=NB), v_pad[:, :, PADF:],
                                  beta[:, :].rearrange("p (b t) -> p b t", b=NB), ALU.mult).then_inc(s("vb"), 1)
                dve.transpose(ka[:, :, 0:32], k_n[:, :].rearrange("p (g i) -> p g i", g=G)).then_inc(s("ka"), 1)
                dve.wait_ge(s("kbq"), 2)
                dve.transpose(kv[:, :, 0:32], kbq[:, 0, :].rearrange("p (g i) -> p g i", g=G)).then_inc(s("kv"), 1)
                dve.wait_ge(s("vb"), 1)
                dve.transpose(kv[:, :, 32:64], vb[:, :].rearrange("p (g i) -> p g i", g=G)).then_inc(s("kv"), 1)
                for j in range(3):
                    fir_tap(1, j)
                dve.wait_ge(s("r1"), 4)
                for half in range(2):
                    src = banks(6 if half == 0 else 0, 2).rearrange("p (g c) -> p g c", c=64)
                    dve.tensor_tensor(ka[:, 16 * half:16 * half + 16, 32:64], src[:, :, 32:64],
                                      keep_j_le_i[:, :].unsqueeze(1).broadcast_to([P, 16, CH]),
                                      ALU.mult).then_inc(s("ka"), 1)
                    dve.tensor_copy(wu[:, 16 * half:16 * half + 16, 0:32], src[:, :, 0:32]).then_inc(s("a_copy"), 1)
                dve.wait_ge(s("a_copy"), 2)
                dve.transpose(Dm[:, :, :], wu[:, :, 0:32].rearrange("p g i -> p i g")).then_inc(s("inv"), 1)
                dve.wait_ge(s("inv"), 1)
                dve.tensor_tensor(Dm[:, :, :], Dm[:, :, :], low_free[:, :, :], ALU.mult).then_inc(s("inv"), 1)
                for j in range(1, CH - 1):
                    r = CH - 1 - j
                    dve.wait_ge(s("inv"), 2 * j)
                    t2 = tmp[:, 0:r * j].rearrange("p (r c) -> p r c", c=j)
                    dve.tensor_tensor(t2, Dm[:, j + 1:, j:j + 1].broadcast_to([P, r, j]),
                                      Dm[:, j:j + 1, 0:j].broadcast_to([P, r, j]), ALU.mult).then_inc(s("inv"), 1)
                    dve.wait_ge(s("inv"), 1 + 2 * j)
                    dve.tensor_tensor(Dm[:, j + 1:, 0:j], Dm[:, j + 1:, 0:j], t2, ALU.add).then_inc(s("inv"), 1)
                dve.wait_ge(s("inv"), 2 + 2 * 30)
                dve.transpose(Dt[:, :, :].rearrange("p g i -> p i g"), Dm[:, :, :]).then_inc(s("inv"), 1)
                dve.wait_ge(s("inv"), 3 + 2 * 30)
                dve.tensor_tensor(Dt[:, :, :], Dt[:, :, :], eye_quad[:, :].unsqueeze(1).broadcast_to([P, G, CH]), ALU.add)\
                    .then_inc(s("Dt"), 1)
                for j in range(7):
                    fir_tap(2, j)
                dst = fir[:, 4, :].rearrange("p (b t) -> p b t", b=NB)
                for j in range(DVE_TAPS):
                    dve.wait_ge(s("fir31"), j + 1)
                    dve.scalar_tensor_tensor(out=dst, in0=v_pad[:, :, j:j + L], scalar=fir_w[:, FOFF[4] + j:FOFF[4] + j + 1], in1=dst,
                                             op0=ALU.mult, op1=ALU.add).then_inc(s("fir31"), 1)
                dve.wait_ge(s("r3"), 4)
                src = banks(0, 4).rearrange("p (g c) -> p g c", c=64)
                dve.scalar_tensor_tensor(out=pt[:, :, :], in0=src[:, :, 0:32], scalar=-1.0,
                                         in1=eye_quad[:, :].unsqueeze(1).broadcast_to([P, G, DH]),
                                         op0=ALU.mult, op1=ALU.add).then_inc(s("pt"), 1)
                dve.tensor_tensor(qwT[:, :].rearrange("p (g i) -> p g i", g=G),
                                  kbq[:, 1, :].rearrange("p (g i) -> p g i", g=G), src[:, :, 32:64],
                                  ALU.subtract).then_inc(s("qwT"), 1)
                dve.wait_ge(s("gk"), 1)
                dve.tensor_copy(state[:, :, 1, :], gk[:, :, 0, :]).then_inc(s("state"), 1)
                for n in range(1, NC - 1):
                    fir_tap(3, n - 1)
                    dve.wait_ge(s("scan"), n)
                    dve.tensor_tensor(state[:, :, n + 1, :], banks(6)[:, 0:64].rearrange("p (b e) -> p b e", b=NB),
                                      gk[:, :, n, :], ALU.add).then_inc(s("state"), 1)
                fir_tap(3, 14)
                dve.wait_ge(s("logits"), 1)
                dve.tensor_tensor(gl[:, 3], banks(6)[:, 0:NT * 28].rearrange("p (t c) -> p t c", c=28),
                                  gb2[:, :].unsqueeze(1).broadcast_to([P, NT, 28]), ALU.add).then_inc(s("sp_bias"), 1)
                dve.wait_ge(s("sp_bias"), 1)
                dve.wait_ge(s("logits"), 2)
                dve.tensor_tensor(gl[:, 0], gl[:, 3], banks(2)[:, 0:NT * 28].rearrange("p (t c) -> p t c", c=28), ALU.add)\
                    .then_inc(s("sp_bias"), 1)
                dve.wait_ge(s("sp_bias"), 2)
                dve.tensor_scalar(gl[:, 1], gl[:, 0], 0.0, None, ALU.max).then_inc(s("sp_max"), 1)
                dve.wait_ge(s("sp_max"), 1)
                dve.wait_ge(s("sp_ln"), 1)
                dve.scalar_tensor_tensor(out=gl[:, 3], in0=gl[:, 2], scalar=0.02, in1=gl[:, 1],
                                         op0=ALU.add, op1=ALU.add).then_inc(s("wraw"), 1)
                of_head = gl[:, 3].rearrange("p t (h s) -> p (t h) s", s=S7)
                dve.wait_ge(s("wraw"), 1)
                dve.tensor_reduce(gden[:, 0], of_head, AX.X, ALU.add).then_inc(s("den"), 1)
                dve.wait_ge(s("den"), 1)
                dve.reciprocal(gden[:, 1], gden[:, 0]).then_inc(s("rden"), 1)
                dve.wait_ge(s("rden"), 1)
                dve.tensor_tensor(of_head, of_head, gden[:, 1].unsqueeze(2).broadcast_to([P, NT * H, S7]), ALU.mult)\
                    .then_inc(s("wts"), 1)
                dve.wait_ge(s("wts_turned"), 1)
                dve.tensor_copy(halves[0:28], banks(0, 2)[0:28]).then_inc(s("halves"), 1)
                dve.wait_ge(s("halves"), 1)
                dve.tensor_tensor(halves[32:60], banks(0, 2)[0:28], halves[0:28].bitcast(F32), ALU.subtract).then_inc(s("halves"), 1)
                ab_flat = [ab[:, n, :] for n in range(2)]
                goes_to = (acc[:, :], hmid[:, 0, :], ab_flat[0], hmid[:, 1, :], ab_flat[1], hmid[:, 1, :], ab_flat[0])
                adds = 0
                for k in range(S7):
                    st = fir[:, k, :] if k < 5 else delta[:, :] if k == 5 else v_pad[:, :, PADF:]
                    dve.wait_ge(s("expand"), 2 * k + 2)
                    if k == 0:
                        dve.wait_ge(s("streams"), 7)
                    src, dst = banks(4 + 2 * (k % 2), 2), goes_to[k]
                    if k == 5:
                        dve.wait_ge(s("pool_sum"), 1)
                    if k == 6:
                        dve.wait_ge(s("o_sum"), 1)
                        src, dst = (z.rearrange("p (b t) -> p b t", b=NB) for z in (src, dst))
                    dve.tensor_tensor(dst, src, st, ALU.mult).then_inc(s("prod"), 1)
                    if k in (2, 4, 6):
                        dve.wait_ge(s("prod"), k + 1)
                        if adds:
                            dve.wait_ge(s("o_sum"), adds)
                        dve.tensor_tensor(acc[:, :], acc[:, :], goes_to[k], ALU.add).then_inc(s("o_sum"), 1)
                        adds += 1
                dve.wait_ge(s("o_sum"), adds)
                dve.wait_ge(s("pool_sum"), 2)
                for b in range(NB):
                    at = slice(b * L, (b + 1) * L)
                    dve.tensor_tensor(acc[:, at], acc[:, at], hmid[:, 0, at], ALU.add).then_inc(s("o_sum"), 1)
                for b in range(NB):
                    at = slice(b * L, (b + 1) * L)
                    dve.wait_ge(s("o_rroot"), b + 1)
                    dve.tensor_tensor(acc[:, at], acc[:, at], ab[:, 1, at], ALU.mult).then_inc(s("o_n"), 1)

                def norm(n, name, bank, resid, dst):
                    for b in range(NB):
                        of_b = slice(4 * b, 4 * b + 4)
                        dve.wait_ge(s(name + "_out"), b + 1)
                        dve.tensor_tensor(dst[:, of_b, :], banks(bank + b).rearrange("p (t d) -> p t d", d=D), resid[:, of_b, :],
                                          ALU.add).then_inc(s("ln_res"), 1)
                        dve.wait_ge(s("ln_res"), NB * n + b + 1)
                        for tt in range(4 * b, 4 * b + 4):
                            dve.bn_stats(bn6[:, tt, :], dst[:, tt, :]).then_inc(s("ln_stats"), 1)
                        dve.wait_ge(s("ln_stats"), NT * n + 4 * b + 4)
                        for tt in range(4 * b, 4 * b + 4):
                            dve.bn_aggr(bn2[:, tt, :], bn6[:, tt, :]).then_inc(s("ln_var"), 1)
                    for b in range(NB):
                        of_b = slice(4 * b, 4 * b + 4)
                        dve.wait_ge(s("ln_root"), NB * n + b + 1)
                        dve.reciprocal(rstd[:, of_b], rstd[:, of_b]).then_inc(s("ln_rstd"), 1)
                        dve.wait_ge(s("ln_rstd"), NB * n + b + 1)
                        for tt in range(4 * b, 4 * b + 4):
                            dve.tensor_scalar(dst[:, tt, :], dst[:, tt, :], bn2[:, tt, 0:1], rstd[:, tt:tt + 1],
                                              ALU.subtract, ALU.mult).then_inc(s(name), 1)

                norm(0, "x1", 0, x_tc, x1)
                dve.wait_ge(s("x1T"), 2)
                for b in range(NB):
                    dve.tensor_scalar(pooled_b[:, b, :], ones[:, :], pooled[:, b:b + 1], 1 / L, ALU.mult, ALU.mult)\
                        .then_inc(s("pooled_b"), 1)
                e8 = lambda n: rt[:, n, :].rearrange("p (b e) -> p b e", b=NB)
                e1 = lambda n: rt[:, n, 0:NB]
                wide = lambda ap: ap.unsqueeze(2).broadcast_to([P, NB, E])
                dve.wait_ge(s("gate8"), 1)
                dve.tensor_reduce(e1(0), banks(6)[:, 0:2 * E].rearrange("p (b e) -> p b e", b=NB), AX.X, ALU.max)\
                    .then_inc(s("choice"), 1)
                dve.wait_ge(s("choice"), 1)
                dve.tensor_tensor(e8(1), banks(6)[:, 0:2 * E].rearrange("p (b e) -> p b e", b=NB), wide(e1(0)),
                                  ALU.subtract).then_inc(s("choice"), 1)
                dve.wait_ge(s("gate_exp"), 1)
                dve.tensor_reduce(e1(2), e8(1), AX.X, ALU.add).then_inc(s("choice"), 1)
                dve.wait_ge(s("choice"), 3)
                dve.reciprocal(e1(3), e1(2)).then_inc(s("choice"), 1)
                dve.wait_ge(s("choice"), 4)
                dve.tensor_tensor(e8(4), e8(1), wide(e1(3)), ALU.mult).then_inc(s("choice"), 1)
                dve.wait_ge(s("choice"), 5)
                mine = e8(4).unsqueeze(3).broadcast_to([P, NB, E, E])
                others = e8(4).unsqueeze(2).broadcast_to([P, NB, E, E])
                dve.tensor_tensor(pair8[:, :, :, :], others, mine, ALU.is_gt).then_inc(s("choice"), 1)
                dve.tensor_tensor(eq8[:, :, :, :], others, mine, ALU.is_equal).then_inc(s("choice"), 1)
                dve.wait_ge(s("choice"), 7)
                dve.tensor_tensor(eq8[:, :, :, :], eq8[:, :, :, :], eight_low[:, :, :].unsqueeze(1).broadcast_to([P, NB, E, E]),
                                  ALU.mult).then_inc(s("choice"), 1)
                dve.wait_ge(s("choice"), 8)
                dve.tensor_tensor(pair8[:, :, :, :], pair8[:, :, :, :], eq8[:, :, :, :], ALU.add).then_inc(s("choice"), 1)
                dve.wait_ge(s("choice"), 9)
                dve.tensor_reduce(e8(5), pair8[:, :, :, :], AX.X, ALU.add).then_inc(s("choice"), 1)
                dve.wait_ge(s("choice"), 10)
                dve.scalar_tensor_tensor(out=e8(5), in0=e8(5), scalar=1.5, in1=e8(4), op0=ALU.is_lt, op1=ALU.mult)\
                    .then_inc(s("choice"), 1)
                dve.wait_ge(s("choice"), 11)
                dve.tensor_reduce(e1(2), e8(5), AX.X, ALU.add).then_inc(s("choice"), 1)
                dve.wait_ge(s("choice"), 12)
                dve.tensor_scalar(e1(2), e1(2), 1e-8, None, ALU.add).then_inc(s("choice"), 1)
                dve.wait_ge(s("choice"), 13)
                dve.reciprocal(e1(3), e1(2)).then_inc(s("choice"), 1)
                dve.wait_ge(s("choice"), 14)
                dve.tensor_tensor(e8(6), e8(5), wide(e1(3)), ALU.mult).then_inc(s("choice"), 1)
                dve.wait_ge(s("choice"), 15)
                for b in range(NB):
                    dve.tensor_tensor(pair8[:, b, 0:4, :], e8(6)[:, b:b + 1, :].broadcast_to([P, 4, E]), pick[:, :, :],
                                      ALU.mult).then_inc(s("choice"), 1)
                dve.tensor_tensor(cdiag[:, :, :], e8(6)[0:E], ident[0:E, 0:E].unsqueeze(1).broadcast_to([E, NB, E]),
                                  ALU.mult).then_inc(s("choice"), 1)
                dve.wait_ge(s("choice"), 18)
                dve.tensor_reduce(cvec[:, :, :], pair8[:, :, 0:4, :], AX.X, ALU.add).then_inc(s("choice"), 1)
                dve.tensor_reduce(cd[:, :], cdiag[:, :, :], AX.X, ALU.add).then_inc(s("choice"), 1)
                dve.wait_ge(s("choice"), 20)
                for b in range(NB):
                    for m in range(4):
                        dve.tensor_scalar(ups[:, b, m, :], upT[:, m, :], cvec[:, b, m:m + 1], None, ALU.mult).then_inc(s("ups"), 1)
                    dve.tensor_scalar(c_rows[:, b, :], ones[0:E, :], cd[:, b:b + 1], None, ALU.mult).then_inc(s("ups"), 1)

                norm(1, "x2", 2, x1, x2)
                for half in range(2):
                    dve.wait_ge(s("v_proj2"), 2 * half + 2)
                    dve.tensor_copy(ve[:, 8 * half:8 * half + 8, :, 0:DH],
                                    banks((6, 0)[half], 2).rearrange("p (j h d) -> p j h d", h=H, d=DH)).then_inc(s("ve"), 1)
                for b in range(NB):
                    for m in range(2):
                        dve.wait_ge(s("scores"), 4 * b + 2 * m + 2)
                        bank = ((2, 4), (6, 0))[b][m]
                        dve.tensor_tensor(sc[b][:, 8 * m:8 * m + 8, :], banks(bank, 2).rearrange("p (n k) -> p n k", k=P),
                                          wmask[:, :].unsqueeze(1).broadcast_to([P, 8, P]), ALU.add).then_inc(s("masked"), 1)
                    dve.wait_ge(s("masked"), 2 * b + 2)
                    dve.tensor_reduce(mx[:, b, :], sc[b], AX.X, ALU.max).then_inc(s("row_max"), 1)
                    dve.wait_ge(s("row_max"), b + 1)
                    dve.tensor_tensor(sc[b], sc[b], mx[:, b, :].unsqueeze(2).broadcast_to([P, 16, P]), ALU.subtract)\
                        .then_inc(s("shifted"), 1)
                for t in range(NT):
                    if t % 4 == 0:
                        dve.wait_ge(s("pv"), t // 4 + 1)
                    at = banks(2 + t // 2)[:, (t % 2) * 132:(t % 2) * 132 + 132].rearrange("p (h e) -> p h e", h=H)
                    dve.reciprocal(ri[:, t, :].unsqueeze(2), at[:, :, DH:DH + 1]).then_inc(s("ri"), 1)
                    dve.wait_ge(s("ri"), t + 1)
                    dve.tensor_tensor(ao[:, t, :].rearrange("p (h e) -> p h e", h=H), at[:, :, 0:DH],
                                      ri[:, t, :].unsqueeze(2).broadcast_to([P, H, DH]), ALU.mult).then_inc(s("ao"), 1)
                dve.wait_ge(s("pred"), 2)
                dve.wait_ge(s("swaT"), 1)
                dve.scalar_tensor_tensor(out=eT.rearrange("p b t -> p (b t)"), in0=banks(2, 2), scalar=b2c[:, 0:1], in1=swaT,
                                         op0=ALU.add, op1=ALU.subtract).then_inc(s("eT"), 1)
                def z_bias(t):
                    dve.wait_ge(s("z"), t + 1)
                    dve.tensor_tensor(zb[:, t % 2, :], banks((6, 0)[t % 2]), b1r[:, :], ALU.add).then_inc(s("zb"), 1)

                z_bias(0)
                for t in range(NT):
                    o = t % 2
                    if t + 1 < NT:
                        z_bias(t + 1)
                    if t >= 2:
                        dve.wait_ge(s("dw"), t - 1)
                    if t == 0:
                        dve.wait_ge(s("eT"), 1)
                        dve.tensor_reduce(esum[:, :], eT.rearrange("p b t -> p (b t)"), AX.X, ALU.add).then_inc(s("esum"), 1)
                        dve.wait_ge(s("esum"), 1)
                        dve.tensor_tensor(gb2s[:, :], gb2s[:, :], esum[:, :], ALU.add).then_inc(s("gb2"), 1)
                    dve.wait_ge(s("a_th"), 2 * t + 2)
                    if t >= 2:
                        dve.wait_ge(s("dzsum"), t - 1)
                    dve.scalar_tensor_tensor(out=t1[:, o, :], in0=zb[:, o, :], scalar=1.0, in1=a_tc[:, o, :], op0=ALU.add,
                                             op1=ALU.subtract).then_inc(s("dz_steps"), 1)
                    dve.wait_ge(s("dz_steps"), 2 * t + 1)
                    dve.scalar_tensor_tensor(out=t1[:, o, :], in0=th[:, o, :], scalar=1.0, in1=t1[:, o, :], op0=ALU.add,
                                             op1=ALU.mult).then_inc(s("dz_steps"), 1)
                    dve.wait_ge(s("dz_steps"), 2 * t + 2)
                    dve.wait_ge(s("da"), t + 1)
                    dve.scalar_tensor_tensor(out=dz[:, o, :], in0=t1[:, o, :], scalar=0.5, in1=banks((7, 1)[o]), op0=ALU.mult,
                                             op1=ALU.mult).then_inc(s("dz"), 1)
                dve.wait_ge(s("dw"), NT)
                dve.tensor_tensor(gW2[:, :], gW2[:, :], banks(2), ALU.add).then_inc(s("gw"), 1)
                dve.tensor_tensor(gW1[:, :], gW1[:, :], banks(3), ALU.add).then_inc(s("gw"), 1)
                dve.wait_ge(s("gw"), 2)
                dve.wait_ge(s("gb2"), 1)
                dve.sem_inc(s("step_done"), 1)
                dve.wait_ge(step_go, i + 1)

            dve.tensor_scalar(keep_lr[:, 0:1], keep_lr[:, 0:1], -1.0, 1.0, ALU.mult, ALU.add).then_inc(s2("lr"), 1)
            dve.tensor_scalar(keep_lr[:, 1:2], keep_lr[:, 1:2], -1.0, None, ALU.mult).then_inc(s2("lr"), 1)
            dve.wait_ge(s2("lr"), 2)
            one_less, step = keep_lr[:, 0:1], keep_lr[:, 1:2]
            w1flat = w1T[:, :, :].rearrange("p m c -> p (m c)")
            dve.wait_ge(s2("db1"), 1)
            for grad, g_in in ((gW2[:, :], gW2[:, :]), (gW1[:, :], gW1[:, :]), (gb2s[:, :], gb2s[:, :]), (rt[:, 0, 0:4], banks(7)[:, 0:4])):
                dve.tensor_scalar(grad, g_in, step, None, ALU.mult).then_inc(s2("stepped"), 1)
            for n, (w, grad) in enumerate(((w2[:, :], gW2[:, :]), (w1flat, gW1[:, :]), (b2c[:, :], gb2s[:, :]), (b1c[:, :], rt[:, 0, 0:4]))):
                dve.wait_ge(s2("stepped"), n + 1)
                dve.scalar_tensor_tensor(out=w, in0=w, scalar=one_less, in1=grad, op0=ALU.mult, op1=ALU.add)\
                    .then_inc(s2("updated"), 1)
            for n in range(E):
                dve.wait_ge(s2("w1_high"), n + 1)
                dve.tensor_tensor(w1_low[n][:, :, :], banks(turn_bank(n)).rearrange("p (m c) -> p m c", m=4), w1_high[:, n, :, :].bitcast(F32),
                                  ALU.subtract).then_inc(s2("w1_low"), 1)
            for n in range(0, E, 2):
                dve.wait_ge(s2("e_turned"), E + n + 1)
                dve.tensor_copy(w2eT[:, n, :, :], banks(turn_bank(E + n)).rearrange("p (m c) -> p m c", m=4)).then_inc(s2("e_even"), 1)
            dve.wait_ge(s2("w2_turned"), 1)
            dve.tensor_copy(w2T[:, :, :], banks(0).rearrange("p (m c) -> p m c", m=4)).then_inc(s2("ready2"), 1)
            dve.wait_ge(s2("w2_turned"), 2)
            dve.tensor_copy(lT[:, :, :], banks(1)[:, 0:2 * D].rearrange("p (m c) -> p m c", m=2)).then_inc(s2("ready2"), 1)

            def norm2(name, src, dst):
                for t in range(NT):
                    dve.bn_stats(bn6[:, t, :], src[:, t * D:(t + 1) * D]).then_inc(s2(name + "_stats"), 1)
                dve.wait_ge(s2(name + "_stats"), NT)
                for t in range(NT):
                    dve.bn_aggr(bn2[:, t, :], bn6[:, t, :]).then_inc(s2(name + "_var"), 1)
                dve.wait_ge(s2(name + "_root"), 1)
                dve.reciprocal(rstd[:, :], rstd[:, :]).then_inc(s2(name + "_rstd"), 1)
                dve.wait_ge(s2(name + "_rstd"), 1)
                for t in range(NT):
                    dve.tensor_scalar(dst[:, t * D:(t + 1) * D], src[:, t * D:(t + 1) * D], bn2[:, t, 0:1], rstd[:, t:t + 1],
                                      ALU.subtract, ALU.mult).then_inc(s2(name), 1)

            def merge():
                dve.wait_ge(s2("tg"), 1)
                dve.scalar_tensor_tensor(out=mT, in0=tg[:, 0, :], scalar=1.0, in1=bswaT, op0=ALU.add, op1=ALU.mult)\
                    .then_inc(s2("merge"), 1)
                dve.wait_ge(s2("tg"), 2)
                dve.scalar_tensor_tensor(out=tg[:, 1, :], in0=tg[:, 1, :], scalar=1.0, in1=omT, op0=ALU.add, op1=ALU.mult)\
                    .then_inc(s2("merge"), 1)
                dve.wait_ge(s2("merge"), 2)
                dve.tensor_tensor(mT, mT, tg[:, 1, :], ALU.add).then_inc(s2("merged"), 1)

            def third_norm():
                dve.wait_ge(s2("in_x2"), 16)
                dve.wait_ge(s2("m_turned"), 2)
                dve.scalar_tensor_tensor(out=x3, in0=banks(4, 2), scalar=0.5, in1=bx2, op0=ALU.mult, op1=ALU.add)\
                    .then_inc(s2("x3_res"), 1)
                dve.wait_ge(s2("x3_res"), 1)
                norm2("x3", x3, x3)

            def route():
                dve.wait_ge(s2("r_logits"), 1)
                wide3 = lambda ap: ap.unsqueeze(2).broadcast_to([P, NT, E])
                col = lambda n: rw[:, 4, n, 0:NT]
                dve.tensor_tensor(rw[:, 0], banks(4)[:, 0:NT * E].rearrange("p (t e) -> p t e", e=E),
                                  brr[:, :].unsqueeze(1).broadcast_to([P, NT, E]), ALU.add).then_inc(s2("route"), 1)
                dve.wait_ge(s2("route"), 1)
                dve.tensor_reduce(col(0), rw[:, 0], AX.X, ALU.max).then_inc(s2("route"), 1)
                dve.wait_ge(s2("route"), 2)
                dve.tensor_tensor(rw[:, 1], rw[:, 0], wide3(col(0)), ALU.subtract).then_inc(s2("route"), 1)
                mine = rw[:, 0].unsqueeze(3).broadcast_to([P, NT, E, E])
                others = rw[:, 0].unsqueeze(2).broadcast_to([P, NT, E, E])
                dve.tensor_tensor(tok_pair, others, mine, ALU.is_gt).then_inc(s2("route"), 1)
                dve.tensor_tensor(tok_equal, others, mine, ALU.is_equal).then_inc(s2("route"), 1)
                dve.wait_ge(s2("route"), 5)
                dve.tensor_tensor(tok_equal, tok_equal, eight_low[:, :, :].unsqueeze(1).broadcast_to([P, NT, E, E]),
                                  ALU.mult).then_inc(s2("route"), 1)
                dve.wait_ge(s2("route"), 6)
                dve.tensor_tensor(tok_pair, tok_pair, tok_equal, ALU.add).then_inc(s2("route"), 1)
                dve.wait_ge(s2("route"), 7)
                dve.tensor_reduce(rw[:, 2], tok_pair, AX.X, ALU.add).then_inc(s2("route"), 1)
                dve.wait_ge(s2("route"), 8)
                dve.wait_ge(s2("r_exp"), 1)
                dve.scalar_tensor_tensor(out=rw[:, 2], in0=rw[:, 2], scalar=1.5, in1=rw[:, 1], op0=ALU.is_lt, op1=ALU.mult)\
                    .then_inc(s2("route"), 1)
                dve.wait_ge(s2("route"), 9)
                dve.tensor_reduce(col(1), rw[:, 2], AX.X, ALU.add).then_inc(s2("route"), 1)
                dve.wait_ge(s2("route"), 10)
                dve.reciprocal(col(2), col(1)).then_inc(s2("route"), 1)
                dve.wait_ge(s2("route"), 11)
                dve.tensor_tensor(rw[:, 3], rw[:, 2], wide3(col(2)), ALU.mult).then_inc(s2("weights"), 1)

            def fourth_norm(yn, scaled, x4):
                norm2(yn, y, y)
                y3 = y.rearrange("p (t d) -> p t d", d=D)
                dve.wait_ge(s2(yn), NT)
                dve.tensor_tensor(y3, y3, gamma_r[:, :].unsqueeze(1).broadcast_to([P, NT, D]), ALU.mult).then_inc(s2(scaled), 1)
                dve.wait_ge(s2(scaled), 1)
                dve.tensor_tensor(y3, y3, beta_r[:, :].unsqueeze(1).broadcast_to([P, NT, D]), ALU.add).then_inc(s2(scaled), 1)
                dve.wait_ge(s2(scaled), 2)
                dve.tensor_tensor(y, y, x3_keep, ALU.add).then_inc(s2(scaled), 1)
                dve.wait_ge(s2(scaled), 3)
                norm2(x4, y, x3_keep)

            def experts(first, last):
                dve.wait_ge(s2("x3_high"), 1)
                dve.tensor_tensor(x3_low[:, :], x3T, x3_high[:, :].bitcast(F32), ALU.subtract).then_inc(s2("x3_low"), 1)
                dve.tensor_copy(rw_keep, rw[:, 3]).then_inc(s2("rw_keep"), 1)
                if not first:
                    fourth_norm("yn", "scaled", "x4")
                    dve.wait_ge(s2("x4"), NT)
                dve.wait_ge(s2("y_bias"), 2)
                dve.tensor_tensor(y, banks(0, 2), x3, ALU.add).then_inc(s2("y"), 1)
                dve.wait_ge(s2("rw_keep"), 1)
                for e in range(E):
                    for t in range(NT):
                        if t % 4 == 0:
                            dve.wait_ge(s2("o"), 2 * e + t // 4 + 1)
                        dve.wait_ge(s2("y"), 1 + max(0, NT * (e - 1) + t + 1))
                        yt = y[:, t * D:(t + 1) * D]
                        bank = (6, 0)[e % 2] + t // 4
                        dve.scalar_tensor_tensor(out=yt, in0=banks(bank)[:, (t % 4) * D:(t % 4 + 1) * D], scalar=rw_keep[:, t, e:e + 1],
                                                 in1=yt, op0=ALU.mult, op1=ALU.add).then_inc(s2("y"), 1)
                    if e == 3 and not last:
                        merge()
                    if e == 4:
                        if not first:
                            dve.wait_ge(s2("stored"), 16)
                        dve.tensor_copy(x3_keep, x3).then_inc(s2("x3_keep"), 1)
                        if not last:
                            dve.wait_ge(s2("x3_keep"), 1)
                            third_norm()
                    if e == 6 and not last:
                        route()
                dve.wait_ge(s2("y"), 1 + NT * E)
                dve.wait_ge(s2("x3_keep"), 1)

            merge()
            third_norm()
            route()
            dve.wait_ge(s2("weights"), 1)
            dve.sem_inc(s2("step_done"), 1)
            dve.wait_ge(once("step2_go"), 1)
            experts(True, False)
            dve.sem_inc(s2("step_done"), 1)
            dve.wait_ge(once("step2_go"), 2)
            with dve.Fori(1, PAIRS - 1) as i:
                experts(False, False)
                dve.wait_ge(s2("weights"), 1)
                dve.sem_inc(s2("step_done"), 1)
                dve.wait_ge(once("step2_go"), i + 2)
            experts(False, True)
            fourth_norm("last_yn", "last_scaled", "last_x4")

        @block.scalar
        def _(act):
            act.wait_ge(prepared, 3)
            act.wait_ge(once("m_dve"), 6)
            act.activation(m_sc[0:NM, :, :], m_sc[0:NM, :, :], ACT.Exp, scale=DH ** -0.5).then_inc(once("m_act"), 1)
            act.wait_ge(once("m_pe"), 7)
            for m in range(4):
                act.activation(m_aT[:, m, :], banks(2)[:, m * NM:(m + 1) * NM], ACT.Silu, bias=b1c[:, m:m + 1])\
                    .then_inc(once("m_act"), 1)
            act.wait_ge(once("m_dve"), 12)
            act.activation(m_a[0:NM, :], m_zb[0:NM, :], ACT.Silu).then_inc(once("m_act"), 1)
            act.activation(m_th[0:NM, :], m_zb[0:NM, :], ACT.Tanh, scale=0.5).then_inc(once("m_act"), 1)
            act.wait_ge(once("m_done"), 1)
            act.wait_ge(once("filled"), 1)
            with act.Fori(0, PAIRS) as i:
                for b in range(NB):
                    act.wait_ge(s("x_turned"), b + 1)
                    act.activation(xT[:, b, :], banks(b), ACT.Copy).then_inc(s("xT"), 1)
                for name, dst, bank in (("v", v_raw, 6), ("k", k_raw, 4), ("q", q_raw, 2)):
                    for b in range(NB):
                        act.wait_ge(s(name + "_proj"), b + 1)
                        act.activation(dst[:, b, PADC:], banks(bank + b), ACT.Copy).then_inc(s(name + "_raw"), 1)
                act.wait_ge(s("b_proj"), 2)
                act.activation(beta[:, :], banks(0, 2), ACT.Tanh, scale=0.5).then_inc(s("beta_tanh"), 1)
                act.wait_ge(s("v_conv"), 4)
                act.activation(v_pad[:, :, PADF:], conv[:, 2], ACT.Silu).then_inc(s("v_act"), 1)
                act.wait_ge(s("k_conv"), 4)
                act.activation(k_n[:, :], conv[:, 1].rearrange("p b t -> p (b t)"), ACT.Silu).then_inc(s("k_act"), 1)
                act.wait_ge(s("k_act"), 1)
                act.activation(sq[:, 1, :], k_n[:, :], ACT.Square).then_inc(s("k_sq"), 1)
                act.wait_ge(s("q_conv"), 4)
                act.activation(kbq[:, 1, :], conv[:, 0].rearrange("p b t -> p (b t)"), ACT.Silu).then_inc(s("q_act"), 1)
                act.wait_ge(s("q_act"), 1)
                act.activation(sq[:, 0, :], kbq[:, 1, :], ACT.Square).then_inc(s("q_sq"), 1)
                act.wait_ge(s("k_ss"), 2)
                act.activation(nrm[:, 1, :], banks(4, 2), ACT.Ln, bias=eps6[:, 0:1]).then_inc(s("k_norm"), 1)
                act.wait_ge(s("q_ss"), 2)
                act.activation(nrm[:, 0, :], banks(0, 2), ACT.Ln, bias=eps6[:, 0:1]).then_inc(s("q_norm"), 1)
                act.wait_ge(s("k_norm"), 1)
                act.activation(nrm[:, 1, :], nrm[:, 1, :], ACT.Exp, scale=-0.5).then_inc(s("k_rnorm"), 1)
                act.wait_ge(s("q_norm"), 1)
                act.activation(nrm[:, 0, :], nrm[:, 0, :], ACT.Exp, scale=-0.5).then_inc(s("q_rnorm"), 1)
                act.wait_ge(s("v_act"), 1)
                act.activation(fir[:, 0, :].rearrange("p (b t) -> p b t", b=NB), v_pad[:, :, PADF:], ACT.Copy,
                               scale=fir_w[:, 0:1]).then_inc(s("fir1"), 1)

                def magnitude(n, src, k):
                    if n >= 2:
                        act.wait_ge(s("stat"), 2 * (n - 1))
                    dst = ab[:, n % 2, :]
                    if k == 6:
                        dst = dst.rearrange("p (b t) -> p b t", b=NB)
                    act.activation(dst, src, ACT.Abs).then_inc(s("streams"), 1)

                magnitude(0, v_pad[:, :, PADF:], 6)
                act.wait_ge(s("fir1"), 1)
                magnitude(1, fir[:, 0, :], 0)
                act.wait_ge(s("fir31_psum"), 2)
                act.activation(fir[:, 4, :], banks(2, 2), ACT.Copy).then_inc(s("fir31"), 1)
                for m in range(2):
                    act.wait_ge(s("r2"), 2 * m + 2)
                    act.activation(wu[:, 16 * m:16 * m + 16, :].rearrange("p g c -> p (g c)"), banks(4 + 2 * m, 2),
                                   ACT.Copy).then_inc(s("wu"), 1)
                act.wait_ge(s("r4"), 2)
                act.activation(gk[:, :, :, :].rearrange("p b n e -> p (b n e)"), banks(4, 2), ACT.Copy).then_inc(s("gk"), 1)
                act.wait_ge(s("delta_psum"), 1)
                act.activation(delta[:, :], banks(0, 2), ACT.Copy).then_inc(s("delta"), 1)
                act.wait_ge(s("fir3"), 3)
                magnitude(2, fir[:, 1, :], 1)
                act.wait_ge(s("fir31"), 1 + DVE_TAPS)
                magnitude(3, fir[:, 4, :], 4)
                act.wait_ge(s("fir7"), 7)
                magnitude(4, fir[:, 2, :], 2)
                act.wait_ge(s("fir15"), 15)
                magnitude(5, fir[:, 3, :], 3)
                act.wait_ge(s("delta"), 1)
                magnitude(6, delta[:, :], 5)
                act.wait_ge(s("stat"), 14)
                act.activation(stats[:, :], banks(4, 2)[0:28], ACT.Copy).then_inc(s("stats"), 1)
                for m in range(2):
                    act.wait_ge(s("gate_h"), 2 * m + 2)
                    act.activation(hmid[:, m, :], banks((6, 2)[m], 2), ACT.Gelu, bias=gb1[:, m:m + 1]).then_inc(s("hmid"), 1)
                act.wait_ge(s("sp_bias"), 2)
                act.activation(gl[:, 2], gl[:, 0], ACT.Abs).then_inc(s("sp_abs"), 1)
                act.wait_ge(s("sp_abs"), 1)
                act.activation(gl[:, 2], gl[:, 2], ACT.Exp, scale=-1.0).then_inc(s("sp_exp"), 1)
                act.wait_ge(s("sp_exp"), 1)
                act.activation(gl[:, 2], gl[:, 2], ACT.Ln, bias=one1[:, 0:1]).then_inc(s("sp_ln"), 1)
                for b in range(NB):
                    at = slice(b * L, (b + 1) * L)
                    act.wait_ge(s("o_sum"), 4 + b)
                    act.activation(ab[:, 1, at], acc[:, at], ACT.Square).then_inc(s("o_sq"), 1)
                for b in range(NB):
                    at = slice(b * L, (b + 1) * L)
                    act.wait_ge(s("o_ms"), b + 1)
                    act.activation(ab[:, 1, at], banks(2 + b), ACT.Ln, bias=eps5[:, 0:1], scale=1 / DH).then_inc(s("o_root"), 1)
                for b in range(NB):
                    at = slice(b * L, (b + 1) * L)
                    act.wait_ge(s("o_root"), b + 1)
                    act.activation(ab[:, 1, at], ab[:, 1, at], ACT.Exp, scale=-0.5).then_inc(s("o_rroot"), 1)

                def ln_root(n):
                    for b in range(NB):
                        act.wait_ge(s("ln_var"), NT * n + 4 * b + 4)
                        act.activation(rstd[:, 4 * b:4 * b + 4], bn2[:, 4 * b:4 * b + 4, 1], ACT.Sqrt, bias=eps5[:, 0:1])\
                            .then_inc(s("ln_root"), 1)

                ln_root(0)
                for b in range(NB):
                    act.wait_ge(s("x1_turned"), b + 1)
                    act.activation(x1T[:, b, :], banks(4 + b), ACT.Copy, accum_out=pooled[:, b:b + 1]).then_inc(s("x1T"), 1)
                act.wait_ge(s("choice"), 2)
                act.activation(rt[:, 1, :], rt[:, 1, :], ACT.Exp).then_inc(s("gate_exp"), 1)
                for m in range(4):
                    act.wait_ge(s("down"), 2 * m + 2)
                    act.activation(hf[:, m, :], banks((2, 0, 4, 6)[m], 2), ACT.Gelu, bias=dnb[:, m:m + 1]).then_inc(s("hf"), 1)
                ln_root(1)
                for b in range(NB):
                    act.wait_ge(s("x2_turned"), b + 1)
                    act.activation(xe[:, b, NM:], banks(b), ACT.Copy).then_inc(s("xe"), 1)
                act.wait_ge(s("q_proj2"), 2)
                act.activation(qs, banks(2, 2), ACT.Copy).then_inc(s("qs"), 1)
                act.wait_ge(s("k_proj2"), 2)
                act.activation(ke[:, :, NM:], banks(4, 2).rearrange("p (b t) -> p b t", b=NB), ACT.Copy).then_inc(s("ke"), 1)
                for b in range(NB):
                    act.wait_ge(s("shifted"), b + 1)
                    act.activation(sc[b], sc[b], ACT.Exp, scale=DH ** -0.5).then_inc(s("probs"), 1)
                    for m in range(2):
                        act.wait_ge(s("probs_turned"), 4 * b + 2 * m + 2)
                        bank = ((2, 4), (6, 0))[b][m]
                        act.activation(prT[b][:, 8 * m:8 * m + 8, :].rearrange("p n q -> p (n q)"), banks(bank, 2), ACT.Copy)\
                            .then_inc(s("prT"), 1)
                for b in range(NB):
                    act.wait_ge(s("ao_turned"), b + 1)
                    act.activation(aoT[:, b * L:(b + 1) * L], banks(6 + b), ACT.Copy).then_inc(s("aoT"), 1)
                act.wait_ge(s("wo"), 2)
                act.activation(swaT, banks(0, 2), ACT.Copy).then_inc(s("swaT"), 1)
                for n in range(8):
                    b, m = n // 4, n % 4
                    act.wait_ge(s("zT"), n + 1)
                    act.activation(aT[:, m, b * L:(b + 1) * L], banks(4 + n % 2), ACT.Silu, bias=b1c[:, m:m + 1])\
                        .then_inc(s("aT"), 1)
                act.wait_ge(s("e_turned"), 2)
                act.activation(e_tc.rearrange("p t d -> p (t d)"), banks(4, 2), ACT.Copy).then_inc(s("e_tc"), 1)
                for t in range(NT):
                    o = t % 2
                    act.wait_ge(s("zb"), t + 1)
                    if t >= 2:
                        act.wait_ge(s("dw"), t - 1)
                    act.activation(a_tc[:, o, :], zb[:, o, :], ACT.Silu).then_inc(s("a_th"), 1)
                    act.activation(th[:, o, :], zb[:, o, :], ACT.Tanh, scale=0.5).then_inc(s("a_th"), 1)
                act.wait_ge(s("a_th"), 2 * NT)
                act.sem_inc(s("step_done"), 1)
                act.wait_ge(step_go, i + 1)

            for n in range(E):
                act.wait_ge(s2("e_turned"), n + 1)
                act.activation(w1_high[:, n, :, :].rearrange("p m c -> p (m c)"), banks(turn_bank(n)), ACT.Copy).then_inc(s2("w1_high"), 1)

            def memory_hidden(n):
                b, m = n // 4, n % 4
                act.wait_ge(s2("zT"), n + 1)
                act.activation(baT[:, m, b * L:(b + 1) * L], banks(4 + n % 2), ACT.Silu, bias=b1c[:, m:m + 1]).then_inc(s2("aT"), 1)

            def memory_out():
                act.wait_ge(s2("om"), 2)
                act.activation(omT, banks(4, 2), ACT.Identity, bias=b2c[:, 0:1]).then_inc(s2("omT"), 1)

            def gate(n):
                act.wait_ge(s2(f"g{n + 1}"), 2)
                act.activation(tg[:, n, :], banks(4, 2), ACT.Tanh, scale=0.5).then_inc(s2("tg"), 1)

            def root(name):
                act.wait_ge(s2(name + "_var"), NT)
                act.activation(rstd[:, :], bn2[:, :, 1], ACT.Sqrt, bias=eps5[:, 0:1]).then_inc(s2(name + "_root"), 1)

            def x3_transposed():
                act.wait_ge(s2("x3_turned"), 2)
                act.activation(x3T, banks(4, 2), ACT.Copy).then_inc(s2("x3T"), 1)

            def route_exp():
                act.wait_ge(s2("route"), 3)
                act.activation(rw[:, 1], rw[:, 1], ACT.Exp).then_inc(s2("r_exp"), 1)

            def weights_transposed():
                act.wait_ge(s2("rw_turned"), 1)
                act.activation(rwT, banks(4, 2)[0:E], ACT.Copy).then_inc(s2("rwT"), 1)

            def hidden(e, m):
                for b in range(NB):
                    act.wait_ge(s2("h"), 2 * (4 * e + m) + b + 1)
                    if e >= 2:
                        act.wait_ge(s2("o"), 2 * (e - 1))
                    act.activation(hT[e % 2][:, m, b * L:(b + 1) * L], banks(2 + b), ACT.Relu, bias=b1e[:, e, m:m + 1])\
                        .then_inc(s2("hT"), 1)

            def experts(first, last):
                act.activation(x3_high[:, :], x3T, ACT.Copy).then_inc(s2("x3_high"), 1)
                for m in range(4):
                    hidden(0, m)
                    if m == 1 and not first:
                        root("yn")
                for e in range(E):
                    for m in range(4):
                        if e + 1 < E:
                            hidden(e + 1, m)
                        if e == 0 and m == 0 and not first:
                            root("x4")
                        if e == 0 and not last:
                            memory_hidden(2 * m)
                            memory_hidden(2 * m + 1)
                    if last:
                        continue
                    if e == 1:
                        memory_out()
                    if e == 2:
                        gate(0)
                    if e == 3:
                        gate(1)
                    if e == 4:
                        root("x3")
                    if e == 5:
                        x3_transposed()
                    if e == 6:
                        route_exp()
                    if e == 7:
                        weights_transposed()

            act.wait_ge(s2("updated"), 4)
            for n in range(E):
                if n % 2:
                    act.wait_ge(s2("e_turned"), E + n + 1)
                    act.activation(w2eT[:, n, :, :].rearrange("p m c -> p (m c)"), banks(turn_bank(E + n)), ACT.Copy)\
                        .then_inc(s2("e_odd"), 1)
                memory_hidden(n)
            memory_out()
            gate(0)
            gate(1)
            root("x3")
            x3_transposed()
            route_exp()
            weights_transposed()
            act.wait_ge(s2("rwT"), 1)
            act.sem_inc(s2("step_done"), 1)
            act.wait_ge(once("step2_go"), 1)
            experts(True, False)
            act.wait_ge(s2("rwT"), 1)
            act.sem_inc(s2("step_done"), 1)
            act.wait_ge(once("step2_go"), 2)
            with act.Fori(1, PAIRS - 1) as i:
                experts(False, False)
                act.wait_ge(s2("rwT"), 1)
                act.sem_inc(s2("step_done"), 1)
                act.wait_ge(once("step2_go"), i + 2)
            experts(False, True)
            root("last_yn")
            root("last_x4")

        @block.tensor
        def _(pe):
            pe.wait_ge(prepared, 3)
            up_blocks = up_in.rearrange("p (m a) c -> p m (a c)", a=2)
            for n, block_of in enumerate((lambda m: dn_in[:, m, :], lambda m: up_blocks[:, m, :], lambda m: w1_in[:, m, :],
                                          lambda m: w2[:, m * P:(m + 1) * P], lambda m: sq_in[:, m, :])):
                for m in range(4):
                    mm = pe.transpose(banks(n)[:, m * P:(m + 1) * P], block_of(m), ident[:, :])
                mm.then_inc(once("turned"), 1)
            pe.transpose(banks(5)[:, 0:NM], mem_in[:, :], ident[0:NM, 0:NM]).then_inc(once("turned"), 1)
            pe.wait_ge(once("turned_sb"), 6)
            pe.matmul(banks(0)[:, 0:NM], aw[:, 0, :], memT[:, :], start=True, stop=True)
            pe.matmul(banks(0)[:, NM:2 * NM], aw[:, 1, :], memT[:, :], start=True, stop=True)
            pe.matmul(banks(0)[0:NM, P:P + D], memT[:, :], aw[:, 2, :], start=True, stop=True).then_inc(once("m_pe"), 1)
            pe.wait_ge(once("m_dve"), 3)
            for h in range(H):
                r = slice(DH * h, DH * h + DH)
                mm = pe.matmul(banks(2 + h)[0:NM, 0:NM], m_q[r, :], ke[r, 0, 0:NM], start=True, stop=True)
            mm.then_inc(once("m_pe"), 1)
            pe.wait_ge(once("m_act"), 1)
            for h in range(H):
                mm = pe.transpose(banks(6)[0:NM, h * NM:(h + 1) * NM], m_sc[0:NM, h, :], ident[0:NM, 0:NM])
            mm.then_inc(once("m_pe"), 1)
            pe.wait_ge(once("m_dve"), 7)
            for h in range(H):
                mm = pe.matmul(banks(7)[0:NM, h * 33:(h + 1) * 33], m_prT[0:NM, h, :], m_v[0:NM, h, :], start=True, stop=True)
            mm.then_inc(once("m_pe"), 1)
            pe.wait_ge(once("m_dve"), 9)
            pe.transpose(banks(0)[:, 0:NM], m_ao[0:NM, :], ident[0:NM, 0:NM]).then_inc(once("m_pe"), 1)
            pe.wait_ge(once("m_dve"), 10)
            pe.matmul(banks(1)[:, 0:NM], aw[:, 3, :], m_aoT, start=True, stop=True).then_inc(once("m_pe"), 1)
            for m in range(4):
                mm = pe.matmul(banks(2)[:, m * NM:(m + 1) * NM], w1T[:, m, :], memT[:, :], start=True, stop=True)
            mm.then_inc(once("m_pe"), 1)
            pe.matmul(banks(5)[0:NM], memT[:, :], w1T[:, :, :].rearrange("p m c -> p (m c)"), start=True, stop=True)\
                .then_inc(once("m_pe"), 1)
            pe.wait_ge(once("m_act"), 5)
            for m in range(4):
                mm = pe.matmul(banks(3)[:, 0:NM], w2T[:, m, :], m_aT[:, m, :], start=(m == 0), stop=(m == 3))
            mm.then_inc(once("m_pe"), 1)
            pe.wait_ge(once("m_dve"), 14)
            pe.transpose(banks(4)[0:NM, 0:P], m_eT, ident[:, :]).then_inc(once("m_pe"), 1)
            pe.matmul(banks(6)[0:NM], m_eT, w2[:, :], start=True, stop=True).then_inc(once("m_pe"), 1)
            pe.wait_ge(once("m_dve"), 15)
            pe.wait_ge(once("m_dve"), 18)
            pe.matmul(banks(7), m_e[0:NM, :], m_a[0:NM, :], start=True, stop=True)
            pe.matmul(banks(0), mem_in[:, :], m_t1[0:NM, :], start=True, stop=True).then_inc(once("m_pe"), 1)
            pe.wait_ge(once("m_done"), 1)
            pe.wait_ge(once("diagonals"), 33 - DVE_TAPS)
            pe.wait_ge(once("filled"), 1)
            pe.wait_ge(x_in, 16)
            with pe.Fori(0, PAIRS) as i:
                for b in range(NB):
                    for t in range(4):
                        mm = pe.transpose(banks(b)[:, t * P:(t + 1) * P], x_tc[:, 4 * b + t, :], ident[:, :])
                    mm.then_inc(s("x_turned"), 1)

                def project(name, w, rhs, bank):
                    for b in range(NB):
                        pe.matmul(banks(bank + b), w, rhs(b), start=True, stop=True).then_inc(s(name), 1)

                pe.wait_ge(s("xT"), 2)
                of_x = lambda b: xT[:, b, :]
                project("v_proj", w_v[:, :], of_x, 6)
                project("k_proj", w_k[:, :], of_x, 4)
                project("q_proj", w_q[:, :], of_x, 2)
                project("b_proj", w_bx[:, :], of_x, 0)

                def fir31_taps(b, first, last):
                    for j in range(first, last):
                        mm = pe.matmul(banks(2 + b), fir_diag[:, j, :], v_pad[:, b, j:j + L], start=(j == DVE_TAPS), stop=(j == 30))
                    if last == 31:
                        mm.then_inc(s("fir31_psum"), 1)

                pe.wait_ge(s("q_raw"), 2)
                pe.wait_ge(s("v_act"), 1)
                fir31_taps(0, DVE_TAPS, 8)
                pe.wait_ge(s("k_sq"), 1)
                pe.wait_ge(s("k_raw"), 2)
                project("k_ss", headones[:, :], lambda b: sq[:, 1, b * L:(b + 1) * L], 4)
                fir31_taps(0, 8, 12)
                pe.wait_ge(s("q_sq"), 1)
                pe.wait_ge(s("beta_tanh"), 1)
                project("q_ss", headones[:, :], lambda b: sq[:, 0, b * L:(b + 1) * L], 0)
                fir31_taps(0, 12, 20)
                pe.wait_ge(s("kbq"), 2)
                pe.wait_ge(s("v_raw"), 2)
                for g in range(G):
                    at = banks((6, 7, 0, 1)[g // 8])[:, (g % 8) * 64:(g % 8) * 64 + 64]
                    for h in range(H):
                        r = slice(DH * h, DH * h + DH)
                        mm = pe.matmul(at[r].rearrange("p (a c) -> p a c", a=2), k_n[r, g * CH:(g + 1) * CH],
                                       kbq[r, :, g * CH:(g + 1) * CH], start=True, stop=True)
                    if g % 8 == 7:
                        mm.then_inc(s("r1"), 1)
                fir31_taps(0, 20, 31)
                fir31_taps(1, DVE_TAPS, 31)

                stat_order = (6, 0, 1, 4, 2, 3, 5)

                def stat(n, b):
                    if b == 0:
                        pe.wait_ge(s("streams"), n + 1)
                    pe.matmul(banks(4 + b)[0:28], statsel[:, stat_order[n], :], ab[:, n % 2, b * L:(b + 1) * L],
                              start=(n == 0), stop=(n == 6), skip_group_check=True).then_inc(s("stat"), 1)

                def small(name, g, at, lhs, rhs, inc=False, **kw):
                    for h in range(H):
                        r = slice(DH * h, DH * h + DH)
                        mm = pe.matmul(at[r], lhs[r], rhs[r], **kw)
                    if inc:
                        mm.then_inc(s(name), 1)

                pe.wait_ge(s("k_norm"), 1)
                pe.wait_ge(s("Dt"), 1)
                pe.wait_ge(s("kv"), 2)
                for g in range(G):
                    small("r2", g, banks(4 + g // 8)[:, (g % 8) * 64:(g % 8) * 64 + 64], Dt[:, g, :], kv[:, g, :],
                          inc=g % 8 == 7, start=True, stop=True)
                pe.wait_ge(s("fir31"), 1)
                pe.wait_ge(s("ka"), 3)
                for g in range(G):
                    if g % 16 == 0:
                        pe.wait_ge(s("wu"), g // 16 + 1)
                    small("r3", g, banks(g // 8)[:, (g % 8) * 64:(g % 8) * 64 + 64], wu[:, g, 0:32], ka[:, g, :],
                          inc=g % 8 == 7, start=True, stop=True)
                for g in range(G):
                    small("r4", g, banks(4 + g // 16)[:, (g % 16) * 32:(g % 16) * 32 + 32], ka[:, g, 0:32], wu[:, g, 32:64],
                          inc=g % 16 == 15, start=True, stop=True)

                def chunk_out(n):
                    for b in range(NB):
                        g = b * NC + n
                        at = banks(b)[:, n * CH:(n + 1) * CH]
                        for h in range(H):
                            r = slice(DH * h, DH * h + DH)
                            mm = pe.matmul(at[r], wu[r, g, 32:64], ka[r, g, 32:64], start=True, stop=(n == 0))
                            if n:
                                mm = pe.matmul(at[r], state[r, b, n, :], qwT[r, g * CH:(g + 1) * CH], start=False, stop=True)
                    return mm

                pe.wait_ge(s("pt"), 1)
                pe.wait_ge(s("qwT"), 1)
                for n in range(1, NC):
                    pe.wait_ge(s("state"), n)
                    if n < NC - 1:
                        for b in range(NB):
                            for h in range(H):
                                r = slice(DH * h, DH * h + DH)
                                mm = pe.matmul(banks(6)[r, b * DH:(b + 1) * DH], pt[r, b * NC + n, :], state[r, b, n, :],
                                               start=True, stop=True)
                        mm.then_inc(s("scan"), 1)
                    chunk_out(n - 1)
                chunk_out(NC - 1).then_inc(s("delta_psum"), 1)
                for n in range(S7):
                    for b in range(NB):
                        stat(n, b)
                for m in range(2):
                    for b in range(NB):
                        at = banks((6, 2)[m] + b)
                        pe.matmul(at, gw1a[:, m * P:(m + 1) * P], xT[:, b, :], start=True, stop=False)
                        if m == 0 and b == 0:
                            pe.wait_ge(s("stats"), 1)
                        pe.matmul(at, gw1b[:, m * P:(m + 1) * P], stats[:, b * L:(b + 1) * L], start=False,
                                  stop=True).then_inc(s("gate_h"), 1)
                for m in range(2):
                    pe.wait_ge(s("hmid"), m + 1)
                    for tt in range(NT):
                        mm = pe.matmul(banks((6, 2)[m])[:, tt * 28:(tt + 1) * 28], hmid[:, m, tt * P:(tt + 1) * P], gw2[:, m, :],
                                       start=True, stop=True)
                    mm.then_inc(s("logits"), 1)
                pe.wait_ge(s("wts"), 1)
                pe.wait_ge(s("delta"), 1)
                for tt in range(NT):
                    mm = pe.transpose(banks(tt // 4)[0:28, (tt % 4) * P:(tt % 4 + 1) * P], gl[:, 3, tt, :], ident[:, :])
                mm.then_inc(s("wts_turned"), 1)
                pe.wait_ge(s("halves"), 2)
                for k in range(S7):
                    if k >= 2:
                        pe.wait_ge(s("prod"), k - 1)
                    for b in range(NB):
                        pe.matmul(banks(4 + 2 * (k % 2) + b), expand[0:60, k, :], halves[0:60, b * L:(b + 1) * L],
                                  start=True, stop=True).then_inc(s("expand"), 1)
                for b in range(NB):
                    pe.wait_ge(s("o_sq"), b + 1)
                    pe.matmul(banks(2 + b), headones[:, :], ab[:, 1, b * L:(b + 1) * L], start=True, stop=True).then_inc(s("o_ms"), 1)
                for b in range(NB):
                    pe.wait_ge(s("o_n"), b + 1)
                    for tt in range(4):
                        mm = pe.matmul(banks(b)[:, tt * D:(tt + 1) * D], acc[:, (4 * b + tt) * P:(4 * b + tt + 1) * P], w_on[:, :],
                                       start=True, stop=True)
                    mm.then_inc(s("x1_out"), 1)

                def turn(name, src, bank, rows):
                    for b in range(NB):
                        pe.wait_ge(s(rows), 4 * b + 4)
                        for t in range(4):
                            mm = pe.transpose(banks(bank + b)[:, t * P:(t + 1) * P], src[:, 4 * b + t, :], ident[:, :])
                        mm.then_inc(s(name), 1)

                pe.wait_ge(s("prod"), 7)
                turn("x1_turned", x1, 4, "x1")
                pe.wait_ge(s("pooled_b"), 2)
                for b in range(NB):
                    mm = pe.matmul(banks(6)[:, b * E:(b + 1) * E], pooled_b[:, b, :], gwT[:, :], start=True, stop=True)
                mm.then_inc(s("gate8"), 1)
                pe.wait_ge(s("x1T"), 2)
                for m in range(4):
                    if m == 3:
                        pe.wait_ge(s("choice"), 2)
                    project("down", dnT[:, m, :], lambda b: x1T[:, b, :], (2, 0, 4, 6)[m])
                pe.wait_ge(s("hf"), 4)
                pe.wait_ge(s("ups"), 10)
                for t in range(NT):
                    at = banks(2 + t // 4)[:, (t % 4) * D:(t % 4 + 1) * D]
                    for m in range(4):
                        pe.matmul(at, hf[:, m, t * P:(t + 1) * P], ups[:, t // 4, m, :], start=(m == 0), stop=False)
                    mm = pe.matmul(at, c_rows[:, t // 4, :], upb[:, :], start=False, stop=True)
                    if t % 4 == 3:
                        mm.then_inc(s("x2_out"), 1)
                turn("x2_turned", x2, 0, "x2")
                for b in range(NB):
                    pe.wait_ge(s("xe"), b + 1)
                    pe.matmul(banks(2 + b), aw[:, 0, :], xe[:, b, NM:], start=True, stop=True).then_inc(s("q_proj2"), 1)
                project("k_proj2", aw[:, 1, :], lambda b: xe[:, b, NM:], 4)
                for j in range(2 * NT):
                    b, k = j // 8, j % 8
                    mm = pe.matmul(banks((6, 7, 0, 1)[j // 4])[:, (j % 4) * D:(j % 4 + 1) * D],
                                   xe[:, b, NM * k:NM * k + P], aw[:, 2, :], start=True, stop=True)
                    if j % 4 == 3:
                        mm.then_inc(s("v_proj2"), 1)
                pe.wait_ge(s("qs"), 1)
                pe.wait_ge(s("ke"), 1)
                for b in range(NB):
                    if b == 1:
                        pe.wait_ge(s("ve"), 2)
                    for t in range(4):
                        for half in range(2):
                            for h in range(H):
                                r = slice(DH * h, DH * h + DH)
                                k0 = t * P + NM * half
                                mm = pe.matmul(banks(((2, 3, 4, 5), (6, 7, 0, 1))[b][h])[NM * half:NM * half + NM, t * P:(t + 1) * P],
                                               qs[r, b * L + k0:b * L + k0 + NM], ke[r, b, k0:k0 + P], start=True, stop=True)
                                if t == 3 and half == 1:
                                    mm.then_inc(s("scores"), 1)
                pe.wait_ge(s("ones_column"), 1)
                for b in range(NB):
                    pe.wait_ge(s("probs"), b + 1)
                    for n in range(16):
                        mm = pe.transpose(banks(((2, 3, 4, 5), (6, 7, 0, 1))[b][n // 4])[:, (n % 4) * P:(n % 4 + 1) * P],
                                          sc[b][:, n, :], ident[:, :])
                        if n % 4 == 3:
                            mm.then_inc(s("probs_turned"), 1)
                for b in range(NB):
                    pe.wait_ge(s("prT"), 2 * b + 2)
                    for t in range(4):
                        for half in range(2):
                            for h in range(H):
                                c = (t % 2) * 132 + h * 33
                                mm = pe.matmul(banks(2 + (4 * b + t) // 2)[NM * half:NM * half + NM, c:c + 33],
                                               prT[b][:, 4 * h + t, NM * half:NM * half + NM], ve[:, 8 * b + 2 * t + half, h, :],
                                               start=True, stop=True)
                    mm.then_inc(s("pv"), 1)
                pe.wait_ge(s("prT"), 4)
                turn("ao_turned", ao, 6, "ao")
                for b in range(NB):
                    pe.wait_ge(s("aoT"), b + 1)
                    pe.matmul(banks(b), aw[:, 3, :], aoT[:, b * L:(b + 1) * L], start=True, stop=True).then_inc(s("wo"), 1)
                for n in range(8):
                    b, m = n // 4, n % 4
                    if n >= 2:
                        pe.wait_ge(s("aT"), n - 1)
                    pe.matmul(banks(4 + n % 2), w1T[:, m, :], xe[:, b, NM:], start=True, stop=True).then_inc(s("zT"), 1)
                for b in range(NB):
                    pe.wait_ge(s("aT"), 4 * b + 4)
                    for m in range(4):
                        mm = pe.matmul(banks(2 + b), w2T[:, m, :], aT[:, m, b * L:(b + 1) * L], start=(m == 0), stop=(m == 3))
                    mm.then_inc(s("pred"), 1)

                def z_of(t):
                    b, c = t // 4, t % 4
                    o = t % 2
                    if t >= 2:
                        pe.wait_ge(s("zb"), t - 1)
                    pe.matmul(banks((6, 0)[o]), xe[:, b, NM + c * P:NM + (c + 1) * P], w1T[:, :, :].rearrange("p m c -> p (m c)"),
                              start=True, stop=True).then_inc(s("z"), 1)

                def da_of(t):
                    b, c = t // 4, t % 4
                    o = t % 2
                    if t >= 2:
                        pe.wait_ge(s("dz"), t - 1)
                    if t == 0:
                        pe.wait_ge(s("eT"), 1)
                        for bb in range(NB):
                            for cc in range(4):
                                mm = pe.transpose(banks(4 + bb)[:, cc * P:(cc + 1) * P], eT[:, bb, cc * P:(cc + 1) * P], ident[:, :])
                            mm.then_inc(s("e_turned"), 1)
                    pe.matmul(banks((7, 1)[o]), eT[:, b, c * P:(c + 1) * P], w2[:, :], start=True, stop=True).then_inc(s("da"), 1)

                pe.wait_ge(s("swaT"), 1)
                z_of(0)
                z_of(1)
                da_of(0)
                for t in range(NT):
                    if t + 2 < NT:
                        z_of(t + 2)
                    if t + 1 < NT:
                        da_of(t + 1)
                    o = t % 2
                    if t == 0:
                        pe.wait_ge(s("e_tc"), 1)
                    pe.wait_ge(s("a_th"), 2 * t + 2)
                    pe.matmul(banks(2), e_tc[:, t, :], a_tc[:, o, :], start=(t == 0), stop=(t == NT - 1))
                    pe.wait_ge(s("dz"), t + 1)
                    pe.matmul(banks(3), x2[:, t, :], dz[:, o, :], start=(t == 0), stop=(t == NT - 1)).then_inc(s("dw"), 1)
                pe.wait_ge(s("dw"), NT)
                pe.sem_inc(s("step_done"), 1)
                pe.wait_ge(step_go, i + 1)

            for m in range(4):
                mm = pe.matmul(banks(7)[:, m:m + 1], dzsum[:, m * P:(m + 1) * P], ones[:, 0:1], start=True, stop=True)
            mm.then_inc(s2("db1"), 1)
            pe.wait_ge(once("e_loaded"), 16 * (len(small_late_loads) + len(expert_loads)))
            def memory_z(n):
                b, m = n // 4, n % 4
                if n == 0:
                    pe.wait_ge(s2("in_x2T"), 16)
                if n >= 2:
                    pe.wait_ge(s2("aT"), n - 1)
                pe.matmul(banks(4 + n % 2), w1T[:, m, :], bx2T[:, b * L:(b + 1) * L], start=True, stop=True).then_inc(s2("zT"), 1)

            def memory_answer(n):
                b, m = n // 4, n % 4
                if n == 0:
                    pe.wait_ge(s2("aT"), 8)
                mm = pe.matmul(banks(4 + b), w2T[:, m, :], baT[:, m, b * L:(b + 1) * L], start=(m == 0), stop=(m == 3))
                if m == 3:
                    mm.then_inc(s2("om"), 1)

            def gate(n):
                if n == 0:
                    pe.wait_ge(s2("in_swaT"), 16)
                    pe.wait_ge(s2("omT"), 1)
                else:
                    pe.wait_ge(s2("tg"), 1)
                for b in range(NB):
                    pe.matmul(banks(4 + b), lT[:, n, :], (bswaT, omT)[n][:, b * L:(b + 1) * L], start=True, stop=True)\
                        .then_inc(s2(f"g{n + 1}"), 1)

            def turn2(name, src, t):
                mm = pe.transpose(banks(4 + t // 4)[:, (t % 4) * P:(t % 4 + 1) * P], src[:, t * P:(t + 1) * P], ident[:, :])
                if t % 4 == 3:
                    mm.then_inc(s2(name), 1)

            def turn_merged():
                pe.wait_ge(s2("tg"), 2)
                pe.wait_ge(s2("merged"), 1)
                for t in range(NT):
                    turn2("m_turned", mT, t)

            def turn_x3():
                pe.wait_ge(s2("x3"), NT)
                for t in range(NT):
                    turn2("x3_turned", x3, t)

            def route():
                pe.wait_ge(s2("x3T"), 1)
                for t in range(NT):
                    mm = pe.matmul(banks(4)[:, t * E:(t + 1) * E], x3T[:, t * P:(t + 1) * P], wrT[:, :], start=True, stop=True)
                mm.then_inc(s2("r_logits"), 1)

            def turn_weights():
                pe.wait_ge(s2("weights"), 1)
                for t in range(NT):
                    mm = pe.transpose(banks(4 + t // 4)[0:E, (t % 4) * P:(t % 4 + 1) * P], rw[:, 3, t, :], ident[:, :])
                mm.then_inc(s2("rw_turned"), 1)

            def hidden(e, m):
                n = 4 * e + m
                for b in range(NB):
                    at = slice(b * L, (b + 1) * L)
                    if n == 0 and b == 0:
                        pe.wait_ge(s2("x3_high"), 1)
                        pe.wait_ge(s2("x3_low"), 1)
                    if n >= 1:
                        pe.wait_ge(s2("hT"), 2 * (n - 1) + b + 1)
                    pe.matmul(banks(2 + b), w1_high[:, e, m, :], x3_high[:, at], start=True, stop=False)
                    pe.matmul(banks(2 + b), w1_high[:, e, m, :], x3_low[:, at], start=False, stop=False)
                    pe.matmul(banks(2 + b), w1_low[e][:, m, :], x3_high[:, at], start=False, stop=True).then_inc(s2("h"), 1)

            def experts(last):
                for m in range(4):
                    hidden(0, m)
                for t in range(NT):
                    mm = pe.matmul(banks(t // 4)[:, (t % 4) * D:(t % 4 + 1) * D], rwT[:, t * P:(t + 1) * P], b2e[:, :],
                                   start=True, stop=True)
                    if t % 4 == 3:
                        mm.then_inc(s2("y_bias"), 1)
                for e in range(E):
                    for t in range(NT):
                        if e + 1 < E and t % 2 == 0:
                            hidden(e + 1, t // 2)
                        if t == 0:
                            pe.wait_ge(s2("hT"), 8 * e + 8)
                            if e == 1:
                                pe.wait_ge(s2("y"), 1)
                            if e >= 2:
                                pe.wait_ge(s2("y"), 1 + NT * (e - 1))
                        at = banks((6, 0)[e % 2] + t // 4)[:, (t % 4) * D:(t % 4 + 1) * D]
                        for m in range(4):
                            mm = pe.matmul(at, hT[e % 2][:, m, t * P:(t + 1) * P], w2eT[:, e, m, :], start=(m == 0), stop=(m == 3))
                        if t % 4 == 3:
                            mm.then_inc(s2("o"), 1)
                        if last:
                            continue
                        if e == 0:
                            memory_z(t)
                        if e == 1:
                            memory_answer(t)
                        if e == 2 and t == 5:
                            gate(0)
                        if e == 3 and t == 3:
                            gate(1)
                        if e == 4 and t == 5:
                            turn_merged()
                        if e == 5 and t == 6:
                            turn_x3()
                        if e == 6 and t == 5:
                            route()
                        if e == 7 and t == 7:
                            turn_weights()

            for n in range(2 * E):
                if n == 5:
                    pe.wait_ge(s2("stepped"), 4)
                if n >= 6:
                    if n - 6 < E:
                        pe.wait_ge(s2("w1_low"), n - 5)
                    else:
                        pe.wait_ge(s2(("e_even", "e_odd")[n % 2]), (n - 6 - E) // 2 + 1)
                for m in range(4):
                    src = w1n[:, n, m, :] if n < E else w2n[:, n - E, m * P:(m + 1) * P]
                    mm = pe.transpose(banks(turn_bank(n))[:, m * P:(m + 1) * P], src, ident[:, :])
                mm.then_inc(s2("e_turned"), 1)
                if n == E:
                    pe.wait_ge(s2("updated"), 2)
                if n >= E:
                    memory_z(n - E)
            pe.wait_ge(s2("updated"), 1)
            pe.wait_ge(s2("e_even"), 3)
            for m in range(4):
                mm = pe.transpose(banks(0)[:, m * P:(m + 1) * P], w2[:, m * P:(m + 1) * P], ident[:, :])
            mm.then_inc(s2("w2_turned"), 1)
            pe.wait_ge(s2("e_odd"), 3)
            for m in range(2):
                mm = pe.transpose(banks(1)[:, m * P:(m + 1) * P], lin_in[:, m, :], ident[:, :])
            mm.then_inc(s2("w2_turned"), 1)
            pe.wait_ge(s2("ready2"), 1)
            for n in range(8):
                memory_answer(n)
            pe.wait_ge(s2("ready2"), 2)
            gate(0)
            gate(1)
            turn_merged()
            turn_x3()
            route()
            turn_weights()
            pe.wait_ge(s2("rw_turned"), 1)
            pe.sem_inc(s2("step_done"), 1)
            pe.wait_ge(once("step2_go"), 1)
            experts(False)
            pe.wait_ge(s2("rw_turned"), 1)
            pe.sem_inc(s2("step_done"), 1)
            pe.wait_ge(once("step2_go"), 2)
            with pe.Fori(1, PAIRS - 1) as i:
                experts(False)
                pe.wait_ge(s2("rw_turned"), 1)
                pe.sem_inc(s2("step_done"), 1)
                pe.wait_ge(once("step2_go"), i + 2)
            experts(True)

        @block.sync
        def _(sp_):
            for dst, src in loads:
                sp_.dma_start(dst, src, allow_slow_non_contiguous=True).then_inc(loaded, 16)

            def take_x(k, signal):
                sp_.dma_start(x_tc[:, :, :].rearrange("p (b t) d -> p b t d", b=NB),
                              A["L0_attn_hidden_states"][bass.ds(k * NB, NB), :, :].rearrange("b (t p) d -> p b t d", p=P))\
                    .then_inc(signal, 16)

            def keep_pair(k, last):
                sp_.wait_ge(s("x1"), NT)
                if not last:
                    take_x(k + 1, s("next_x"))
                else:
                    for dst, src in small_late_loads:
                        sp_.dma_start(dst, src, allow_slow_non_contiguous=True).then_inc(once("e_loaded"), 16)
                sp_.wait_ge(s("x2"), NT)
                sp_.dma_start(x2_d[bass.ds(k, 1), :, :].rearrange("a p n -> p (a n)"), x2.rearrange("p t d -> p (t d)"))\
                    .then_inc(s("kept"), 16)
                sp_.wait_ge(s("xe"), 2)
                sp_.dma_start(x2T_d[bass.ds(k, 1), :, :].rearrange("a p (b t) -> p (a b) t", b=NB), xe[:, :, NM:])\
                    .then_inc(s("kept"), 16)
                sp_.wait_ge(s("swaT"), 1)
                sp_.dma_start(swaT_d[bass.ds(k, 1), :, :].rearrange("a p n -> p (a n)"), swaT).then_inc(s("kept"), 16)
                if not last:
                    sp_.wait_ge(s("next_x"), 16)
                else:
                    sp_.wait_ge(s("ao"), NT)
                    for dst, src in expert_loads:
                        sp_.dma_start(dst, src).then_inc(once("e_loaded"), 16)
                    for dst, src in ((bx2T, x2T_d), (bswaT, swaT_d), (bx2, x2_d)):
                        sp_.dma_start(dst, src[0]).then_inc(once("first_in"), 16)
                sp_.wait_ge(s("step_done"), 4)
                sp_.wait_ge(s("kept"), 48)
                sp_.sem_clear(range(min(z.num for z in sems.values()), max(z.num for z in sems.values()) + 1))
                sp_.sem_inc(step_go, 1)

            take_x(0, x_in)
            with sp_.Fori(0, PAIRS - 1) as i:
                keep_pair(i, False)
            keep_pair(PAIRS - 1, True)
            if out is not None:
                def take(k):
                    for name, dst, src in (("in_x2T", bx2T, x2T_d), ("in_swaT", bswaT, swaT_d), ("in_x2", bx2, x2_d)):
                        sp_.dma_start(dst, src[bass.ds(k, 1), :, :].rearrange("a p n -> p (a n)")).then_inc(s2(name), 16)

                def store(k, x4):
                    sp_.wait_ge(s2(x4), NT)
                    sp_.dma_start(out[bass.ds(k * NB, NB), :, :].rearrange("b (t p) d -> p b t d", p=P),
                                  x3_keep.rearrange("p (b t d) -> p b t d", b=NB, d=D)).then_inc(s2("stored"), 16)

                def next_step():
                    sp_.wait_ge(s2("step_done"), 3)
                    sp_.sem_clear(range(min(z.num for z in sems.values()), max(z.num for z in sems.values()) + 1))
                    sp_.sem_inc(once("step2_go"), 1)

                sp_.wait_ge(once("first_in"), 48)
                for name in ("in_x2T", "in_swaT", "in_x2"):
                    sp_.sem_inc(s2(name), 16)
                next_step()
                take(1)
                next_step()
                with sp_.Fori(1, PAIRS - 1) as i:
                    take(i + 1)
                    store(i - 1, "x4")
                    sp_.wait_ge(s2("stored"), 16)
                    next_step()
                store(PAIRS - 2, "x4")
                store(PAIRS - 1, "last_x4")
                sp_.wait_ge(s2("stored"), 32)


_INS = [
    "L0_attn_hidden_states", "L0_attn_w_q", "L0_attn_w_k", "L0_attn_w_v", "L0_attn_w_b", "L0_attn_conv_q_w",
    "L0_attn_conv_k_w", "L0_attn_conv_v_w", "L0_attn_fir1", "L0_attn_fir3", "L0_attn_fir7", "L0_attn_fir15",
    "L0_attn_fir31", "L0_attn_gate_w1", "L0_attn_gate_b1", "L0_attn_gate_w2", "L0_attn_gate_b2",
    "L0_attn_norm_w", "L0_attn_w_o", "L0_ffn_gate_w", "L0_ffn_down_w", "L0_ffn_down_b", "L0_ffn_up_w",
    "L0_ffn_up_b", "L1_attn_mem", "L1_attn_wq", "L1_attn_wk", "L1_attn_wv", "L1_attn_wo", "L1_attn_w1",
    "L1_attn_b1", "L1_attn_w2", "L1_attn_b2", "L1_attn_lin1", "L1_attn_lin2", "L1_attn_alpha",
    "L1_attn_theta", "L1_ffn_Wr", "L1_ffn_br", "L1_ffn_W1", "L1_ffn_b1", "L1_ffn_W2", "L1_ffn_b2",
    "L1_ffn_gamma", "L1_ffn_beta",
]
_OUTS = [((B, L, D), "float32")]


def kernel(**inputs):
    import numpy as _np
    import concourse.bacc as _bacc
    from concourse import mybir as _mybir
    from concourse.bass_utils import run_bass_kernel_spmd as _run

    nc = _bacc.Bacc("TRN2", target_bir_lowering=False, num_devices=1)
    arrays, args = {}, {}
    for name in _INS:
        a = _np.ascontiguousarray(inputs[name])
        if a.ndim == 0:
            a = a.reshape(1)
        arrays[f"in_{name}_dram"] = a
        args[name] = nc.dram_tensor(f"in_{name}_dram", a.shape, _mybir.dt.from_np(a.dtype), kind="ExternalInput").ap()
    outs = []
    for i, (shape, dtype) in enumerate(_OUTS):
        dt = _mybir.dt.from_np(_np.dtype(dtype))
        outs.append(nc.dram_tensor(f"out_{i}_dram", shape, dt, kind="ExternalOutput").ap())
    program(nc, args, outs[0])
    r = _run(nc, [arrays], core_ids=[0])
    got = tuple(r.results[0][f"out_{i}_dram"] for i in range(len(_OUTS)))
    return got[0]
```
